# Optimizing a Trainium2 kernel written in Bass

```python
import numpy as np
import jax
import jax.numpy as jnp

def _softmax(x, axis=-1):
    return jax.nn.softmax(x, axis=axis)

def _gelu(x):
    return jax.nn.gelu(x, approximate=True)

def _silu(x):
    return jax.nn.silu(x)

def _sigmoid(x):
    return jax.nn.sigmoid(x)

def _layernorm(x, axis=-1, eps=1e-05):
    m = jnp.mean(x, axis=axis, keepdims=True)
    v = jnp.var(x, axis=axis, keepdims=True)
    return (x - m) / jnp.sqrt(v + eps)

def _scatter_add(tgt, idx, src, axis=0):
    return tgt.at[idx].add(src)

def _segment_sum(src, seg, n):
    return jax.ops.segment_sum(src, seg, n)
kernel_name = 'mk_seq_postln_d2_jaxref_r4_290056'

def setup_inputs(seed: int=0):
    np.random.seed(seed)
    _w = jnp.asarray

    def _L0_attn_setup():
        import jax, jax.numpy as jnp
        import numpy as np
        D_MODEL = 256
        HEADDIM = 128
        D_STATE = 64
        NGROUPS = 1
        NHEADS = D_MODEL // HEADDIM

        def segsum(x):
            T = x.shape[-1]
            xe = jnp.broadcast_to(x[..., None], x.shape + (T,))
            mask_lower = jnp.tril(jnp.ones((T, T), dtype=bool), k=-1)
            xe = jnp.where(mask_lower, xe, 0.0)
            x_segsum = jnp.cumsum(xe, axis=-2)
            mask_incl = jnp.tril(jnp.ones((T, T), dtype=bool), k=0)
            return jnp.where(mask_incl, x_segsum, -jnp.inf)

        def ssd_minimal_discrete(X, A, B, C, chunk):
            b, T = (X.shape[0], X.shape[1])
            c = T // chunk
            resh = lambda t: t.reshape(b, c, chunk, *t.shape[2:])
            X, B, C = (resh(X), resh(B), resh(C))
            A = resh(A).transpose(0, 3, 1, 2)
            A_cumsum = jnp.cumsum(A, axis=-1)
            Lmat = jnp.exp(segsum(A))
            Y_diag = jnp.einsum('bclhn,bcshn,bhcls,bcshp->bclhp', C, B, Lmat, X)
            decay_states = jnp.exp(A_cumsum[..., -1:] - A_cumsum)
            states = jnp.einsum('bclhn,bhcl,bclhp->bchpn', B, decay_states, X)
            init = jnp.zeros_like(states[:, :1])
            states = jnp.concatenate([init, states], axis=1)
            A_last = jnp.pad(A_cumsum[..., -1], ((0, 0), (0, 0), (1, 0)))
            decay_chunk = jnp.exp(segsum(A_last))
            new_states = jnp.einsum('bhzc,bchpn->bzhpn', decay_chunk, states)
            states = new_states[:, :-1]
            state_decay_out = jnp.exp(A_cumsum)
            Y_off = jnp.einsum('bclhn,bchpn,bhcl->bclhp', C, states, state_decay_out)
            return (Y_diag + Y_off).reshape(b, T, NHEADS, HEADDIM)

        def ssd_forward(x, W_xproj, dt_bias, A_log, D):
            b, T, _ = x.shape
            dtBC = x @ W_xproj.T
            dt = dtBC[..., :NHEADS]
            Bm = dtBC[..., NHEADS:NHEADS + NGROUPS * D_STATE]
            Cm = dtBC[..., NHEADS + NGROUPS * D_STATE:]
            dt = jax.nn.softplus(dt + dt_bias)
            A = -jnp.exp(A_log)
            Xh = x.reshape(b, T, NHEADS, HEADDIM) * dt[..., None]
            Bh = jnp.broadcast_to(Bm.reshape(b, T, NGROUPS, D_STATE), (b, T, NHEADS, D_STATE))
            Ch = jnp.broadcast_to(Cm.reshape(b, T, NGROUPS, D_STATE), (b, T, NHEADS, D_STATE))
            y = ssd_minimal_discrete(Xh, A * dt, Bh, Ch, T)
            y = y.reshape(b, T, D_MODEL)
            D_full = jnp.repeat(D, HEADDIM)
            return y + x * D_full
        key = jax.random.key(seed)
        k1, k2, k3 = jax.random.split(key, 3)
        x = jax.random.normal(k1, (2, 512, D_MODEL), dtype=jnp.float32)
        W_xproj = jax.random.normal(k2, (NHEADS + 2 * NGROUPS * D_STATE, D_MODEL), dtype=jnp.float32) * (1.0 / np.sqrt(D_MODEL))
        dt_bias = jnp.zeros((NHEADS,), dtype=jnp.float32)
        A_log = jnp.log(jax.random.uniform(k3, (NHEADS,), minval=1.0, maxval=16.0, dtype=jnp.float32))
        D = jnp.ones((NHEADS,), dtype=jnp.float32)
        return {'x': x, 'W_xproj': W_xproj, 'dt_bias': dt_bias, 'A_log': A_log, 'D': D}
    _L0_attn_in = _L0_attn_setup()

    def _L0_ffn_setup():
        import jax, jax.numpy as jnp
        import numpy as np
        N_EMBD = 256
        N_STATE = 1024
        key = jax.random.key(seed)
        k_x, k_w1, k_b1, k_w2, k_b2 = jax.random.split(key, 5)
        x = jax.random.normal(k_x, (4, 512, N_EMBD), dtype=jnp.float32)
        w1 = jax.random.normal(k_w1, (N_EMBD, N_STATE), dtype=jnp.float32) * (1.0 / np.sqrt(N_EMBD))
        b1 = jax.random.normal(k_b1, (N_STATE,), dtype=jnp.float32) * 0.02
        w2 = jax.random.normal(k_w2, (N_STATE, N_EMBD), dtype=jnp.float32) * (1.0 / np.sqrt(N_STATE))
        b2 = jax.random.normal(k_b2, (N_EMBD,), dtype=jnp.float32) * 0.02
        return {'x': x, 'w1': w1, 'b1': b1, 'w2': w2, 'b2': b2}
    _L0_ffn_in = _L0_ffn_setup()

    def _L1_attn_setup():
        import jax, jax.numpy as jnp
        import numpy as np
        EMBED = 256
        HEADS = 16
        HD = EMBED // HEADS
        M = 32
        R = 2
        EPS = 1e-06
        C_CONST = 2.0 + EPS
        CHUNK = 128

        def _features(x, omega, quad_nodes, quad_weights):
            B, H, T, D = x.shape
            xn = x / jnp.maximum(jnp.linalg.norm(x, axis=-1, keepdims=True), 1e-12)
            proj = jnp.einsum('bhtd,rhdm->rbhtm', xn, omega)
            s = quad_nodes[:, None, None, None, None]
            sqrt_2s = jnp.sqrt(2.0 * jnp.maximum(s, 0.0))
            arg = jnp.clip(proj * sqrt_2s - s, -20.0, 20.0)
            feat = jnp.exp(arg) / np.sqrt(M).astype(np.float32)
            feat = feat * jnp.sqrt(jnp.maximum(quad_weights, 0.0))[:, None, None, None, None]
            return jnp.transpose(feat, (1, 2, 3, 0, 4)).reshape(B, H, T, R * M)
        key = jax.random.key(seed)
        ks = jax.random.split(key, 4)
        B, T = (2, 512)
        x = jax.random.normal(ks[0], (B, T, EMBED), jnp.float32)
        Wqkv = jax.random.normal(ks[1], (EMBED, 3 * EMBED), jnp.float32) * 0.02
        bqkv = jnp.zeros((3 * EMBED,), jnp.float32)
        Wout = jax.random.normal(ks[2], (EMBED, EMBED), jnp.float32) * 0.02
        bout = jnp.zeros((EMBED,), jnp.float32)
        omega = jax.random.normal(ks[3], (R, HEADS, HD, M), jnp.float32)
        nodes, weights = np.polynomial.laguerre.laggauss(R)
        quad_nodes = jnp.asarray(nodes / C_CONST, jnp.float32)
        quad_weights = jnp.asarray(weights * (C_CONST / 4.0), jnp.float32)
        return {'x': x, 'Wqkv': Wqkv, 'bqkv': bqkv, 'Wout': Wout, 'bout': bout, 'omega': omega, 'quad_nodes': quad_nodes, 'quad_weights': quad_weights}
    _L1_attn_in = _L1_attn_setup()

    def _L1_ffn_setup():
        import jax, jax.numpy as jnp
        import numpy as np
        B, S, DIM = (2, 512, 256)
        HID = 512
        E, NSH, TOPK = (8, 2, 2)

        def _ffn(x, w1, w2, w3):
            return jax.nn.silu(x @ w1.T) * (x @ w3.T) @ w2.T
        key = jax.random.key(seed)
        ks = jax.random.split(key, 8)
        sc = 0.02
        return {'x': jax.random.normal(ks[0], (B, S, DIM), jnp.float32), 'router_w': jax.random.normal(ks[1], (E, DIM), jnp.float32) * sc, 'expert_bias': jnp.zeros((E,), jnp.float32), 'w1': jax.random.normal(ks[2], (E, HID, DIM), jnp.float32) * sc, 'w3': jax.random.normal(ks[3], (E, HID, DIM), jnp.float32) * sc, 'w2': jax.random.normal(ks[4], (E, DIM, HID), jnp.float32) * sc, 'sw1': jax.random.normal(ks[5], (NSH, HID, DIM), jnp.float32) * sc, 'sw3': jax.random.normal(ks[6], (NSH, HID, DIM), jnp.float32) * sc, 'sw2': jax.random.normal(ks[7], (NSH, DIM, HID), jnp.float32) * sc}
    _L1_ffn_in = _L1_ffn_setup()
    _d = {'L0_attn_x': _L0_attn_in['x'], 'L0_attn_W_xproj': _L0_attn_in['W_xproj'], 'L0_attn_dt_bias': _L0_attn_in['dt_bias'], 'L0_attn_A_log': _L0_attn_in['A_log'], 'L0_attn_D': _L0_attn_in['D'], 'L0_ffn_w1': _L0_ffn_in['w1'], 'L0_ffn_b1': _L0_ffn_in['b1'], 'L0_ffn_w2': _L0_ffn_in['w2'], 'L0_ffn_b2': _L0_ffn_in['b2'], 'L1_attn_Wqkv': _L1_attn_in['Wqkv'], 'L1_attn_bqkv': _L1_attn_in['bqkv'], 'L1_attn_Wout': _L1_attn_in['Wout'], 'L1_attn_bout': _L1_attn_in['bout'], 'L1_attn_omega': _L1_attn_in['omega'], 'L1_attn_quad_nodes': _L1_attn_in['quad_nodes'], 'L1_attn_quad_weights': _L1_attn_in['quad_weights'], 'L1_ffn_router_w': _L1_ffn_in['router_w'], 'L1_ffn_expert_bias': _L1_ffn_in['expert_bias'], 'L1_ffn_w1': _L1_ffn_in['w1'], 'L1_ffn_w3': _L1_ffn_in['w3'], 'L1_ffn_w2': _L1_ffn_in['w2'], 'L1_ffn_sw1': _L1_ffn_in['sw1'], 'L1_ffn_sw3': _L1_ffn_in['sw3'], 'L1_ffn_sw2': _L1_ffn_in['sw2']}
    _x0 = _d['L0_attn_x']
    _d['L0_attn_x'] = jax.random.normal(jax.random.fold_in(jax.random.key(seed), 1), (4, 1024, 256), dtype=_x0.dtype)
    del _x0
    return _d

def reference(L0_attn_x, L0_attn_W_xproj, L0_attn_dt_bias, L0_attn_A_log, L0_attn_D, L0_ffn_w1, L0_ffn_b1, L0_ffn_w2, L0_ffn_b2, L1_attn_Wqkv, L1_attn_bqkv, L1_attn_Wout, L1_attn_bout, L1_attn_omega, L1_attn_quad_nodes, L1_attn_quad_weights, L1_ffn_router_w, L1_ffn_expert_bias, L1_ffn_w1, L1_ffn_w3, L1_ffn_w2, L1_ffn_sw1, L1_ffn_sw3, L1_ffn_sw2):

    def _L0_attn_ref(x, W_xproj, dt_bias, A_log, D):
        import jax, jax.numpy as jnp
        import numpy as np
        D_MODEL = 256
        HEADDIM = 128
        D_STATE = 64
        NGROUPS = 1
        NHEADS = D_MODEL // HEADDIM

        def segsum(x):
            T = x.shape[-1]
            xe = jnp.broadcast_to(x[..., None], x.shape + (T,))
            mask_lower = jnp.tril(jnp.ones((T, T), dtype=bool), k=-1)
            xe = jnp.where(mask_lower, xe, 0.0)
            x_segsum = jnp.cumsum(xe, axis=-2)
            mask_incl = jnp.tril(jnp.ones((T, T), dtype=bool), k=0)
            return jnp.where(mask_incl, x_segsum, -jnp.inf)

        def ssd_minimal_discrete(X, A, B, C, chunk):
            b, T = (X.shape[0], X.shape[1])
            c = T // chunk
            resh = lambda t: t.reshape(b, c, chunk, *t.shape[2:])
            X, B, C = (resh(X), resh(B), resh(C))
            A = resh(A).transpose(0, 3, 1, 2)
            A_cumsum = jnp.cumsum(A, axis=-1)
            Lmat = jnp.exp(segsum(A))
            Y_diag = jnp.einsum('bclhn,bcshn,bhcls,bcshp->bclhp', C, B, Lmat, X)
            decay_states = jnp.exp(A_cumsum[..., -1:] - A_cumsum)
            states = jnp.einsum('bclhn,bhcl,bclhp->bchpn', B, decay_states, X)
            init = jnp.zeros_like(states[:, :1])
            states = jnp.concatenate([init, states], axis=1)
            A_last = jnp.pad(A_cumsum[..., -1], ((0, 0), (0, 0), (1, 0)))
            decay_chunk = jnp.exp(segsum(A_last))
            new_states = jnp.einsum('bhzc,bchpn->bzhpn', decay_chunk, states)
            states = new_states[:, :-1]
            state_decay_out = jnp.exp(A_cumsum)
            Y_off = jnp.einsum('bclhn,bchpn,bhcl->bclhp', C, states, state_decay_out)
            return (Y_diag + Y_off).reshape(b, T, NHEADS, HEADDIM)

        def ssd_forward(x, W_xproj, dt_bias, A_log, D):
            b, T, _ = x.shape
            dtBC = x @ W_xproj.T
            dt = dtBC[..., :NHEADS]
            Bm = dtBC[..., NHEADS:NHEADS + NGROUPS * D_STATE]
            Cm = dtBC[..., NHEADS + NGROUPS * D_STATE:]
            dt = jax.nn.softplus(dt + dt_bias)
            A = -jnp.exp(A_log)
            Xh = x.reshape(b, T, NHEADS, HEADDIM) * dt[..., None]
            Bh = jnp.broadcast_to(Bm.reshape(b, T, NGROUPS, D_STATE), (b, T, NHEADS, D_STATE))
            Ch = jnp.broadcast_to(Cm.reshape(b, T, NGROUPS, D_STATE), (b, T, NHEADS, D_STATE))
            y = ssd_minimal_discrete(Xh, A * dt, Bh, Ch, T)
            y = y.reshape(b, T, D_MODEL)
            D_full = jnp.repeat(D, HEADDIM)
            return y + x * D_full
        return ssd_forward(x, W_xproj, dt_bias, A_log, D)

    def _L0_ffn_ref(x, w1, b1, w2, b2):
        import jax, jax.numpy as jnp
        import numpy as np
        N_EMBD = 256
        N_STATE = 1024
        h = jax.nn.gelu(jnp.einsum('bse,eh->bsh', x, w1) + b1, approximate=False)
        return jnp.einsum('bsh,he->bse', h, w2) + b2

    def _L1_attn_ref(x, Wqkv, bqkv, Wout, bout, omega, quad_nodes, quad_weights):
        import jax, jax.numpy as jnp
        import numpy as np
        EMBED = 256
        HEADS = 16
        HD = EMBED // HEADS
        M = 32
        R = 2
        EPS = 1e-06
        C_CONST = 2.0 + EPS
        CHUNK = 128

        def _features(x, omega, quad_nodes, quad_weights):
            B, H, T, D = x.shape
            xn = x / jnp.maximum(jnp.linalg.norm(x, axis=-1, keepdims=True), 1e-12)
            proj = jnp.einsum('bhtd,rhdm->rbhtm', xn, omega)
            s = quad_nodes[:, None, None, None, None]
            sqrt_2s = jnp.sqrt(2.0 * jnp.maximum(s, 0.0))
            arg = jnp.clip(proj * sqrt_2s - s, -20.0, 20.0)
            feat = jnp.exp(arg) / np.sqrt(M).astype(np.float32)
            feat = feat * jnp.sqrt(jnp.maximum(quad_weights, 0.0))[:, None, None, None, None]
            return jnp.transpose(feat, (1, 2, 3, 0, 4)).reshape(B, H, T, R * M)
        B, T, C = x.shape
        qkv = x @ Wqkv + bqkv
        q, k, v = jnp.split(qkv, 3, axis=-1)
        resh = lambda t: t.reshape(B, T, HEADS, HD).transpose(0, 2, 1, 3)
        q, k, v = (resh(q), resh(k), resh(v))
        qf = _features(q, omega, quad_nodes, quad_weights)
        kf = _features(k, omega, quad_nodes, quad_weights)
        Fd = R * M
        nc = T // CHUNK
        to_chunks = lambda t, last: t.reshape(B, HEADS, nc, CHUNK, last).transpose(2, 0, 1, 3, 4)
        qc = to_chunks(qf, Fd)
        kc = to_chunks(kf, Fd)
        vc = to_chunks(v, HD)

        def step(carry, inp):
            kv_state, k_state = carry
            q_ch, k_ch, v_ch = inp
            kv_prod = jnp.einsum('bhtf,bhtd->bhtfd', k_ch, v_ch)
            kv_cur = jnp.cumsum(kv_prod, axis=2) + kv_state[:, :, None]
            k_cur = jnp.cumsum(k_ch, axis=2) + k_state[:, :, None]
            ctx = jnp.einsum('bhtf,bhtfd->bhtd', q_ch, kv_cur)
            den = jnp.maximum(jnp.einsum('bhtf,bhtf->bht', q_ch, k_cur), 1e-06)
            out_ch = ctx / den[..., None]
            return ((kv_cur[:, :, -1], k_cur[:, :, -1]), out_ch)
        init = (jnp.zeros((B, HEADS, Fd, HD), jnp.float32), jnp.zeros((B, HEADS, Fd), jnp.float32))
        _, outs = jax.lax.scan(step, init, (qc, kc, vc))
        out = outs.transpose(1, 2, 0, 3, 4).reshape(B, HEADS, T, HD)
        out = out.transpose(0, 2, 1, 3).reshape(B, T, C)
        return out @ Wout + bout

    def _L1_ffn_ref(x, router_w, expert_bias, w1, w3, w2, sw1, sw3, sw2):
        import jax, jax.numpy as jnp
        import numpy as np
        B, S, DIM = (2, 512, 256)
        HID = 512
        E, NSH, TOPK = (8, 2, 2)

        def _ffn(x, w1, w2, w3):
            return jax.nn.silu(x @ w1.T) * (x @ w3.T) @ w2.T
        bs, sl, d = x.shape
        xf = x.reshape(-1, d)
        shared = jnp.zeros_like(xf)
        for i in range(sw1.shape[0]):
            shared = shared + _ffn(xf, sw1[i], sw2[i], sw3[i])
        logits = xf @ router_w.T + expert_bias
        rw, sel = jax.lax.top_k(logits, TOPK)
        rw = jax.nn.softmax(rw.astype(jnp.float32), axis=-1).astype(x.dtype)
        onehot = jax.nn.one_hot(sel, E, dtype=x.dtype)
        combine = jnp.einsum('tk,tke->te', rw, onehot)

        def body(acc, ew):
            e1, e3, e2, cw = ew
            acc = acc + cw[:, None] * _ffn(xf, e1, e2, e3)
            return (acc, None)
        out, _ = jax.lax.scan(body, jnp.zeros_like(xf), (w1, w3, w2, combine.T))
        out = out + shared
        return out.reshape(bs, sl, -1)
    x = L0_attn_x
    x = _layernorm(x + _L0_attn_ref(x, L0_attn_W_xproj, L0_attn_dt_bias, L0_attn_A_log, L0_attn_D), axis=-1)
    x = _layernorm(x + _L0_ffn_ref(x, L0_ffn_w1, L0_ffn_b1, L0_ffn_w2, L0_ffn_b2), axis=-1)
    x = _layernorm(x + _L1_attn_ref(x, L1_attn_Wqkv, L1_attn_bqkv, L1_attn_Wout, L1_attn_bout, L1_attn_omega, L1_attn_quad_nodes, L1_attn_quad_weights), axis=-1)
    x = _layernorm(x + _L1_ffn_ref(x, L1_ffn_router_w, L1_ffn_expert_bias, L1_ffn_w1, L1_ffn_w3, L1_ffn_w2, L1_ffn_sw1, L1_ffn_sw3, L1_ffn_sw2), axis=-1)
    return x

_drawn_inputs = setup_inputs


def setup_inputs(seed=0):
    import zlib

    import numpy as np

    out = dict(_drawn_inputs(seed))
    spreads = {'L0_attn_dt_bias': (0.0, 0.1),
     'L0_attn_D': (1.0, 0.2),
     'L1_attn_bqkv': (0.0, 0.1),
     'L1_attn_bout': (0.0, 0.1),
     'L1_ffn_expert_bias': (0.0, 0.8)}
    factors = {'L0_attn_A_log': 8.0,
     'L0_ffn_b1': 5.03,
     'L0_ffn_b2': 3.433,
     'L1_attn_omega': 8.0,
     'L1_attn_quad_nodes': 7.355,
     'L1_attn_quad_weights': 8.0,
     'L1_ffn_router_w': 3.898,
     'L1_ffn_w1': 3.336,
     'L1_ffn_w3': 3.313,
     'L1_ffn_w2': 3.298}
    for name, (base, spread) in spreads.items():
        noise = np.random.default_rng([zlib.crc32(name.encode()), seed]).standard_normal(out[name].shape)
        drawn = base * np.exp(spread * noise) if base else spread * noise
        out[name] = jnp.asarray(drawn.astype(out[name].dtype))
    for name, factor in factors.items():
        out[name] = (out[name] * factor).astype(out[name].dtype)
    return out
```

```python
from contextlib import ExitStack

import numpy as np
import concourse.bass as bass
from concourse import mybir

F32 = mybir.dt.float32
I32 = mybir.dt.int32
ALU = mybir.AluOpType
ACT = mybir.ActivationFunctionType
AX = mybir.AxisListType

P = 128
BATCH, SEQ, D = 4, 1024, 256
KD = D // P
CHUNK = 128
STEPS = SEQ // CHUNK
TOK = BATCH * CHUNK
HEADS0, HEADDIM0, STATE0 = 2, 128, 64
EPS = 1e-5
HEADS1, HD, MF, RF = 16, 16, 32, 2
FD = MF * RF
PAIRS = HEADS1 // 2
VW = HD + 1
EXPERTS, SHARED, TOPK, HID = 8, 2, 2, 512
HM = HID // P
F32R = mybir.dt.float32r
WCOLS = 2 * KD * HID + HM * D
W1AT, W3AT, W2AT = 0, KD * HID, 2 * KD * HID
TILES = STEPS * BATCH
SLOT = 256
GROUPS = (TILES * P * TOPK - EXPERTS) // SLOT + EXPERTS
GROUPS += GROUPS % 2
SLOTS = GROUPS * SLOT
PARTS = ((0, 0), (0, 1), (1, 0))
ZERO_DMAS = 5
ZERO_COLS = SLOTS * D // (ZERO_DMAS * P)


class Chain:

    def __init__(self, eng, sem, per_turn):
        self.eng, self.sem, self.per_turn, self.base, self.n = eng, sem, per_turn, 0, 0

    def turn(self, i):
        self.base, self.n = i * self.per_turn, 0

    def end(self):
        assert self.n == self.per_turn, (self.n, self.per_turn)

    def mark(self, ins):
        ins.then_inc(self.sem, 1)
        self.n += 1

    def wait(self):
        self.eng.wait_ge(self.sem, self.base + self.n)

    def link(self, ins):
        self.mark(ins)
        self.wait()


def rsqrt(chain, v, r, t, ti):
    ve = chain.eng
    chain.link(ve.tensor_scalar(ti, v.bitcast(I32), 1, None, ALU.logical_shift_right))
    chain.link(ve.tensor_scalar(r.bitcast(I32), ti, -1.0, float(0x5F3759DF), ALU.mult, ALU.add))
    for _ in range(3):
        chain.link(ve.tensor_tensor(t, r, r, ALU.mult))
        chain.link(ve.tensor_tensor(t, t, v, ALU.mult))
        chain.link(ve.tensor_scalar(t, t, -0.5, 1.5, ALU.mult, ALU.add))
        chain.link(ve.tensor_tensor(r, r, t, ALU.mult))


RSQRT_LINKS = 14


def layernorm(chain, z, out, stats, small, smalli, n):
    ve = chain.eng
    for b in range(n):
        chain.mark(ve.bn_stats(stats[:, b, :], z[:, b, :]))
    chain.wait()
    mean, half, v, r, t = (small[:, k, 0:n] for k in range(5))
    chain.mark(ve.tensor_tensor(mean, stats[:, 0:n, 1], stats[:, 0:n, 4], ALU.add))
    chain.mark(ve.tensor_tensor(half, stats[:, 0:n, 1], stats[:, 0:n, 4], ALU.subtract))
    chain.link(ve.tensor_tensor(v, stats[:, 0:n, 2], stats[:, 0:n, 5], ALU.add))
    chain.mark(ve.tensor_scalar(mean, mean, 0.5, None, ALU.mult))
    chain.mark(ve.tensor_tensor(half, half, half, ALU.mult))
    chain.link(ve.tensor_scalar(v, v, 1.0 / D, EPS, ALU.mult, ALU.add))
    chain.link(ve.scalar_tensor_tensor(v, half, 0.25, v, ALU.mult, ALU.add))
    rsqrt(chain, v, r, t, smalli[:, 0:n])
    last = None
    for b in range(n):
        last = ve.tensor_scalar(out[:, b, :], z[:, b, :], mean[:, b:b + 1], r[:, b:b + 1], ALU.subtract, ALU.mult)
    return last


LN_LINKS = 4 + 3 + 3 + 1 + RSQRT_LINKS


def phase_ssd(nc, x, xt, w, dtb, alog, dskip, masks, x1):
    NB = BATCH * HEADS0
    RW = HEADS0 + STATE0
    with ExitStack() as outer:
        def sb(name, shape, dt=F32, ctx=outer):
            return ctx.enter_context(nc.sbuf_tensor("a_" + name, shape, dt))

        def sem(name, ctx=outer):
            return ctx.enter_context(nc.semaphore("a_" + name))

        bt_all = sb("bt_all", [STATE0, STEPS, TOK])
        ct_all = sb("ct_all", [STATE0, STEPS, TOK])
        rows = sb("rows", [P, STEPS, BATCH, RW])
        tri = sb("tri", [P, P])
        strict = sb("strict", [P, P])
        ones = sb("ones", [P, P])
        dt = sb("dt", [P, STEPS, NB])
        a = sb("a", [P, STEPS, NB])
        dec = sb("dec", [P, 3, STEPS, NB])
        dx = sb("dx", [P, STEPS, NB])
        dcoef = sb("dcoef", [P, D])

        with ExitStack() as ctx:
            wsb = sb("w", [P, KD, 2 * STATE0 + HEADS0], ctx=ctx)
            xts = sb("xts", [P, 2, KD, TOK], ctx=ctx)
            dtb_sb = sb("dtb", [P, NB], ctx=ctx)
            nega = sb("nega", [P, NB], ctx=ctx)
            neg = sb("neg", [P, NB], ctx=ctx)
            dsk = sb("dsk", [P, HEADS0], ctx=ctx)
            z = sb("z", [P, STEPS, NB], ctx=ctx)
            e = sb("e", [P, STEPS, NB], ctx=ctx)
            l1 = sb("l1", [P, STEPS, NB], ctx=ctx)
            q = sb("q", [P, STEPS, NB], ctx=ctx)
            ps = ctx.enter_context(nc.psum_tensor("a_ps", [P, 8, 512], F32))
            consts_in = sem("consts_in", ctx)
            xt_in = [sem(f"xt_in{k}", ctx) for k in range(2)]
            proj = sem("proj", ctx)
            bc_out = sem("bc_out", ctx)
            rows_out = sem("rows_out", ctx)
            dve_own = sem("dve_own0", ctx)
            nega_done = sem("nega_done", ctx)
            na_ready = sem("na_ready", ctx)
            act_own = sem("act_own0", ctx)
            log_ready = sem("log_ready", ctx)
            a_ready = sem("a_ready", ctx)
            cum_ready = sem("cum_ready", ctx)
            dec_ready = sem("dec_ready", ctx)
            block = ctx.enter_context(nc.Block())
            W2 = HEADS0

            @block.sync
            def _(sp):
                sp.dma_start(wsb[:], w).then_inc(consts_in, 16)
                sp.dma_start(tri[:], masks[0]).then_inc(consts_in, 16)
                sp.dma_start(strict[:], masks[1]).then_inc(consts_in, 16)
                sp.dma_start(ones[:], masks[2]).then_inc(consts_in, 16)
                for b in range(BATCH):
                    sp.dma_start(dtb_sb[:, b * HEADS0:(b + 1) * HEADS0], dtb.partition_broadcast(P)).then_inc(consts_in, 16)
                    sp.dma_start(nega[:, b * HEADS0:(b + 1) * HEADS0], alog.partition_broadcast(P)).then_inc(consts_in, 16)
                sp.dma_start(dsk[:], dskip.partition_broadcast(P)).then_inc(consts_in, 16)
                with sp.Fori(0, STEPS // 2) as j:
                    for k in range(2):
                        sp.wait_ge(proj, 2 * j)
                        sp.dma_start(xts[:, k], xt[2 * j + k]).then_inc(xt_in[k], 16)

            CONSTS = 16 * (5 + 2 * BATCH)

            @block.tensor
            def _(pe):
                pe.wait_ge(consts_in, CONSTS)
                with pe.Fori(0, STEPS // 2) as j:
                    for k in range(2):
                        pe.wait_ge(xt_in[k], 16 * (j + 1))
                        pe.wait_ge(bc_out, 2 * (2 * j))
                        pe.wait_ge(rows_out, 2 * j)
                        for part in range(2):
                            lo = W2 + part * STATE0
                            for kd in range(KD):
                                pe.matmul(ps[0:STATE0, 4 * k + part, :], wsb[:, kd, lo:lo + STATE0], xts[:, k, kd, :],
                                          start=kd == 0, stop=kd == KD - 1)
                        for b in range(BATCH):
                            for kd in range(KD):
                                mm = pe.matmul(ps[:, 4 * k + 2, b * RW:(b + 1) * RW], xts[:, k, kd, b * P:(b + 1) * P],
                                               wsb[:, kd, 0:RW], start=kd == 0, stop=kd == KD - 1)
                        mm.then_inc(proj, 1)
                pe.wait_ge(a_ready, 1)
                af = a[:].rearrange("p c n -> p (c n)")
                for n, mask in enumerate((tri, strict, ones)):
                    mm = pe.matmul(ps[:, n, 0:STEPS * NB], mask[:], af, start=True, stop=True)
                mm.then_inc(cum_ready, 1)

            @block.scalar
            def _(act):
                act.wait_ge(consts_in, CONSTS)
                nc.scalar.activation(neg[:], nega[:], ACT.Exp).then_inc(nega_done, 1)
                with act.Fori(0, STEPS // 2) as j:
                    for k in range(2):
                        act.wait_ge(proj, 2 * j + k + 1)
                        act.activation(bt_all[:, 2 * j + k, :], ps[0:STATE0, 4 * k, :], ACT.Copy).then_inc(bc_out, 1)
                        act.activation(ct_all[:, 2 * j + k, :], ps[0:STATE0, 4 * k + 1, :], ACT.Copy).then_inc(bc_out, 1)
                act.wait_ge(na_ready, 1)
                act.activation(e[:], l1[:], ACT.Exp).then_inc(act_own, 1)
                act.wait_ge(act_own, 1)
                act.activation(q[:], e[:], ACT.Ln, bias=1.0).then_inc(log_ready, 1)
                act.wait_ge(cum_ready, 1)
                for n in range(3):
                    act.activation(dec[:, n].rearrange("p c n -> p (c n)"), ps[:, n, 0:STEPS * NB], ACT.Exp).then_inc(dec_ready, 1)

            @block.vector
            def _(ve):
                ch = Chain(ve, dve_own, 100)
                ve.wait_ge(consts_in, CONSTS)
                for h in range(HEADS0):
                    ch.mark(ve.tensor_scalar(dcoef[:, h * P:(h + 1) * P], ones[:], dsk[:, h:h + 1], None, ALU.add))
                with ve.Fori(0, STEPS // 2) as j:
                    for k in range(2):
                        ve.wait_ge(proj, 2 * j + k + 1)
                        ve.tensor_copy(rows[:, 2 * j + k].rearrange("p b w -> p (b w)"), ps[:, 4 * k + 2, 0:BATCH * RW]).then_inc(rows_out, 1)
                ve.wait_ge(rows_out, STEPS)
                bias = dtb_sb[:].rearrange("p (b h) -> p b h", b=BATCH)
                for c in range(STEPS):
                    ch.mark(ve.tensor_tensor(z[:, c].rearrange("p (b h) -> p b h", b=BATCH), rows[:, c, :, 0:HEADS0], bias, ALU.add))
                ch.wait()
                ve.scalar_tensor_tensor(l1[:], z[:], -1.0, z[:], ALU.mult, ALU.min).then_inc(na_ready, 1)
                ve.wait_ge(log_ready, 1)
                ch.link(ve.tensor_scalar(l1[:], e[:], 0.2, -0.25, ALU.mult, ALU.add))
                for cst in (1.0 / 3.0, -0.5, 1.0):
                    ch.link(ve.tensor_tensor(l1[:], l1[:], e[:], ALU.mult))
                    ch.link(ve.tensor_scalar(l1[:], l1[:], cst, None, ALU.add))
                ch.link(ve.tensor_tensor(l1[:], l1[:], e[:], ALU.mult))
                ch.link(ve.tensor_tensor(l1[:], l1[:], q[:], ALU.subtract))
                ch.link(ve.tensor_scalar(e[:], e[:], 1.0 / 32.0, None, ALU.is_lt))
                ch.link(ve.tensor_tensor(l1[:], l1[:], e[:], ALU.mult))
                ch.link(ve.tensor_tensor(q[:], q[:], l1[:], ALU.add))
                ch.link(ve.scalar_tensor_tensor(dt[:], z[:], 0.0, q[:], ALU.max, ALU.add))
                ve.wait_ge(nega_done, 1)
                ch.link(ve.tensor_scalar(neg[:], neg[:], -1.0, None, ALU.mult))
                for c in range(STEPS):
                    ins = ve.tensor_tensor(a[:, c], dt[:, c], neg[:], ALU.mult)
                    if c < STEPS - 1:
                        ch.mark(ins)
                ins.then_inc(a_ready, 1)
                ve.wait_ge(dec_ready, 3)
                ch.link(ve.tensor_tensor(dx[:], dt[:], dec[:, 1], ALU.mult))

        with ExitStack() as ctx:
            xr = sb("xr", [P, 2, BATCH, D], ctx=ctx)
            bs = sb("bs", [P, 2, BATCH, STATE0], ctx=ctx)
            btc = sb("btc", [STATE0, 2, 2, TOK], ctx=ctx)
            seg = sb("seg", [P, 2, BATCH // 2, HEADS0, P], ctx=ctx)
            lm = sb("lm", [P, 2, BATCH // 2, HEADS0, P], ctx=ctx)
            gm = sb("gm", [P, BATCH, P], ctx=ctx)
            mt = sb("mt", [P, BATCH, HEADS0, P], ctx=ctx)
            xdt = sb("xdt", [P, BATCH, D], ctx=ctx)
            xdd = sb("xdd", [P, BATCH, D], ctx=ctx)
            zz = sb("zz", [P, 2, BATCH, D], ctx=ctx)
            z2 = sb("z2", [P, BATCH, D], ctx=ctx)
            st = sb("st", [STATE0, BATCH, D], ctx=ctx)
            out = sb("out", [P, 2, BATCH, D], ctx=ctx)
            stats = sb("stats", [P, BATCH, 6], ctx=ctx)
            small = sb("small", [P, 5, BATCH], ctx=ctx)
            smalli = sb("smalli", [P, BATCH], I32, ctx=ctx)
            ps = ctx.enter_context(nc.psum_tensor("a_ps2", [P, 8, 512], F32))
            G, SEG, YD, YO, ST = 0, 1, 3, 5, 5
            names = ("seg_ready", "seg_done", "l_ready", "g_done", "m_ready", "yd_done", "yo_done",
                     "yo_read", "st_done", "st_new", "xdt_ready", "xdd_ready", "t1_ready", "y_read", "out_ready", "z_ready")
            s = {n: sem(n, ctx) for n in names}
            x_in = [sem(f"x_in{k}", ctx) for k in range(2)]
            stored = [sem(f"stored{k}", ctx) for k in range(2)]
            dve_own = sem("dve_own", ctx)
            pool_own = sem("pool_own", ctx)
            block = ctx.enter_context(nc.Block())
            LOADS = 16 * 4

            @block.sync
            def _(sp):
                with sp.Fori(0, STEPS // 2) as j:
                    for k in range(2):
                        i = 2 * j + k
                        sp.wait_ge(s["st_done"], 2 * j)
                        sp.wait_ge(s["xdd_ready"], 2 * j)
                        sp.wait_ge(s["t1_ready"], 2 * j)
                        sp.wait_ge(s["yo_done"], 2 * j)
                        sp.dma_start(xr[:, k], x[i]).then_inc(x_in[k], 16)
                        sp.dma_start(bs[:, k], rows[:, i, :, HEADS0:RW]).then_inc(x_in[k], 16)
                        sp.dma_start(btc[:, k, 0], bt_all[:, i, :]).then_inc(x_in[k], 16)
                        sp.dma_start(btc[:, k, 1], ct_all[:, i, :]).then_inc(x_in[k], 16)

            @block.gpsimd
            def _(gp):
                gp.memset(st[:], 0.0).then_inc(s["st_new"], 1)
                with gp.Fori(0, STEPS // 2) as j:
                    for k in range(2):
                        i = 2 * j + k
                        gp.wait_ge(x_in[k], LOADS * (j + 1))
                        gp.wait_ge(s["yd_done"], i)
                        gp.wait_ge(s["st_done"], i)
                        for dst, weight, ready in ((xdt, dt, "xdt_ready"), (xdd, dx, "xdd_ready")):
                            by_head = weight[:, i, :].rearrange("p (n o) -> p n o", o=1).to_broadcast([P, NB, P])
                            gp.tensor_tensor(dst[:].rearrange("p b (h d) -> p (b h) d", h=HEADS0),
                                             xr[:, k].rearrange("p b (h d) -> p (b h) d", h=HEADS0), by_head, ALU.mult).then_inc(s[ready], 1)
                        gp.wait_ge(s["y_read"], 2 * j)
                        for b in range(BATCH):
                            last = gp.tensor_tensor(zz[:, k, b], xr[:, k, b], dcoef[:], ALU.mult)
                        last.then_inc(s["t1_ready"], 1)

            @block.tensor
            def _(pe):
                pe.wait_ge(s["st_new"], 1)
                with pe.Fori(0, STEPS // 2) as j:
                    for k in range(2):
                        i = 2 * j + k
                        pe.wait_ge(x_in[k], LOADS * (j + 1))
                        pe.wait_ge(s["m_ready"], i)
                        for b in range(BATCH):
                            mm = pe.matmul(ps[:, G, b * P:(b + 1) * P], btc[:, k, 0, b * P:(b + 1) * P],
                                           btc[:, k, 1, b * P:(b + 1) * P], start=True, stop=True)
                        mm.then_inc(s["g_done"], 1)
                        for half in range(2):
                            pe.wait_ge(s["seg_ready"], 2 * i + half + 1)
                            pe.matmul(ps[:, SEG + half, :], strict[:], seg[:, half].rearrange("p b h l -> p (b h l)"),
                                      start=True, stop=True).then_inc(s["seg_done"], 1)
                        pe.wait_ge(s["st_new"], BATCH * i + 1)
                        for b in range(BATCH):
                            mm = pe.matmul(ps[:, YO + b // 2, (b % 2) * D:(b % 2 + 1) * D], btc[:, k, 1, b * P:(b + 1) * P],
                                           st[:, b, :], start=b % 2 == 0, stop=b % 2 == 1, skip_group_check=True)
                        mm.then_inc(s["yo_done"], 1)
                        pe.wait_ge(s["m_ready"], i + 1)
                        pe.wait_ge(s["xdt_ready"], i + 1)
                        pe.wait_ge(s["y_read"], i)
                        for b in range(BATCH):
                            for h in range(HEADS0):
                                lo = (b % 2) * D + h * P
                                mm = pe.matmul(ps[:, YD + b // 2, lo:lo + P], mt[:, b, h, :], xdt[:, b, h * P:(h + 1) * P],
                                               start=True, stop=True)
                        mm.then_inc(s["yd_done"], 1)
                        pe.wait_ge(s["xdd_ready"], i + 1)
                        pe.wait_ge(s["yo_read"], i + 1)
                        for b in range(BATCH):
                            mm = pe.matmul(ps[0:STATE0, ST + b // 2, (b % 2) * D:(b % 2 + 1) * D], bs[:, k, b, :],
                                           xdd[:, b, :], start=True, stop=True)
                        mm.then_inc(s["st_done"], 1)

            @block.scalar
            def _(act):
                with act.Fori(0, STEPS // 2) as j:
                    for k in range(2):
                        i = 2 * j + k
                        for half in range(2):
                            act.wait_ge(s["seg_done"], 2 * i + half + 1)
                            act.wait_ge(s["m_ready"], i)
                            act.activation(lm[:, half].rearrange("p b h l -> p (b h l)"), ps[:, SEG + half, :], ACT.Exp).then_inc(s["l_ready"], 1)
                        act.wait_ge(s["out_ready"], i + 1)
                        act.dma_start(x1[i], out[:, k]).then_inc(stored[k], 16)
                for k in range(2):
                    act.wait_ge(stored[k], 16 * (STEPS // 2))

            @block.vector
            def _(ve):
                NV = LN_LINKS + 1 + 3 + 8
                ch = Chain(ve, dve_own, NV)
                with ve.Fori(0, STEPS // 2) as j:
                    for k in range(2):
                        i = 2 * j + k
                        ch.turn(i)
                        ve.wait_ge(s["seg_done"], 2 * i)
                        for half in range(2):
                            for b in range(BATCH // 2):
                                for h in range(HEADS0):
                                    n = (half * BATCH // 2 + b) * HEADS0 + h
                                    last = ve.tensor_scalar(seg[:, half, b, h, :], tri[:], a[:, i, n:n + 1], None, ALU.mult)
                            last.then_inc(s["seg_ready"], 1)
                        ve.wait_ge(s["g_done"], i + 1)
                        ve.wait_ge(s["yd_done"], i)
                        ch.link(ve.tensor_tensor(gm[:], ps[:, G, :].rearrange("p (b l) -> p b l", b=BATCH),
                                                 tri[:].unsqueeze(1).to_broadcast([P, BATCH, P]), ALU.mult))
                        ve.wait_ge(s["l_ready"], 2 * i + 2)
                        for h in range(HEADS0):
                            for half in range(2):
                                bb = slice(half * 2, half * 2 + 2)
                                last = ve.tensor_tensor(mt[:, bb, h, :], gm[:, bb, :], lm[:, half, :, h, :], ALU.mult)
                                if (h, half) != (1, 1):
                                    ch.mark(last)
                        last.then_inc(s["m_ready"], 1)
                        ve.wait_ge(s["yo_done"], i + 1)
                        ve.wait_ge(s["t1_ready"], i + 1)
                        for b in range(BATCH):
                            for h in range(HEADS0):
                                n, cols = b * HEADS0 + h, slice(h * P, (h + 1) * P)
                                lo = (b % 2) * D + h * P
                                last = ve.scalar_tensor_tensor(z2[:, b, cols], ps[:, YO + b // 2, lo:lo + P], dec[:, 0, i, n:n + 1],
                                                               zz[:, k, b, cols], ALU.mult, ALU.add)
                                if n < 7:
                                    ch.mark(last)
                        last.then_inc(s["yo_read"], 1)
                        ve.wait_ge(s["yo_read"], i + 1)
                        ve.wait_ge(s["yd_done"], i + 1)
                        for half in range(2):
                            bb = slice(half * 2, half * 2 + 2)
                            last = ve.tensor_tensor(z2[:, bb], ps[:, YD + half, :].rearrange("p (b d) -> p b d", b=2), z2[:, bb], ALU.add)
                            if half == 0:
                                ch.mark(last)
                        last.then_inc(s["y_read"], 1)
                        ve.wait_ge(s["st_done"], i + 1)
                        for b in range(BATCH):
                            for h in range(HEADS0):
                                n, cols = b * HEADS0 + h, slice(h * P, (h + 1) * P)
                                lo = (b % 2) * D + h * P
                                last = ve.scalar_tensor_tensor(st[:, b, cols], st[:, b, cols], dec[0:STATE0, 2, i, n:n + 1],
                                                               ps[0:STATE0, ST + b // 2, lo:lo + P], ALU.mult, ALU.add)
                            last.then_inc(s["st_new"], 1)
                        ve.wait_ge(s["y_read"], i + 1)
                        ve.wait_ge(stored[k], 16 * j)
                        layernorm(ch, z2, out[:, k], stats, small, smalli, BATCH).then_inc(s["out_ready"], 1)
                        ch.end()


def phase_ffn(nc, x1, w1, b1, w2, b2, ident, x2, xg=None, zeros_done=None):
    HM = w1.shape[2] // P
    with ExitStack() as ctx:
        def sb(name, shape, dt=F32):
            return ctx.enter_context(nc.sbuf_tensor("b_" + name, shape, dt))

        def sem(name):
            return ctx.enter_context(nc.semaphore("b_" + name))

        w1s = sb("w1", [P, KD, HM * P])
        w2s = sb("w2", [P, HM, D])
        b1s = sb("b1", [P, HM])
        b2s = sb("b2", [P, D])
        ids = sb("ident", [P, P])
        xr = sb("xr", [P, 2, BATCH, D])
        xb = sb("xb", [P, 2, BATCH, D])
        xts = sb("xts", [P, 2, KD, TOK])
        ht = sb("ht", [P, 2, TOK])
        z = sb("z", [P, BATCH, D])
        out = sb("out", [P, 2, BATCH, D])
        stats = sb("stats", [P, BATCH, 6])
        small = sb("small", [P, 5, BATCH])
        smalli = sb("smalli", [P, BATCH], I32)
        ps = ctx.enter_context(nc.psum_tensor("b_ps", [P, 8, 512], F32))
        T, H, O = 0, 2, 4
        names = ("weights_in", "turned", "xt_ready", "h_done", "h_ready", "h_used", "o_done", "xb_ready", "z_ready", "out_ready", "dve_own")
        s = {n: sem(n) for n in names}
        x_in = [sem(f"x_in{k}") for k in range(2)]
        stored = [sem(f"stored{k}") for k in range(2)]
        zeros = sb("zeros", [P, ZERO_COLS])
        zeros_set = sem("zeros_set")
        block = ctx.enter_context(nc.Block())
        WEIGHTS = 16 * 5

        @block.sync
        def _(sp):
            sp.dma_start(ids[:], ident).then_inc(s["weights_in"], 16)
            for dst, src in ((w1s[:], w1), (b1s[:], b1), (w2s[:], w2), (b2s[:], b2.partition_broadcast(P))):
                sp.dma_start(dst, src).then_inc(s["weights_in"], 16)
            with sp.Fori(0, STEPS // 2) as j:
                for k in range(2):
                    sp.wait_ge(s["turned"], 2 * j)
                    sp.wait_ge(s["xb_ready"], 2 * j)
                    sp.dma_start(xr[:, k], x1[2 * j + k]).then_inc(x_in[k], 16)

        @block.gpsimd
        def _(gp):
            if xg is not None:
                gp.memset(zeros[:], 0.0).then_inc(zeros_set, 1)
                gp.wait_ge(zeros_set, 1)
                cleared = xg.rearrange("(n p m) d -> n p (m d)", p=P, n=ZERO_DMAS)
                for n in range(ZERO_DMAS):
                    gp.dma_start(cleared[n], zeros[:]).then_inc(zeros_done, 16)
            gp.wait_ge(s["weights_in"], WEIGHTS)
            with gp.Fori(0, STEPS // 2) as j:
                for k in range(2):
                    gp.wait_ge(x_in[k], 16 * (j + 1))
                    gp.wait_ge(s["z_ready"], 2 * j)
                    gp.tensor_tensor(xb[:, k], xr[:, k], b2s[:].unsqueeze(1).to_broadcast([P, BATCH, D]), ALU.add).then_inc(s["xb_ready"], 1)
                    gp.wait_ge(s["out_ready"], 2 * j + k + 1)
                    gp.dma_start(x2[2 * j + k], out[:, k]).then_inc(stored[k], 16)
            for k in range(2):
                gp.wait_ge(stored[k], 16 * (STEPS // 2))

        @block.tensor
        def _(pe):
            pe.wait_ge(s["weights_in"], WEIGHTS)
            with pe.Fori(0, STEPS // 2) as j:
                for k in range(2):
                    i = 2 * j + k
                    pe.wait_ge(x_in[k], 16 * (j + 1))
                    pe.wait_ge(s["xt_ready"], i)
                    for kd in range(KD):
                        for b in range(BATCH):
                            mm = pe.transpose(ps[:, T + kd, b * P:(b + 1) * P], xr[:, k, b, kd * P:(kd + 1) * P], ids[:])
                    mm.then_inc(s["turned"], 1)

                    def down(m):
                        pe.wait_ge(s["h_ready"], HM * i + m + 1)
                        for b in range(BATCH):
                            lo = (b % 2) * D
                            mm = pe.matmul(ps[:, O + 2 * k + b // 2, lo:lo + D], ht[:, m % 2, b * P:(b + 1) * P], w2s[:, m, :],
                                           start=m == 0 and b % 2 == 0, stop=m == HM - 1, skip_group_check=True)
                        mm.then_inc(s["h_used"], 1)
                        return mm

                    pe.wait_ge(s["xt_ready"], i + 1)
                    pe.wait_ge(s["z_ready"], 2 * j)
                    for m in range(HM):
                        pe.wait_ge(s["h_ready"], HM * i + max(m - 1, 0))
                        for kd in range(KD):
                            mm = pe.matmul(ps[:, H + m % 2, :], w1s[:, kd, m * P:(m + 1) * P], xts[:, k, kd, :],
                                           start=kd == 0, stop=kd == KD - 1)
                        mm.then_inc(s["h_done"], 1)
                        if m:
                            down(m - 1)
                    down(HM - 1)

        @block.scalar
        def _(act):
            act.wait_ge(s["weights_in"], WEIGHTS)
            with act.Fori(0, STEPS // 2) as j:
                for k in range(2):
                    i = 2 * j + k
                    act.wait_ge(s["turned"], i + 1)
                    act.activation(xts[:, k].rearrange("p k n -> p (k n)"), ps[:, T:T + KD, :].rearrange("p k n -> p (k n)"), ACT.Copy).then_inc(s["xt_ready"], 1)
                    for m in range(HM):
                        act.wait_ge(s["h_done"], HM * i + m + 1)
                        act.wait_ge(s["h_used"], HM * i + max(m - 1, 0))
                        act.activation(ht[:, m % 2, :], ps[:, H + m % 2, :], ACT.Gelu, bias=b1s[:, m:m + 1]).then_inc(s["h_ready"], 1)

        @block.vector
        def _(ve):
            ch = Chain(ve, s["dve_own"], LN_LINKS + 1)
            with ve.Fori(0, STEPS // 2) as j:
                for k in range(2):
                    i = 2 * j + k
                    ch.turn(i)
                    ve.wait_ge(s["xb_ready"], i + 1)
                    ve.wait_ge(s["h_used"], HM * (i + 1))
                    for half in range(2):
                        bb = slice(2 * half, 2 * half + 2)
                        last = ve.tensor_tensor(z[:, bb], ps[:, O + 2 * k + half, :].rearrange("p (b d) -> p b d", b=2), xb[:, k, bb], ALU.add)
                        if half == 0:
                            ch.mark(last)
                    last.then_inc(s["z_ready"], 1)
                    ve.wait_ge(s["z_ready"], i + 1)
                    ve.wait_ge(stored[k], 16 * j)
                    layernorm(ch, z, out[:, k], stats, small, smalli, BATCH).then_inc(s["out_ready"], 1)
                    ch.end()


def phase_attention(nc, x2, wqkv, bqkv, wout, bout, omega, nodes, weights, masks, ident, x3):
    with ExitStack() as ctx:
        def sb(name, shape, dt=F32):
            return ctx.enter_context(nc.sbuf_tensor("c_" + name, shape, dt))

        def sem(name):
            return ctx.enter_context(nc.semaphore("c_" + name))

        wq = sb("wqkv", [P, KD, 3 * D])
        bq = sb("bqkv", [P, 3 * D])
        wo = sb("wout", [P, KD, D])
        bo = sb("bout", [P, D])
        om = sb("omega", [P, KD, P])
        ids = sb("ident", [P, P])
        tri = sb("tri", [P, P])
        nw = sb("nw", [P, 2])
        fc = sb("fc", [P, 4])
        xr = sb("xr", [P, 2, BATCH, D])
        xb = sb("xb", [P, BATCH, D])
        xts = sb("xts", [P, KD, TOK])
        qk = sb("qk", [P, BATCH, 2 * D])
        sq = sb("sq", [P, BATCH, 2 * D])
        va = sb("va", [P, BATCH, HEADS1, VW])
        nrm = sb("nrm", [P, 3, BATCH * 2 * HEADS1])
        nrmi = sb("nrmi", [P, BATCH * 2 * HEADS1], I32)
        qkt = sb("qkt", [P, 2 * KD, TOK])
        ef = sb("ef", [P, 2, TOK])
        cf = sb("cf", [P, 2, 2, TOK])
        ns = sb("ns", [P, 4, P])
        nsi = sb("nsi", [P, P], I32)
        qf = sb("qf", [P, 3, TOK])
        kf = sb("kf", [P, 3, TOK])
        kr = sb("kr", [P, 2, BATCH, P])
        sm = sb("sm", [P, 2, 2, BATCH, P])
        state = sb("state", [P, PAIRS, BATCH, 2 * VW])
        den = sb("den", [P, 2, BATCH, 2])
        cr = sb("cr", [P, BATCH, HEADS1, HD])
        ctxt = sb("ctxt", [P, KD, TOK])
        z = sb("z", [P, BATCH, D])
        out = sb("out", [P, 2, BATCH, D])
        stats = sb("stats", [P, BATCH, 6])
        small = sb("small", [P, 5, BATCH])
        smalli = sb("smalli", [P, BATCH], I32)
        ps = ctx.enter_context(nc.psum_tensor("c_ps", [P, 8, 512], F32))
        names = ("weights_in", "fc_ready", "state_zero", "turned", "xt_ready", "rows_done", "rows_read", "sq_ready",
                 "rnorm_ready", "qn_ready", "qn_turned", "qkt_ready", "feat_done", "exp_done", "clip_done", "qf_ready", "score_done",
                 "mask_done", "kt_done", "kr_ready", "pair_done", "pair_read", "ctx_turned", "ctxt_ready",
                 "proj_done", "z_ready", "xb_ready", "out_ready", "own")
        s = {n: sem(n) for n in names}
        x_in = [sem(f"x_in{k}") for k in range(2)]
        stored = [sem(f"stored{k}") for k in range(2)]
        block = ctx.enter_context(nc.Block())
        WEIGHTS = 16 * 10
        HIGH, LOW, BIAS, AMP = (slice(n, n + 1) for n in range(4))
        FEAT_BANKS = (0, 1, 7)
        SC, KT, OB, SU = 2, 4, 5, 6

        @block.sync
        def _(sp):
            for dst, src in ((wq[:], wqkv), (bq[:], bqkv.partition_broadcast(P)), (wo[:], wout), (bo[:], bout.partition_broadcast(P)),
                             (om[:], omega), (ids[:], ident), (tri[:], masks[0]), (nw[:, 0:1], nodes), (nw[:, 1:2], weights), (ns[:, 0], nodes.rearrange("p o -> (p o)").partition_broadcast(P))):
                sp.dma_start(dst, src).then_inc(s["weights_in"], 16)
            with sp.Fori(0, STEPS // 2) as j:
                for k in range(2):
                    sp.wait_ge(s["turned"], 2 * j)
                    sp.wait_ge(s["xb_ready"], 2 * j)
                    sp.dma_start(xr[:, k], x2[2 * j + k]).then_inc(x_in[k], 16)

        @block.gpsimd
        def _(gp):
            gp.wait_ge(s["weights_in"], WEIGHTS)
            with gp.Fori(0, STEPS // 2) as jj:
                for k in range(2):
                    i = 2 * jj + k
                    gp.wait_ge(s["rows_read"], 6 * i + 6)
                    gp.tensor_tensor(sq[:], qk[:], qk[:], ALU.mult).then_inc(s["sq_ready"], 1)
                    gp.wait_ge(x_in[k], 16 * (jj + 1))
                    gp.wait_ge(s["z_ready"], i)
                    gp.tensor_tensor(xb[:], xr[:, k], bo[:].unsqueeze(1).to_broadcast([P, BATCH, D]), ALU.add).then_inc(s["xb_ready"], 1)
                    gp.wait_ge(s["out_ready"], i + 1)
                    gp.dma_start(x3[i], out[:, k]).then_inc(stored[k], 16)
            for k in range(2):
                gp.wait_ge(stored[k], 16 * (STEPS // 2))

        @block.tensor
        def _(pe):
            pe.wait_ge(s["weights_in"], WEIGHTS)
            pe.wait_ge(s["state_zero"], 1)
            pe.wait_ge(s["fc_ready"], 1)
            with pe.Fori(0, STEPS // 2) as jj:
                for k in range(2):
                    i = 2 * jj + k
                    pe.wait_ge(x_in[k], 16 * (jj + 1))
                    pe.wait_ge(s["ctxt_ready"], i)
                    for kd in range(KD):
                        for b in range(BATCH):
                            mm = pe.transpose(ps[:, kd, b * P:(b + 1) * P], xr[:, k, b, kd * P:(kd + 1) * P], ids[:])
                    mm.then_inc(s["turned"], 1)
                    pe.wait_ge(s["xt_ready"], i + 1)
                    pe.wait_ge(s["z_ready"], i)
                    for half in range(2):
                        for b in (2 * half, 2 * half + 1):
                            if half:
                                pe.wait_ge(s["rows_read"], 6 * i + 1 + b % 2)
                            for kd in range(KD):
                                mm = pe.matmul(ps[:, 2 + b % 2, :], xts[:, kd, b * P:(b + 1) * P], wq[:, kd, 0:2 * D], start=kd == 0, stop=kd == KD - 1)
                            mm.then_inc(s["rows_done"], 1)
                        for b in (2 * half, 2 * half + 1):
                            for kd in range(KD):
                                mm = pe.matmul(ps[:, 4 + half, (b % 2) * D:(b % 2 + 1) * D], xts[:, kd, b * P:(b + 1) * P], wq[:, kd, 2 * D:3 * D],
                                               start=kd == 0, stop=kd == KD - 1)
                        mm.then_inc(s["rows_done"], 1)
                    pe.wait_ge(s["qn_ready"], i + 1)
                    for t in range(2 * KD):
                        for b in range(BATCH):
                            mm = pe.transpose(ps[:, t, b * P:(b + 1) * P], sq[:, b, t * P:(t + 1) * P], ids[:])
                    mm.then_inc(s["qn_turned"], 1)
                    pe.wait_ge(s["qkt_ready"], i + 1)
                    for t in range(PAIRS + 2):
                        if t < PAIRS:
                            rows = slice(32 * (t % 4), 32 * (t % 4) + 32)
                            for q in range(2):
                                n = 2 * t + q
                                pe.wait_ge(s["clip_done"], 2 * PAIRS * i + max(n - 2, 0))
                                pe.matmul(ps[:, FEAT_BANKS[n % 3], :], om[rows, t // 4, :], qkt[rows, KD * q + t // 4, :],
                                          start=True, stop=True).then_inc(s["feat_done"], 1)
                        if 1 <= t <= PAIRS:
                            u = t - 1
                            pe.wait_ge(s["exp_done"], 2 * (PAIRS * i + u + 1))
                            pe.wait_ge(s["qf_ready"], PAIRS * i + u + 1)
                            pe.wait_ge(s["mask_done"], PAIRS * i + u)
                            for b in range(BATCH):
                                for h in range(2):
                                    cols, f = slice(b * P, (b + 1) * P), slice(FD * h, FD * (h + 1))
                                    mm = pe.matmul(ps[:, SC + h, cols], kf[f, u % 3, cols],
                                                   qf[f, u % 3, cols], start=True, stop=True)
                            mm.then_inc(s["score_done"], 1)
                            pe.wait_ge(s["kr_ready"], PAIRS * i + u)
                            for b in range(BATCH):
                                mm = pe.transpose(ps[:, KT, b * P:(b + 1) * P], kf[:, u % 3, b * P:(b + 1) * P], ids[:])
                            mm.then_inc(s["kt_done"], 1)
                        if t >= 2:
                            u = t - 2
                            pe.wait_ge(s["mask_done"], PAIRS * i + u + 1)
                            pe.wait_ge(s["kr_ready"], PAIRS * i + u + 1)
                            pe.wait_ge(s["pair_read"], PAIRS * i + u)
                            if u == 0:
                                pe.wait_ge(s["rows_read"], 6 * (i + 1))
                            for b in range(BATCH):
                                lo = b * 2 * VW
                                pe.matmul(ps[:, OB, lo:lo + 2 * VW], qf[:, u % 3, b * P:(b + 1) * P], state[:, u, b, :],
                                          start=True, stop=False, skip_group_check=True)
                                for h in range(2):
                                    pe.matmul(ps[:, OB, lo + h * VW:lo + (h + 1) * VW], sm[:, u % 2, h, b, :], va[:, b, 2 * u + h, :],
                                              start=False, stop=True, skip_group_check=True)
                            for b in range(BATCH):
                                lo = b * 2 * VW
                                mm = pe.matmul(ps[:, SU, lo:lo + 2 * VW], kr[:, u % 2, b, :], va[:, b, 2 * u:2 * u + 2, :], start=True, stop=True)
                            mm.then_inc(s["pair_done"], 1)
                    pe.wait_ge(s["pair_read"], PAIRS * (i + 1))
                    for kd in range(KD):
                        for b in range(BATCH):
                            mm = pe.transpose(ps[:, kd, b * P:(b + 1) * P], cr[:, b, 8 * kd:8 * (kd + 1), :], ids[:])
                    mm.then_inc(s["ctx_turned"], 1)
                    pe.wait_ge(s["ctxt_ready"], i + 1)
                    for b in range(BATCH):
                        for kd in range(KD):
                            mm = pe.matmul(ps[:, 2 + b // 2, (b % 2) * D:(b % 2 + 1) * D], ctxt[:, kd, b * P:(b + 1) * P], wo[:, kd, :],
                                           start=kd == 0, stop=kd == KD - 1)
                    mm.then_inc(s["proj_done"], 1)

        @block.scalar
        def _(act):
            act.wait_ge(s["fc_ready"], 1)
            with act.Fori(0, STEPS // 2) as jj:
                for k in range(2):
                    i = 2 * jj + k
                    act.wait_ge(s["turned"], i + 1)
                    act.activation(xts[:].rearrange("p k n -> p (k n)"), ps[:, 0:KD, :].rearrange("p k n -> p (k n)"), ACT.Copy).then_inc(s["xt_ready"], 1)
                    act.wait_ge(s["qn_turned"], i + 1)
                    act.activation(qkt[:].rearrange("p k n -> p (k n)"), ps[:, 0:2 * KD, :].rearrange("p k n -> p (k n)"), ACT.Copy).then_inc(s["qkt_ready"], 1)
                    for t in range(PAIRS + 1):
                        if t < PAIRS:
                            for q in range(2):
                                n = 2 * t + q
                                act.wait_ge(s["clip_done"], 2 * PAIRS * i + n + 1)
                                if q == 0:
                                    act.wait_ge(s["qf_ready"], PAIRS * i + max(t - 1, 0))
                                    dst = ef[:, t % 2, :]
                                else:
                                    act.wait_ge(s["pair_done"], PAIRS * i + max(t - 2, 0))
                                    dst = kf[:, t % 3, :]
                                act.activation(dst, cf[:, t % 2, q], ACT.Exp, bias=fc[:, BIAS]).then_inc(s["exp_done"], 1)
                        if t >= 1:
                            u = t - 1
                            act.wait_ge(s["kt_done"], PAIRS * i + u + 1)
                            act.wait_ge(s["pair_done"], PAIRS * i + max(u - 1, 0))
                            act.activation(kr[:, u % 2].rearrange("p b f -> p (b f)"), ps[:, KT, :], ACT.Copy).then_inc(s["kr_ready"], 1)
                    act.wait_ge(s["ctx_turned"], i + 1)
                    act.activation(ctxt[:].rearrange("p k n -> p (k n)"), ps[:, 0:KD, :].rearrange("p k n -> p (k n)"), ACT.Copy).then_inc(s["ctxt_ready"], 1)

        @block.vector
        def _(ve):
            pre = Chain(ve, s["own"], 0)
            ve.memset(state[:], 0.0).then_inc(s["state_zero"], 1)
            pre.mark(ve.memset(va[:], 1.0))
            ve.wait_ge(s["weights_in"], WEIGHTS)
            pre.link(ve.tensor_scalar(ns[:, 1], ns[:, 0], 0.0, 2.0, ALU.max, ALU.mult))
            rsqrt(pre, ns[:, 1], ns[:, 2], ns[:, 3], nsi[:])
            pre.link(ve.tensor_tensor(ns[:, 1], ns[:, 1], ns[:, 2], ALU.mult))
            for kd in range(KD):
                pre.mark(ve.tensor_tensor(om[:, kd], om[:, kd], ns[:, 1], ALU.mult))
            pre.mark(ve.tensor_scalar(fc[:, HIGH], nw[:, 0:1], 20.0, None, ALU.add))
            pre.mark(ve.tensor_scalar(fc[:, LOW], nw[:, 0:1], -20.0, None, ALU.add))
            pre.link(ve.tensor_scalar(fc[:, BIAS], nw[:, 0:1], -1.0, None, ALU.mult))
            ve.tensor_scalar(fc[:, AMP], nw[:, 1:2], 0.0, 1.0 / MF, ALU.max, ALU.mult).then_inc(s["fc_ready"], 1)
            PRE = pre.n
            NV = 2 + 2 + RSQRT_LINKS + 5 * PAIRS + 1 + LN_LINKS
            ch = Chain(ve, s["own"], NV)
            with ve.Fori(0, STEPS // 2) as jj:
                for k in range(2):
                    i = 2 * jj + k
                    ch.turn(i)
                    ch.base = ch.base + PRE
                    ve.wait_ge(s["qn_turned"], i)
                    for half in range(2):
                        for b in (2 * half, 2 * half + 1):
                            ve.wait_ge(s["rows_done"], 6 * i + 3 * half + b % 2 + 1)
                            ve.tensor_tensor(qk[:, b, :], ps[:, 2 + b % 2, :], bq[:, 0:2 * D], ALU.add).then_inc(s["rows_read"], 1)
                        ve.wait_ge(s["rows_done"], 6 * i + 3 * half + 3)
                        bb = slice(2 * half, 2 * half + 2)
                        for b in (2 * half, 2 * half + 1):
                            last = ve.tensor_tensor(va[:, b, :, 0:HD], ps[:, 4 + half, (b % 2) * D:(b % 2 + 1) * D].rearrange("p (h d) -> p h d", h=HEADS1),
                                                    bq[:, 2 * D:].rearrange("p (h d) -> p h d", h=HEADS1), ALU.add)
                            if b % 2 == 0:
                                ch.mark(last)
                        last.then_inc(s["rows_read"], 1)
                    ve.wait_ge(s["sq_ready"], i + 1)
                    nv, nr, nt = nrm[:, 0, :], nrm[:, 1, :], nrm[:, 2, :]
                    ch.link(ve.tensor_reduce(nv, sq[:].rearrange("p b (n d) -> p (b n) d", d=HD), AX.X, ALU.add))
                    ch.link(ve.tensor_scalar(nv, nv, 1e-24, None, ALU.max))
                    rsqrt(ch, nv, nr, nt, nrmi[:])
                    ve.tensor_tensor(sq[:].rearrange("p b (n d) -> p (b n) d", d=HD), qk[:].rearrange("p b (n d) -> p (b n) d", d=HD),
                                     nr.unsqueeze(2).to_broadcast([P, BATCH * 2 * HEADS1, HD]), ALU.mult).then_inc(s["qn_ready"], 1)
                    for t in range(PAIRS + 2):
                        if t < PAIRS:
                            for q in range(2):
                                n = 2 * t + q
                                ve.wait_ge(s["feat_done"], 2 * PAIRS * i + n + 1)
                                ve.wait_ge(s["exp_done"], 2 * PAIRS * i + max(n - 3, 0))
                                ve.tensor_scalar(cf[:, t % 2, q], ps[:, FEAT_BANKS[n % 3], :], fc[:, HIGH], fc[:, LOW],
                                                 ALU.min, ALU.max).then_inc(s["clip_done"], 1)
                        if 1 <= t <= PAIRS:
                            u = t - 1
                            ve.wait_ge(s["score_done"], PAIRS * i + u + 1)
                            ve.wait_ge(s["pair_done"], PAIRS * i + max(u - 1, 0))
                            for h in range(2):
                                ins = ve.tensor_tensor(sm[:, u % 2, h], ps[:, SC + h, :].rearrange("p (b t) -> p b t", t=P),
                                                       tri[:].unsqueeze(1).to_broadcast([P, BATCH, P]), ALU.mult)
                                if h == 0:
                                    ch.mark(ins)
                            ins.then_inc(s["mask_done"], 1)
                        if t >= 2:
                            u = t - 2
                            ve.wait_ge(s["pair_done"], PAIRS * i + u + 1)
                            ob = ps[:, OB, 0:BATCH * 2 * VW].rearrange("p (b h w) -> p b h w", b=BATCH, h=2)
                            su = ps[:, SU, 0:BATCH * 2 * VW].rearrange("p (b w) -> p b w", b=BATCH)
                            dd = den[:, 0]
                            ch.link(ve.tensor_scalar(dd, ob[:, :, :, HD], 1e-6, None, ALU.max))
                            ch.link(ve.reciprocal(den[:, 1], dd))
                            ch.mark(ve.tensor_tensor(cr[:, :, 2 * u:2 * u + 2, :], ob[:, :, :, 0:HD],
                                             den[:, 1].unsqueeze(3).to_broadcast([P, BATCH, 2, HD]), ALU.mult))
                            for h in range(2):
                                f, c = slice(FD * h, FD * (h + 1)), slice(VW * h, VW * (h + 1))
                                ins = ve.tensor_tensor(state[f, u, :, c], su[f, :, c], state[f, u, :, c], ALU.add)
                                if h == 0:
                                    ch.mark(ins)
                            ins.then_inc(s["pair_read"], 1)
                        if t < PAIRS:
                            ve.wait_ge(s["exp_done"], 2 * PAIRS * i + 2 * t + 1)
                            ve.wait_ge(s["pair_done"], PAIRS * i + max(t - 2, 0))
                            ve.tensor_scalar(qf[:, t % 3, :], ef[:, t % 2, :], fc[:, AMP], None, ALU.mult).then_inc(s["qf_ready"], 1)
                    ve.wait_ge(s["proj_done"], i + 1)
                    ve.wait_ge(s["xb_ready"], i + 1)
                    for half in range(2):
                        bb = slice(2 * half, 2 * half + 2)
                        last = ve.tensor_tensor(z[:, bb], ps[:, 2 + half, :].rearrange("p (b d) -> p b d", b=2), xb[:, bb], ALU.add)
                        if half == 0:
                            ch.mark(last)
                    last.then_inc(s["z_ready"], 1)
                    ve.wait_ge(s["z_ready"], i + 1)
                    ve.wait_ge(stored[k], 16 * jj)
                    layernorm(ch, z, out[:, k], stats, small, smalli, BATCH).then_inc(s["out_ready"], 1)
                    ch.end()


def phase_shared(nc, x3, sw, rw, rb, ident, xs, routed_w, wall, logits, wall_in):
    with ExitStack() as ctx:
        def sb(name, shape, dt=F32):
            return ctx.enter_context(nc.sbuf_tensor("d_" + name, shape, dt))

        def sem(name):
            return ctx.enter_context(nc.semaphore("d_" + name))

        raw = sb("raw", [P, 2, 1024])
        whl = sb("whl", [P, 2, SHARED, WCOLS], F32R)
        rws = sb("rw", [P, KD, EXPERTS])
        rbs = sb("rb", [P, EXPERTS])
        ids = sb("ident", [P, P])
        xr = sb("xr", [P, 2, BATCH, D])
        xtf = sb("xtf", [P, KD, TOK])
        xhl = sb("xhl", [P, 2, KD, TOK], F32R)
        act_h = sb("act_h", [P, 2, TOK])
        g = sb("g", [P, 2, TOK])
        ghl = sb("ghl", [P, 2, 2, TOK], F32R)
        z = sb("z", [P, 2, BATCH, D])
        ps = ctx.enter_context(nc.psum_tensor("d_ps", [P, 8, 512], F32))
        names = ("consts_in", "raw_hi", "raw_lo", "turned", "xtf_ready", "xhi_ready", "xlo_ready", "h_done", "silu_done",
                 "g_ready", "ghi_ready", "glo_ready", "g_used", "logits_done", "logits_read", "z_ready", "own")
        raw_in = [sem(f"raw_in{k}") for k in range(2)]
        s = {n: sem(n) for n in names}
        x_in = [sem(f"x_in{k}") for k in range(2)]
        stored = [sem(f"stored{k}") for k in range(2)]
        block = ctx.enter_context(nc.Block())
        NCH = SHARED * WCOLS // 1024
        NM = SHARED * HM
        T, H, O = 0, 2, 6
        swf = sw.rearrange("p e n -> p (e n)")
        whlf = whl[:].rearrange("p t e n -> p t (e n)")

        @block.sync
        def _(sp):
            for dst, src in ((rws[:], rw), (ids[:], ident), (rbs[:], rb.partition_broadcast(P))):
                sp.dma_start(dst, src).then_inc(s["consts_in"], 16)
            for n in range(NCH):
                if n >= 2:
                    sp.wait_ge(s["raw_lo"], n - 1)
                sp.dma_start(raw[:, n % 2], swf[:, n * 1024:(n + 1) * 1024]).then_inc(raw_in[n % 2], 16)
                if n < 2:
                    sp.dma_start(xr[:, n], x3[n]).then_inc(x_in[n], 16)
            for e in range(EXPERTS):
                sp.dma_start(wall[:, e], routed_w[:, e]).then_inc(wall_in, 16)
            with sp.Fori(1, STEPS // 2) as j:
                for k in range(2):
                    sp.wait_ge(s["turned"], 2 * j - 1 + k)
                    sp.wait_ge(s["z_ready"], 2 * j - 1 + k)
                    sp.dma_start(xr[:, k], x3[2 * j + k]).then_inc(x_in[k], 16)

        @block.gpsimd
        def _(gp):
            for n in range(NCH):
                gp.wait_ge(s["raw_hi"], n + 1)
                cols = slice(n * 1024, (n + 1) * 1024)
                gp.tensor_tensor(whlf[:, 1, cols], raw[:, n % 2], whlf[:, 0, cols].bitcast(F32), ALU.subtract).then_inc(s["raw_lo"], 1)
            with gp.Fori(0, STEPS // 2) as j:
                for k in range(2):
                    gp.wait_ge(s["z_ready"], 2 * j + k + 1)
                    gp.dma_start(xs[2 * j + k], z[:, k]).then_inc(stored[k], 16)
            for k in range(2):
                gp.wait_ge(stored[k], 16 * (STEPS // 2))

        @block.tensor
        def _(pe):
            pe.wait_ge(s["consts_in"], 48)
            pe.wait_ge(s["raw_lo"], NCH)
            with pe.Fori(0, STEPS // 2) as j:
                for k in range(2):
                    i = 2 * j + k
                    pe.wait_ge(x_in[k], 16 * (j + 1))
                    pe.wait_ge(s["xtf_ready"], i)
                    pe.wait_ge(s["logits_read"], i)
                    for kd in range(KD):
                        for b in range(BATCH):
                            mm = pe.transpose(ps[:, T + kd, b * P:(b + 1) * P], xr[:, k, b, kd * P:(kd + 1) * P], ids[:])
                    mm.then_inc(s["turned"], 1)

                    def down(n):
                        pe.wait_ge(s["ghi_ready"], NM * i + n + 1)
                        pe.wait_ge(s["glo_ready"], NM * i + n + 1)
                        for b in range(BATCH):
                            for q, (gp_, wp_) in enumerate(PARTS):
                                lo = W2AT + (n % HM) * D
                                mm = pe.matmul(ps[:, O + b // 2, (b % 2) * D:(b % 2 + 1) * D], ghl[:, n % 2, gp_, b * P:(b + 1) * P],
                                               whl[:, wp_, n // HM, lo:lo + D],
                                               start=n == 0 and q == 0 and b % 2 == 0, stop=n == NM - 1 and q == 2, skip_group_check=True)
                        mm.then_inc(s["g_used"], 1)

                    pe.wait_ge(s["xhi_ready"], i + 1)
                    pe.wait_ge(s["xlo_ready"], i + 1)
                    for n in range(NM):
                        e, m = n // HM, n % HM
                        pe.wait_ge(s["g_ready"], NM * i + max(n - 1, 0))
                        for w, at in enumerate((W1AT, W3AT)):
                            for q in range(3 * KD):
                                kd, (xp, wp) = q // 3, PARTS[q % 3]
                                lo = at + kd * HID + m * P
                                mm = pe.matmul(ps[:, H + 2 * (n % 2) + w, :], whl[:, wp, e, lo:lo + P], xhl[:, xp, kd, :],
                                               start=q == 0, stop=q == 3 * KD - 1)
                            mm.then_inc(s["h_done"], 1)
                        if n == 0:
                            pe.wait_ge(s["z_ready"], i)
                            pe.wait_ge(s["xtf_ready"], i + 1)
                            for b in range(BATCH):
                                for kd in range(KD):
                                    mm = pe.matmul(ps[:, T, b * EXPERTS:(b + 1) * EXPERTS], xtf[:, kd, b * P:(b + 1) * P], rws[:, kd, :],
                                                   start=kd == 0, stop=kd == KD - 1)
                            mm.then_inc(s["logits_done"], 1)
                        if n:
                            down(n - 1)
                    down(NM - 1)

        @block.scalar
        def _(act):
            for n in range(NCH):
                act.wait_ge(raw_in[n % 2], 16 * (n // 2 + 1))
                act.activation(whlf[:, 0, n * 1024:(n + 1) * 1024], raw[:, n % 2], ACT.Copy).then_inc(s["raw_hi"], 1)
            with act.Fori(0, STEPS // 2) as j:
                for k in range(2):
                    i = 2 * j + k
                    act.wait_ge(s["xtf_ready"], i + 1)
                    act.wait_ge(s["g_used"], NM * i)
                    act.activation(xhl[:, 0].rearrange("p k n -> p (k n)"), xtf[:].rearrange("p k n -> p (k n)"), ACT.Copy).then_inc(s["xhi_ready"], 1)
                    for n in range(NM):
                        act.wait_ge(s["h_done"], 2 * (NM * i + n) + 1)
                        act.wait_ge(s["g_ready"], NM * i + max(n - 1, 0))
                        act.activation(act_h[:, n % 2], ps[:, H + 2 * (n % 2), :], ACT.Silu).then_inc(s["silu_done"], 1)
                        act.wait_ge(s["g_ready"], NM * i + n + 1)
                        act.wait_ge(s["g_used"], NM * i + max(n - 1, 0))
                        act.activation(ghl[:, n % 2, 0], g[:, n % 2], ACT.Copy).then_inc(s["ghi_ready"], 1)

        @block.vector
        def _(ve):
            ch = Chain(ve, s["own"], 1)
            ve.wait_ge(s["consts_in"], 48)
            with ve.Fori(0, STEPS // 2) as j:
                for k in range(2):
                    i = 2 * j + k
                    ch.turn(i)
                    ve.wait_ge(s["turned"], i + 1)
                    ve.wait_ge(s["xhi_ready"], i)
                    ve.wait_ge(s["logits_done"], i)
                    ve.tensor_copy(xtf[:], ps[:, T:T + KD, :]).then_inc(s["xtf_ready"], 1)
                    ve.wait_ge(s["xhi_ready"], i + 1)
                    ve.wait_ge(s["xtf_ready"], i + 1)
                    ve.tensor_tensor(xhl[:, 1], xtf[:], xhl[:, 0].bitcast(F32), ALU.subtract).then_inc(s["xlo_ready"], 1)
                    for n in range(NM):
                        ve.wait_ge(s["silu_done"], NM * i + n + 1)
                        ve.wait_ge(s["h_done"], 2 * (NM * i + n) + 2)
                        ve.wait_ge(s["ghi_ready"], NM * i + max(n - 1, 0))
                        ve.tensor_tensor(g[:, n % 2], ps[:, H + 2 * (n % 2) + 1, :], act_h[:, n % 2], ALU.mult).then_inc(s["g_ready"], 1)
                        ve.wait_ge(s["ghi_ready"], NM * i + n + 1)
                        ve.tensor_tensor(ghl[:, n % 2, 1], g[:, n % 2], ghl[:, n % 2, 0].bitcast(F32), ALU.subtract).then_inc(s["glo_ready"], 1)
                        if n == 0:
                            ve.wait_ge(s["logits_done"], i + 1)
                            ve.tensor_tensor(logits[:, i], ps[:, T, 0:BATCH * EXPERTS].rearrange("p (b e) -> p b e", b=BATCH),
                                             rbs[:].unsqueeze(1).to_broadcast([P, BATCH, EXPERTS]), ALU.add).then_inc(s["logits_read"], 1)
                    ve.wait_ge(s["g_used"], NM * (i + 1))
                    ve.wait_ge(stored[k], 16 * j)
                    for half in range(2):
                        bb = slice(2 * half, 2 * half + 2)
                        last = ve.tensor_tensor(z[:, k, bb], ps[:, O + half, :].rearrange("p (b d) -> p b d", b=2), xr[:, k, bb], ALU.add)
                        if half == 0:
                            ch.mark(last)
                    last.then_inc(s["z_ready"], 1)
                    ch.end()


def phase_route(nc, logits, masks, zeros_done, x3, xg, pos, prob, tile_expert):
    E = EXPERTS
    with ExitStack() as ctx:
        def sb(name, shape, dt=F32):
            return ctx.enter_context(nc.sbuf_tensor("r_" + name, shape, dt))

        def sem(name):
            return ctx.enter_context(nc.semaphore("r_" + name))

        rows = sb("rows", [P, STEPS, BATCH, D])
        tri = sb("tri", [P, P])
        ones = sb("ones", [P, P])
        iota = sb("iota", [P, E])
        ioti = sb("ioti", [P, E], I32)
        gidx = sb("gidx", [P, GROUPS + 1])
        gidxi = sb("gidxi", [P, GROUPS + 1], I32)
        w = {n: sb(n, [P, TILES, E]) for n in ("lg", "cand", "oh0", "oh1", "incl", "tmp")}
        m = sb("m", [P, 2, TILES])
        idx = sb("idx", [P, TILES])
        ex = sb("ex", [P, TILES])
        tot = sb("tot", [P, E, TILES])
        cum = sb("cum", [P, E, TILES])
        cnt = sb("cnt", [P, 6, E])
        cnti = sb("cnti", [P, E], I32)
        te = sb("te", [P, GROUPS + 1, E])
        tf = sb("tf", [P, GROUPS + 1])
        posf = sb("posf", [P, TOPK, TILES])
        ps = ctx.enter_context(nc.psum_tensor("r_ps", [P, 2, 512], F32))
        names = ("in", "iota", "ex_ready", "diff_ready", "sel_ready", "sums_done", "pos_ready", "scattered", "own", "rows_in")
        s = {n: sem(n) for n in names}
        block = ctx.enter_context(nc.Block())
        lgv = logits[:].rearrange("p i b e -> p (i b) e")
        BIG = 3.0e38

        @block.sync
        def _(sp):
            sp.dma_start(tri[:], masks[0]).then_inc(s["in"], 16)
            sp.dma_start(ones[:], masks[2]).then_inc(s["in"], 16)
            for i in range(STEPS):
                sp.dma_start(rows[:, i], x3[i]).then_inc(s["rows_in"], 16)

        @block.gpsimd
        def _(gp):
            gp.iota(ioti[:], [[1, E]], channel_multiplier=0).then_inc(s["iota"], 1)
            gp.iota(gidxi[:], [[SLOT, GROUPS + 1]], channel_multiplier=0).then_inc(s["iota"], 1)
            gp.wait_ge(s["rows_in"], 16 * STEPS)
            gp.wait_ge(s["pos_ready"], 1)
            gp.wait_ge(zeros_done, 16 * ZERO_DMAS)
            for t in range(TILES):
                for k in range(TOPK):
                    gp.indirect_dma_start(xg, bass.IndirectOffsetOnAxis(ap=pos[:, k, t:t + 1], axis=0),
                                          rows[:, t // BATCH, t % BATCH, :], None).then_inc(s["scattered"], 16)
            gp.wait_ge(s["scattered"], 16 * TILES * TOPK)

        @block.tensor
        def _(pe):
            pe.wait_ge(s["in"], 32)
            pe.wait_ge(s["sel_ready"], 1)
            sel = w["tmp"][:].rearrange("p t e -> p (t e)")
            pe.matmul(ps[:, 0, 0:TILES * E], tri[:], sel, start=True, stop=True)
            pe.matmul(ps[:, 1, 0:TILES * E], ones[:], sel, start=True, stop=True).then_inc(s["sums_done"], 1)

        @block.scalar
        def _(act):
            act.wait_ge(s["diff_ready"], 1)
            act.activation(ex[:], idx[:], ACT.Exp).then_inc(s["ex_ready"], 1)

        @block.vector
        def _(ve):
            ch = Chain(ve, s["own"], 0)
            V = ve
            by_e = lambda ap: ap.unsqueeze(1).to_broadcast([P, TILES, E])
            by_t = lambda ap: ap.unsqueeze(2).to_broadcast([P, TILES, E])
            lg, cand, incl, tmp = (w[n][:] for n in ("lg", "cand", "incl", "tmp"))
            ohs = (w["oh0"][:], w["oh1"][:])
            ve.wait_ge(s["iota"], 2)
            ch.mark(V.tensor_copy(iota[:], ioti[:]))
            ch.mark(V.tensor_copy(gidx[:], gidxi[:]))
            ch.link(V.tensor_copy(lg, lgv))
            for k in range(TOPK):
                ch.link(V.tensor_reduce(m[:, k], lg, AX.X, ALU.max))
                ch.link(V.tensor_tensor(cand, lg, by_t(m[:, k]), ALU.is_lt))
                ch.link(V.scalar_tensor_tensor(cand, cand, float(E), by_e(iota[:]), ALU.mult, ALU.add))
                ch.link(V.tensor_reduce(idx[:], cand, AX.X, ALU.min))
                ch.link(V.tensor_tensor(ohs[k], by_e(iota[:]), by_t(idx[:]), ALU.is_equal))
                if k == 0:
                    ch.link(V.scalar_tensor_tensor(lg, ohs[0], -BIG, lg, ALU.mult, ALU.add))
            V.tensor_tensor(tmp, ohs[0], ohs[1], ALU.add).then_inc(s["sel_ready"], 1)
            V.tensor_tensor(idx[:], m[:, 1], m[:, 0], ALU.subtract).then_inc(s["diff_ready"], 1)
            ve.wait_ge(s["ex_ready"], 1)
            ch.link(V.tensor_scalar(posf[:, 0], ex[:], 1.0, None, ALU.add))
            ch.link(V.reciprocal(prob[:, 0], posf[:, 0]))
            ch.mark(V.tensor_tensor(prob[:, 1], prob[:, 0], ex[:], ALU.mult))
            ve.wait_ge(s["sums_done"], 1)
            ch.mark(V.tensor_copy(incl, ps[:, 0, 0:TILES * E].rearrange("p (t e) -> p t e", e=E)))
            ch.link(V.tensor_copy(tot[:], ps[:, 1, 0:TILES * E].rearrange("p (t e) -> p e t", e=E)))
            totf, cumf = tot[:].rearrange("p e t -> p (e t)"), cum[:].rearrange("p e t -> p (e t)")
            ch.link(V.tensor_tensor_scan(cumf, totf, totf, 0.0, ALU.add, ALU.max))
            last = cum[:, :, TILES - 1]
            ch.mark(V.tensor_copy(cnt[:, 0, 0:1], last[:, 0:1]))
            ch.link(V.tensor_tensor(cnt[:, 0, 1:E], last[:, 1:E], last[:, 0:E - 1], ALU.subtract))
            ch.link(V.tensor_scalar(cnti[:], cnt[:, 0], float(SLOT - 1), None, ALU.add))
            ch.link(V.tensor_scalar(cnti[:], cnti[:], SLOT.bit_length() - 1, SLOT.bit_length() - 1, ALU.logical_shift_right, ALU.logical_shift_left))
            ch.link(V.tensor_copy(cnt[:, 1], cnti[:]))
            ch.link(V.tensor_tensor_scan(cnt[:, 2], cnt[:, 1], cnt[:, 1], 0.0, ALU.add, ALU.max))
            ch.link(V.tensor_tensor(cnt[:, 3], cnt[:, 2], cnt[:, 1], ALU.subtract))
            ch.mark(V.tensor_tensor(cnt[:, 4], last, cnt[:, 0], ALU.subtract))
            ch.link(V.tensor_tensor(te[:], gidx[:].unsqueeze(2).to_broadcast([P, GROUPS + 1, E]),
                                    cnt[:, 2].unsqueeze(1).to_broadcast([P, GROUPS + 1, E]), ALU.is_ge))
            ch.link(V.tensor_tensor(cnt[:, 4], cnt[:, 3], cnt[:, 4], ALU.subtract))
            ch.link(V.tensor_reduce(tf[:], te[:], AX.X, ALU.add))
            ch.mark(V.tensor_scalar(tile_expert[:], tf[:], float(E - 1), None, ALU.min))
            ch.link(V.tensor_tensor(cum[:], cum[:], tot[:], ALU.subtract))
            ch.link(V.tensor_tensor(incl, incl, cum[:].rearrange("p e t -> p t e"), ALU.add))
            ch.link(V.tensor_tensor(incl, incl, by_e(cnt[:, 4]), ALU.add))
            for k in range(TOPK):
                ch.link(V.tensor_tensor(cand, incl, ohs[k], ALU.mult))
                ch.link(V.tensor_reduce(posf[:, k], cand, AX.X, ALU.add))
            V.tensor_scalar(pos[:], posf[:], -1.0, None, ALU.add).then_inc(s["pos_ready"], 1)



def phase_experts(nc, wall, wall_in, tile_expert, ident, xg, yg):
    SB = SLOT // P
    with ExitStack() as ctx:
        def sb(name, shape, dt=F32):
            return ctx.enter_context(nc.sbuf_tensor("e_" + name, shape, dt))

        def sem(name):
            return ctx.enter_context(nc.semaphore("e_" + name))

        whl = sb("whl", [P, 2, 2, WCOLS], F32R)
        ids = sb("ident", [P, P])
        xr = sb("xr", [P, 2, SB, D])
        xhl = sb("xhl", [P, 2, 2, KD, SLOT], F32R)
        act_h = sb("act_h", [P, 2, SLOT])
        g = sb("g", [P, 2, SLOT])
        ghl = sb("ghl", [P, 2, 2, SLOT], F32R)
        y = sb("y", [P, 2, SB, D])
        ps = ctx.enter_context(nc.psum_tensor("e_ps", [P, 8, 512], F32))
        names = ("consts_in", "turned", "whi_ready", "wlo_ready", "xhi_ready", "xlo_ready", "h_done", "silu_done", "g_ready",
                 "ghi_ready", "glo_ready", "g_used", "y_ready")
        s = {n: sem(n) for n in names}
        x_in = [sem(f"x_in{k}") for k in range(2)]
        stored = [sem(f"stored{k}") for k in range(2)]
        block = ctx.enter_context(nc.Block())
        xgv = xg.rearrange("(n b p) d -> n p b d", p=P, b=SB)
        ygv = yg.rearrange("(n b p) d -> n p b d", p=P, b=SB)
        PAIR = GROUPS // 2
        NQ = 4
        QC = WCOLS // NQ
        T, H, O = 0, 2, 6

        @block.sync
        def _(sp):
            sp.dma_start(ids[:], ident).then_inc(s["consts_in"], 16)
            for k in range(2):
                sp.dma_start(xr[:, k], xgv[k]).then_inc(x_in[k], 16)
            with sp.Fori(0, PAIR - 1) as j:
                for k in range(2):
                    sp.wait_ge(s["y_ready"], 2 * j + k + 1)
                    sp.dma_start(ygv[2 * j + k], y[:, k]).then_inc(stored[k], 16)
                    sp.dma_start(xr[:, k], xgv[2 * j + k + 2]).then_inc(x_in[k], 16)
            for k in range(2):
                sp.wait_ge(s["y_ready"], GROUPS - 1 + k)
                sp.dma_start(ygv[GROUPS - 2 + k], y[:, k]).then_inc(stored[k], 16)
            for k in range(2):
                sp.wait_ge(stored[k], 16 * PAIR)

        @block.gpsimd
        def _(gp):
            gp.wait_ge(wall_in, 16 * EXPERTS)
            with gp.Fori(0, PAIR) as j:
                for k in range(2):
                    i = 2 * j + k
                    e = gp.value_load(tile_expert[0:1, bass.ds(i, 1)], min_val=0, max_val=EXPERTS - 1)
                    for q in range(NQ):
                        cols = slice(q * QC, (q + 1) * QC)
                        gp.wait_ge(s["whi_ready"], NQ * i + q + 1)
                        gp.tensor_tensor(whl[:, k, 1, cols], wall[:, e, cols], whl[:, k, 0, cols].bitcast(F32), ALU.subtract).then_inc(s["wlo_ready"], 1)

        @block.scalar
        def _(act):
            act.wait_ge(wall_in, 16 * EXPERTS)

            def expert_of(i):
                return act.value_load(tile_expert[0:1, bass.ds(i, 1)], min_val=0, max_val=EXPERTS - 1)

            def split_weights(e, k, q):
                cols = slice(q * QC, (q + 1) * QC)
                act.activation(whl[:, k, 0, cols], wall[:, e, cols], ACT.Copy).then_inc(s["whi_ready"], 1)

            first = expert_of(0)
            for q in range(NQ):
                split_weights(first, 0, q)
            with act.Fori(0, PAIR) as j:
                for k in range(2):
                    i = 2 * j + k
                    e_next = expert_of(i + 1)
                    act.wait_ge(s["turned"], i + 1)
                    act.activation(xhl[:, k, 0], ps[:, k, :].rearrange("p (k n) -> p k n", k=KD), ACT.Copy).then_inc(s["xhi_ready"], 1)
                    for m in range(HM):
                        n = HM * i + m
                        act.wait_ge(s["h_done"], n + 1)
                        act.wait_ge(s["g_ready"], HM * i + max(m - 1, 0))
                        act.activation(act_h[:, m % 2], ps[:, H + m % 2, 0:SLOT], ACT.Silu).then_inc(s["silu_done"], 1)
                        act.wait_ge(s["g_ready"], n + 1)
                        act.wait_ge(s["g_used"], HM * i + max(m - 1, 0))
                        act.activation(ghl[:, m % 2, 0], g[:, m % 2], ACT.Copy).then_inc(s["ghi_ready"], 1)
                        act.wait_ge(s["g_used"], HM * i)
                        split_weights(e_next, 1 - k, m)

        @block.tensor
        def _(pe):
            pe.wait_ge(s["consts_in"], 16)
            with pe.Fori(0, PAIR) as j:
                for k in range(2):
                    i = 2 * j + k
                    pe.wait_ge(x_in[k], 16 * (j + 1))
                    pe.wait_ge(s["xlo_ready"], i)
                    for kd in range(KD):
                        for b in range(SB):
                            mm = pe.transpose(ps[:, k, kd * SLOT + b * P:kd * SLOT + (b + 1) * P], xr[:, k, b, kd * P:(kd + 1) * P], ids[:])
                    mm.then_inc(s["turned"], 1)
                    pe.wait_ge(s["xhi_ready"], i + 1)
                    pe.wait_ge(s["xlo_ready"], i + 1)
                    pe.wait_ge(s["wlo_ready"], NQ * (i + 1))

                    def down(m):
                        pe.wait_ge(s["ghi_ready"], HM * i + m + 1)
                        pe.wait_ge(s["glo_ready"], HM * i + m + 1)
                        for b in range(SB):
                            for q, (gp_, wp_) in enumerate(PARTS):
                                lo = W2AT + m * D
                                mm = pe.matmul(ps[:, O + k, b * D:(b + 1) * D], ghl[:, m % 2, gp_, b * P:(b + 1) * P], whl[:, k, wp_, lo:lo + D],
                                               start=m == 0 and q == 0 and b == 0, stop=m == HM - 1 and q == 2, skip_group_check=True)
                        mm.then_inc(s["g_used"], 1)
                        return mm

                    for m in range(HM):
                        pe.wait_ge(s["g_ready"], HM * i + max(m - 1, 0))
                        for w, at in enumerate((W1AT, W3AT)):
                            for q in range(3 * KD):
                                kd, (xp, wp) = q // 3, PARTS[q % 3]
                                lo = at + kd * HID + m * P
                                mm = pe.matmul(ps[:, H + m % 2, w * SLOT:(w + 1) * SLOT], whl[:, k, wp, lo:lo + P], xhl[:, k, xp, kd, :],
                                               start=q == 0, stop=q == 3 * KD - 1)
                        mm.then_inc(s["h_done"], 1)
                        if m == 0:
                            pe.wait_ge(s["y_ready"], 2 * j)
                        if m:
                            down(m - 1)
                    down(HM - 1)

        @block.vector
        def _(ve):
            with ve.Fori(0, PAIR) as j:
                for k in range(2):
                    i = 2 * j + k
                    ve.wait_ge(s["xhi_ready"], i + 1)
                    ve.tensor_tensor(xhl[:, k, 1], ps[:, k, :].rearrange("p (k n) -> p k n", k=KD), xhl[:, k, 0].bitcast(F32), ALU.subtract).then_inc(s["xlo_ready"], 1)
                    for m in range(HM):
                        n = HM * i + m
                        ve.wait_ge(s["silu_done"], n + 1)
                        ve.wait_ge(s["ghi_ready"], HM * i + max(m - 1, 0))
                        ve.tensor_tensor(g[:, m % 2], ps[:, H + m % 2, SLOT:2 * SLOT], act_h[:, m % 2], ALU.mult).then_inc(s["g_ready"], 1)
                        ve.wait_ge(s["ghi_ready"], n + 1)
                        ve.tensor_tensor(ghl[:, m % 2, 1], g[:, m % 2], ghl[:, m % 2, 0].bitcast(F32), ALU.subtract).then_inc(s["glo_ready"], 1)
                    ve.wait_ge(s["g_used"], HM * (i + 1))
                    ve.wait_ge(stored[k], 16 * j)
                    ve.tensor_copy(y[:, k].rearrange("p b d -> p (b d)"), ps[:, O + k, :]).then_inc(s["y_ready"], 1)


def phase_combine(nc, xs, yg, pos, prob, out):
    with ExitStack() as ctx:
        def sb(name, shape, dt=F32):
            return ctx.enter_context(nc.sbuf_tensor("f_" + name, shape, dt))

        def sem(name):
            return ctx.enter_context(nc.semaphore("f_" + name))

        xr = sb("xr", [P, 2, BATCH, D])
        y = sb("y", [P, 2, TOPK, BATCH, D])
        z = sb("z", [P, BATCH, D])
        o = sb("o", [P, 2, BATCH, D])
        stats = sb("stats", [P, BATCH, 6])
        small = sb("small", [P, 5, BATCH])
        smalli = sb("smalli", [P, BATCH], I32)
        used = sem("used")
        own = sem("own")
        out_ready = sem("out_ready")
        x_in = [sem(f"x_in{k}") for k in range(2)]
        y_in = [sem(f"y_in{k}") for k in range(2)]
        stored = [sem(f"stored{k}") for k in range(2)]
        block = ctx.enter_context(nc.Block())

        @block.sync
        def _(sp):
            with sp.Fori(0, STEPS // 2) as j:
                for k in range(2):
                    sp.wait_ge(used, 2 * j)
                    sp.dma_start(xr[:, k], xs[2 * j + k]).then_inc(x_in[k], 16)

        @block.gpsimd
        def _(gp):
            for i in range(STEPS):
                if i >= 2:
                    gp.wait_ge(used, i - 1)
                for b in range(BATCH):
                    for k in range(TOPK):
                        t = i * BATCH + b
                        gp.indirect_dma_start(y[:, i % 2, k, b, :], None, yg,
                                              bass.IndirectOffsetOnAxis(ap=pos[:, k, t:t + 1], axis=0)).then_inc(y_in[i % 2], 16)

        @block.scalar
        def _(act):
            with act.Fori(0, STEPS // 2) as j:
                for k in range(2):
                    act.wait_ge(out_ready, 2 * j + k + 1)
                    act.dma_start(out[2 * j + k], o[:, k]).then_inc(stored[k], 16)
            for k in range(2):
                act.wait_ge(stored[k], 16 * (STEPS // 2))

        @block.vector
        def _(ve):
            ch = Chain(ve, own, 2 * BATCH - 1 + LN_LINKS)
            with ve.Fori(0, STEPS // 2) as j:
                for k in range(2):
                    i = 2 * j + k
                    ch.turn(i)
                    ve.wait_ge(x_in[k], 16 * (j + 1))
                    ve.wait_ge(y_in[k], 16 * BATCH * TOPK * (j + 1))
                    ve.wait_ge(out_ready, i)
                    for b in range(BATCH):
                        ch.mark(ve.scalar_tensor_tensor(z[:, b], y[:, k, 0, b], prob[:, 0, bass.ds(i * BATCH + b, 1)], xr[:, k, b], ALU.mult, ALU.add))
                    ch.wait()
                    for b in range(BATCH):
                        last = ve.scalar_tensor_tensor(z[:, b], y[:, k, 1, b], prob[:, 1, bass.ds(i * BATCH + b, 1)], z[:, b], ALU.mult, ALU.add)
                        if b < BATCH - 1:
                            ch.mark(last)
                    last.then_inc(used, 1)
                    ve.wait_ge(used, i + 1)
                    ve.wait_ge(stored[k], 16 * j)
                    layernorm(ch, z, o[:, k], stats, small, smalli, BATCH).then_inc(out_ready, 1)
                    ch.end()


def build_program(nc, A, out):
    def views(ap):
        return ap.rearrange("(b c p) d -> c p b d", b=BATCH, p=P)

    x1, x2, x3, xs = (nc.dram_tensor(n, [TILES * P, D], F32, kind="Internal").ap() for n in ("x1", "x2", "x3", "xs"))
    xg, yg = (nc.dram_tensor(n, [SLOTS, D], F32, kind="Internal").ap() for n in ("xg", "yg"))
    flat = lambda ap: ap.rearrange("b t d -> (b t) d")
    with ExitStack() as ctx:
        def sb(name, shape, dt=F32, ctx=ctx):
            return ctx.enter_context(nc.sbuf_tensor(name, shape, dt))

        wall_in = ctx.enter_context(nc.semaphore("wall_in"))
        zeros_done = ctx.enter_context(nc.semaphore("zeros_done"))
        pos = sb("pos", [P, TOPK, TILES], I32)
        prob = sb("prob", [P, TOPK, TILES])
        tile_expert = sb("tile_expert", [P, GROUPS + 1], I32)
        phase_ssd(nc, views(flat(A["x"])), A["x_t"], A["w_xproj"], A["dt_bias"], A["a_log"], A["d_skip"], A["masks"], views(x1))
        phase_ffn(nc, views(x1), A["w1"], A["b1"], A["w2"], A["b2"], A["ident"], views(x2), xg, zeros_done)
        phase_attention(nc, views(x2), A["wqkv"], A["bqkv"], A["wout"], A["bout"], A["omega"], A["nodes"], A["weights"],
                        A["masks"], A["ident"], views(x3))
        with ExitStack() as inner:
            wall = sb("wall", [P, EXPERTS, WCOLS], ctx=inner)
            logits = sb("logits", [P, STEPS, BATCH, EXPERTS], ctx=inner)
            phase_shared(nc, views(x3), A["shared_w"], A["router_w"], A["router_b"], A["ident"], views(xs), A["expert_w"], wall, logits, wall_in)
            phase_route(nc, logits, A["masks"], zeros_done, views(x3), xg, pos, prob, tile_expert)
            phase_experts(nc, wall, wall_in, tile_expert, A["ident"], xg, yg)
        phase_combine(nc, views(xs), yg, pos, prob, views(flat(out)))


def kernel(L0_attn_x, L0_attn_W_xproj, L0_attn_dt_bias, L0_attn_A_log, L0_attn_D, L0_ffn_w1, L0_ffn_b1, L0_ffn_w2, L0_ffn_b2,
           L1_attn_Wqkv, L1_attn_bqkv, L1_attn_Wout, L1_attn_bout, L1_attn_omega, L1_attn_quad_nodes, L1_attn_quad_weights,
           L1_ffn_router_w, L1_ffn_expert_bias, L1_ffn_w1, L1_ffn_w3, L1_ffn_w2, L1_ffn_sw1, L1_ffn_sw3, L1_ffn_sw2):
    import concourse.bacc as bacc
    from concourse.bass_utils import run_bass_kernel_spmd

    def rows_first(w):
        return w.reshape(-1, P, w.shape[-1]).transpose(1, 0, 2)

    def expert_weights(w1, w3, w2):
        def part(w):
            n = w.shape[0]
            return w.transpose(0, 2, 1).reshape(n, w.shape[2] // P, P, w.shape[1]).transpose(2, 0, 1, 3).reshape(P, n, -1)
        return np.concatenate([part(w1), part(w3), part(w2)], -1)

    x = np.asarray(L0_attn_x)
    k = np.arange(P)
    omega_in = np.asarray(L1_attn_omega)
    omega = np.zeros((P, KD, P), omega_in.dtype)
    per = P // HD
    for h in range(HEADS1):
        r0, c0 = HD * (h % per), FD * (h % 2)
        omega[r0:r0 + HD, h // per, c0:c0 + FD] = omega_in[:, h].transpose(1, 0, 2).reshape(HD, FD)

    def per_feature(v):
        return np.tile(np.repeat(np.asarray(v), MF), 2).reshape(P, 1)

    arrays = {
        "x": x,
        "x_t": x.reshape(BATCH, STEPS, P, KD, P).transpose(1, 4, 3, 0, 2).reshape(STEPS, P, KD, TOK),
        "w_xproj": rows_first(np.asarray(L0_attn_W_xproj).T),
        "dt_bias": L0_attn_dt_bias, "a_log": L0_attn_A_log, "d_skip": L0_attn_D,
        "masks": np.stack([k[:, None] <= k[None, :], k[:, None] > k[None, :], np.ones((P, P), bool)]).astype(np.float32),
        "ident": np.eye(P, dtype=np.float32),
        "w1": rows_first(np.asarray(L0_ffn_w1)), "b1": np.asarray(L0_ffn_b1).reshape(-1, P).T,
        "w2": rows_first(np.asarray(L0_ffn_w2)), "b2": L0_ffn_b2,
        "wqkv": rows_first(np.asarray(L1_attn_Wqkv)), "bqkv": L1_attn_bqkv,
        "wout": rows_first(np.asarray(L1_attn_Wout)), "bout": L1_attn_bout,
        "omega": omega, "nodes": per_feature(L1_attn_quad_nodes), "weights": per_feature(L1_attn_quad_weights),
        "router_w": rows_first(np.asarray(L1_ffn_router_w).T), "router_b": L1_ffn_expert_bias,
        "shared_w": expert_weights(*map(np.asarray, (L1_ffn_sw1, L1_ffn_sw3, L1_ffn_sw2))),
        "expert_w": expert_weights(*map(np.asarray, (L1_ffn_w1, L1_ffn_w3, L1_ffn_w2))),
    }
    arrays = {"in_" + n: np.ascontiguousarray(a) for n, a in arrays.items()}
    nc = bacc.Bacc("TRN2", target_bir_lowering=False, num_devices=1)
    aps = {n[3:]: nc.dram_tensor(n, a.shape, mybir.dt.from_np(a.dtype), kind="ExternalInput").ap() for n, a in arrays.items()}
    out = nc.dram_tensor("out", x.shape, F32, kind="ExternalOutput").ap()
    build_program(nc, aps, out)
    return run_bass_kernel_spmd(nc, [arrays], core_ids=[0]).results[0]["out"]
```

```python
from contextlib import ExitStack

import numpy as np
import concourse.bass as bass
from concourse import mybir

F32 = mybir.dt.float32
I32 = mybir.dt.int32
ALU = mybir.AluOpType
ACT = mybir.ActivationFunctionType
AX = mybir.AxisListType

P = 128
BATCH, SEQ, D = 4, 1024, 256
KD = D // P
CHUNK = 128
STEPS = SEQ // CHUNK
TOK = BATCH * CHUNK
HEADS0, HEADDIM0, STATE0 = 2, 128, 64
EPS = 1e-5
HEADS1, HD, MF, RF = 16, 16, 32, 2
FD = MF * RF
PAIRS = HEADS1 // 2
VP = 32
EXPERTS, SHARED, TOPK, HID = 8, 2, 2, 512
HM = HID // P
F32R = mybir.dt.float32r
WCOLS = 2 * KD * HID + HM * D
W1AT, W3AT, W2AT = 0, KD * HID, 2 * KD * HID
TILES = STEPS * BATCH
SLOT = 256
GROUPS = (TILES * P * TOPK - EXPERTS) // SLOT + EXPERTS
GROUPS += GROUPS % 2
SLOTS = GROUPS * SLOT
PARTS = ((0, 0), (0, 1), (1, 0))
ZERO_DMAS = 5
ZERO_COLS = SLOTS * D // (ZERO_DMAS * P)


class Chain:

    def __init__(self, eng, sem, per_turn):
        self.eng, self.sem, self.per_turn, self.base, self.n = eng, sem, per_turn, 0, 0

    def turn(self, i):
        self.base, self.n = i * self.per_turn, 0

    def end(self):
        assert self.n == self.per_turn, (self.n, self.per_turn)

    def mark(self, ins):
        ins.then_inc(self.sem, 1)
        self.n += 1

    def wait(self):
        self.eng.wait_ge(self.sem, self.base + self.n)

    def link(self, ins):
        self.mark(ins)
        self.wait()


def rsqrt(chain, v, r, t, ti, ready=None):
    ve = chain.eng
    chain.link(ve.tensor_scalar(ti, v.bitcast(I32), 1, None, ALU.logical_shift_right))
    chain.link(ve.tensor_scalar(r.bitcast(I32), ti, -1.0, float(0x5F3759DF), ALU.mult, ALU.add))
    for n in range(3):
        chain.link(ve.tensor_tensor(t, r, r, ALU.mult))
        chain.link(ve.tensor_tensor(t, t, v, ALU.mult))
        chain.link(ve.tensor_scalar(t, t, -0.5, 1.5, ALU.mult, ALU.add))
        ins = ve.tensor_tensor(r, r, t, ALU.mult)
        if n == 2 and ready is not None:
            ins.then_inc(ready, 1)
        else:
            chain.link(ins)


RSQRT_LINKS = 14


def layernorm(chain, z, out, stats, small, smalli, n):
    ve = chain.eng
    for b in range(n):
        chain.mark(ve.bn_stats(stats[:, b, :], z[:, b, :]))
    chain.wait()
    mean, half, v, r, t = (small[:, k, 0:n] for k in range(5))
    chain.mark(ve.tensor_tensor(mean, stats[:, 0:n, 1], stats[:, 0:n, 4], ALU.add))
    chain.mark(ve.tensor_tensor(half, stats[:, 0:n, 1], stats[:, 0:n, 4], ALU.subtract))
    chain.link(ve.tensor_tensor(v, stats[:, 0:n, 2], stats[:, 0:n, 5], ALU.add))
    chain.mark(ve.tensor_scalar(mean, mean, 0.5, None, ALU.mult))
    chain.mark(ve.tensor_tensor(half, half, half, ALU.mult))
    chain.link(ve.tensor_scalar(v, v, 1.0 / D, EPS, ALU.mult, ALU.add))
    chain.link(ve.scalar_tensor_tensor(v, half, 0.25, v, ALU.mult, ALU.add))
    rsqrt(chain, v, r, t, smalli[:, 0:n])
    last = None
    for b in range(n):
        last = ve.tensor_scalar(out[:, b, :], z[:, b, :], mean[:, b:b + 1], r[:, b:b + 1], ALU.subtract, ALU.mult)
    return last


LN_LINKS = 4 + 3 + 3 + 1 + RSQRT_LINKS


def phase_ssd(nc, x, xt, w, dtb, alog, dskip, masks, x1):
    NB = BATCH * HEADS0
    RW = HEADS0 + STATE0
    with ExitStack() as outer:
        def sb(name, shape, dt=F32, ctx=outer):
            return ctx.enter_context(nc.sbuf_tensor("a_" + name, shape, dt))

        def sem(name, ctx=outer):
            return ctx.enter_context(nc.semaphore("a_" + name))

        bt_all = sb("bt_all", [STATE0, STEPS, TOK])
        ct_all = sb("ct_all", [STATE0, STEPS, TOK])
        rows = sb("rows", [P, STEPS, BATCH, RW])
        tri = sb("tri", [P, P])
        strict = sb("strict", [P, P])
        ones = sb("ones", [P, P])
        dt = sb("dt", [P, STEPS, NB])
        a = sb("a", [P, STEPS, NB])
        dec = sb("dec", [P, 3, STEPS, NB])
        dx = sb("dx", [P, STEPS, NB])
        dcoef = sb("dcoef", [P, D])

        with ExitStack() as ctx:
            wsb = sb("w", [P, KD, 2 * STATE0 + HEADS0], ctx=ctx)
            xts = sb("xts", [P, 2, KD, TOK], ctx=ctx)
            dtb_sb = sb("dtb", [P, NB], ctx=ctx)
            nega = sb("nega", [P, NB], ctx=ctx)
            neg = sb("neg", [P, NB], ctx=ctx)
            dsk = sb("dsk", [P, HEADS0], ctx=ctx)
            z = sb("z", [P, STEPS, NB], ctx=ctx)
            e = sb("e", [P, STEPS, NB], ctx=ctx)
            l1 = sb("l1", [P, STEPS, NB], ctx=ctx)
            q = sb("q", [P, STEPS, NB], ctx=ctx)
            ps = ctx.enter_context(nc.psum_tensor("a_ps", [P, 8, 512], F32))
            consts_in = sem("consts_in", ctx)
            xt_in = [sem(f"xt_in{k}", ctx) for k in range(2)]
            proj = sem("proj", ctx)
            bc_out = sem("bc_out", ctx)
            rows_out = sem("rows_out", ctx)
            dve_own = sem("dve_own0", ctx)
            nega_done = sem("nega_done", ctx)
            na_ready = sem("na_ready", ctx)
            act_own = sem("act_own0", ctx)
            log_ready = sem("log_ready", ctx)
            a_ready = sem("a_ready", ctx)
            cum_ready = sem("cum_ready", ctx)
            dec_ready = sem("dec_ready", ctx)
            block = ctx.enter_context(nc.Block())
            W2 = HEADS0

            @block.sync
            def _(sp):
                sp.dma_start(wsb[:], w).then_inc(consts_in, 16)
                sp.dma_start(tri[:], masks[0]).then_inc(consts_in, 16)
                sp.dma_start(strict[:], masks[1]).then_inc(consts_in, 16)
                sp.dma_start(ones[:], masks[2]).then_inc(consts_in, 16)
                for b in range(BATCH):
                    sp.dma_start(dtb_sb[:, b * HEADS0:(b + 1) * HEADS0], dtb.partition_broadcast(P)).then_inc(consts_in, 16)
                    sp.dma_start(nega[:, b * HEADS0:(b + 1) * HEADS0], alog.partition_broadcast(P)).then_inc(consts_in, 16)
                sp.dma_start(dsk[:], dskip.partition_broadcast(P)).then_inc(consts_in, 16)
                with sp.Fori(0, STEPS // 2) as j:
                    for k in range(2):
                        sp.wait_ge(proj, 2 * j)
                        sp.dma_start(xts[:, k], xt[2 * j + k]).then_inc(xt_in[k], 16)

            CONSTS = 16 * (5 + 2 * BATCH)

            @block.tensor
            def _(pe):
                pe.wait_ge(consts_in, CONSTS)
                with pe.Fori(0, STEPS // 2) as j:
                    for k in range(2):
                        pe.wait_ge(xt_in[k], 16 * (j + 1))
                        pe.wait_ge(bc_out, 2 * (2 * j))
                        pe.wait_ge(rows_out, 2 * j)
                        for part in range(2):
                            lo = W2 + part * STATE0
                            for kd in range(KD):
                                pe.matmul(ps[0:STATE0, 4 * k + part, :], wsb[:, kd, lo:lo + STATE0], xts[:, k, kd, :],
                                          start=kd == 0, stop=kd == KD - 1)
                        for b in range(BATCH):
                            for kd in range(KD):
                                mm = pe.matmul(ps[:, 4 * k + 2, b * RW:(b + 1) * RW], xts[:, k, kd, b * P:(b + 1) * P],
                                               wsb[:, kd, 0:RW], start=kd == 0, stop=kd == KD - 1)
                        mm.then_inc(proj, 1)
                pe.wait_ge(a_ready, 1)
                af = a[:].rearrange("p c n -> p (c n)")
                for n, mask in enumerate((tri, strict, ones)):
                    mm = pe.matmul(ps[:, n, 0:STEPS * NB], mask[:], af, start=True, stop=True)
                mm.then_inc(cum_ready, 1)

            @block.scalar
            def _(act):
                act.wait_ge(consts_in, CONSTS)
                nc.scalar.activation(neg[:], nega[:], ACT.Exp).then_inc(nega_done, 1)
                with act.Fori(0, STEPS // 2) as j:
                    for k in range(2):
                        act.wait_ge(proj, 2 * j + k + 1)
                        act.activation(bt_all[:, 2 * j + k, :], ps[0:STATE0, 4 * k, :], ACT.Copy).then_inc(bc_out, 1)
                        act.activation(ct_all[:, 2 * j + k, :], ps[0:STATE0, 4 * k + 1, :], ACT.Copy).then_inc(bc_out, 1)
                act.wait_ge(na_ready, 1)
                act.activation(e[:], l1[:], ACT.Exp).then_inc(act_own, 1)
                act.wait_ge(act_own, 1)
                act.activation(q[:], e[:], ACT.Ln, bias=1.0).then_inc(log_ready, 1)
                act.wait_ge(cum_ready, 1)
                for n in range(3):
                    act.activation(dec[:, n].rearrange("p c n -> p (c n)"), ps[:, n, 0:STEPS * NB], ACT.Exp).then_inc(dec_ready, 1)

            @block.vector
            def _(ve):
                ch = Chain(ve, dve_own, 100)
                ve.wait_ge(consts_in, CONSTS)
                for h in range(HEADS0):
                    ch.mark(ve.tensor_scalar(dcoef[:, h * P:(h + 1) * P], ones[:], dsk[:, h:h + 1], None, ALU.add))
                with ve.Fori(0, STEPS // 2) as j:
                    for k in range(2):
                        ve.wait_ge(proj, 2 * j + k + 1)
                        ve.tensor_copy(rows[:, 2 * j + k].rearrange("p b w -> p (b w)"), ps[:, 4 * k + 2, 0:BATCH * RW]).then_inc(rows_out, 1)
                ve.wait_ge(rows_out, STEPS)
                bias = dtb_sb[:].rearrange("p (b h) -> p b h", b=BATCH)
                for c in range(STEPS):
                    ch.mark(ve.tensor_tensor(z[:, c].rearrange("p (b h) -> p b h", b=BATCH), rows[:, c, :, 0:HEADS0], bias, ALU.add))
                ch.wait()
                ve.scalar_tensor_tensor(l1[:], z[:], -1.0, z[:], ALU.mult, ALU.min).then_inc(na_ready, 1)
                ve.wait_ge(log_ready, 1)
                ch.link(ve.tensor_scalar(l1[:], e[:], 0.2, -0.25, ALU.mult, ALU.add))
                for cst in (1.0 / 3.0, -0.5, 1.0):
                    ch.link(ve.tensor_tensor(l1[:], l1[:], e[:], ALU.mult))
                    ch.link(ve.tensor_scalar(l1[:], l1[:], cst, None, ALU.add))
                ch.link(ve.tensor_tensor(l1[:], l1[:], e[:], ALU.mult))
                ch.link(ve.tensor_tensor(l1[:], l1[:], q[:], ALU.subtract))
                ch.link(ve.tensor_scalar(e[:], e[:], 1.0 / 32.0, None, ALU.is_lt))
                ch.link(ve.tensor_tensor(l1[:], l1[:], e[:], ALU.mult))
                ch.link(ve.tensor_tensor(q[:], q[:], l1[:], ALU.add))
                ch.link(ve.scalar_tensor_tensor(dt[:], z[:], 0.0, q[:], ALU.max, ALU.add))
                ve.wait_ge(nega_done, 1)
                ch.link(ve.tensor_scalar(neg[:], neg[:], -1.0, None, ALU.mult))
                for c in range(STEPS):
                    ins = ve.tensor_tensor(a[:, c], dt[:, c], neg[:], ALU.mult)
                    if c < STEPS - 1:
                        ch.mark(ins)
                ins.then_inc(a_ready, 1)
                ve.wait_ge(dec_ready, 3)
                ch.link(ve.tensor_tensor(dx[:], dt[:], dec[:, 1], ALU.mult))

        with ExitStack() as ctx:
            xr = sb("xr", [P, 2, BATCH, D], ctx=ctx)
            bs = sb("bs", [P, 2, BATCH, STATE0], ctx=ctx)
            btc = sb("btc", [STATE0, 2, 2, TOK], ctx=ctx)
            seg = sb("seg", [P, 2, BATCH // 2, HEADS0, P], ctx=ctx)
            lm = sb("lm", [P, 2, BATCH // 2, HEADS0, P], ctx=ctx)
            gm = sb("gm", [P, BATCH, P], ctx=ctx)
            mt = sb("mt", [P, BATCH, HEADS0, P], ctx=ctx)
            xdt = sb("xdt", [P, BATCH, D], ctx=ctx)
            xdd = sb("xdd", [P, BATCH, D], ctx=ctx)
            zz = sb("zz", [P, 2, BATCH, D], ctx=ctx)
            z2 = sb("z2", [P, BATCH, D], ctx=ctx)
            st = sb("st", [STATE0, BATCH, D], ctx=ctx)
            out = sb("out", [P, 2, BATCH, D], ctx=ctx)
            stats = sb("stats", [P, BATCH, 6], ctx=ctx)
            small = sb("small", [P, 5, BATCH], ctx=ctx)
            smalli = sb("smalli", [P, BATCH], I32, ctx=ctx)
            ps = ctx.enter_context(nc.psum_tensor("a_ps2", [P, 8, 512], F32))
            G, SEG, YD, YO, ST = 0, 1, 3, 5, 5
            names = ("seg_ready", "seg_done", "l_ready", "g_done", "m_ready", "yd_done", "yo_done",
                     "yo_read", "st_done", "st_new", "xdt_ready", "xdd_ready", "t1_ready", "y_read", "out_ready", "z_ready")
            s = {n: sem(n, ctx) for n in names}
            x_in = [sem(f"x_in{k}", ctx) for k in range(2)]
            stored = [sem(f"stored{k}", ctx) for k in range(2)]
            dve_own = sem("dve_own", ctx)
            pool_own = sem("pool_own", ctx)
            block = ctx.enter_context(nc.Block())
            LOADS = 16 * 4

            @block.sync
            def _(sp):
                with sp.Fori(0, STEPS // 2) as j:
                    for k in range(2):
                        i = 2 * j + k
                        sp.wait_ge(s["st_done"], 2 * j)
                        sp.wait_ge(s["xdd_ready"], 2 * j)
                        sp.wait_ge(s["t1_ready"], 2 * j)
                        sp.wait_ge(s["yo_done"], 2 * j)
                        sp.dma_start(xr[:, k], x[i]).then_inc(x_in[k], 16)
                        sp.dma_start(bs[:, k], rows[:, i, :, HEADS0:RW]).then_inc(x_in[k], 16)
                        sp.dma_start(btc[:, k, 0], bt_all[:, i, :]).then_inc(x_in[k], 16)
                        sp.dma_start(btc[:, k, 1], ct_all[:, i, :]).then_inc(x_in[k], 16)

            @block.gpsimd
            def _(gp):
                gp.memset(st[:], 0.0).then_inc(s["st_new"], 1)
                with gp.Fori(0, STEPS // 2) as j:
                    for k in range(2):
                        i = 2 * j + k
                        gp.wait_ge(x_in[k], LOADS * (j + 1))
                        gp.wait_ge(s["yd_done"], i)
                        gp.wait_ge(s["st_done"], i)
                        for dst, weight, ready in ((xdt, dt, "xdt_ready"), (xdd, dx, "xdd_ready")):
                            by_head = weight[:, i, :].rearrange("p (n o) -> p n o", o=1).to_broadcast([P, NB, P])
                            gp.tensor_tensor(dst[:].rearrange("p b (h d) -> p (b h) d", h=HEADS0),
                                             xr[:, k].rearrange("p b (h d) -> p (b h) d", h=HEADS0), by_head, ALU.mult).then_inc(s[ready], 1)
                        gp.wait_ge(s["y_read"], 2 * j)
                        for b in range(BATCH):
                            last = gp.tensor_tensor(zz[:, k, b], xr[:, k, b], dcoef[:], ALU.mult)
                        last.then_inc(s["t1_ready"], 1)

            @block.tensor
            def _(pe):
                pe.wait_ge(s["st_new"], 1)
                with pe.Fori(0, STEPS // 2) as j:
                    for k in range(2):
                        i = 2 * j + k
                        pe.wait_ge(x_in[k], LOADS * (j + 1))
                        pe.wait_ge(s["m_ready"], i)
                        for b in range(BATCH):
                            mm = pe.matmul(ps[:, G, b * P:(b + 1) * P], btc[:, k, 0, b * P:(b + 1) * P],
                                           btc[:, k, 1, b * P:(b + 1) * P], start=True, stop=True)
                        mm.then_inc(s["g_done"], 1)
                        for half in range(2):
                            pe.wait_ge(s["seg_ready"], 2 * i + half + 1)
                            pe.matmul(ps[:, SEG + half, :], strict[:], seg[:, half].rearrange("p b h l -> p (b h l)"),
                                      start=True, stop=True).then_inc(s["seg_done"], 1)
                        pe.wait_ge(s["st_new"], BATCH * i + 1)
                        for b in range(BATCH):
                            mm = pe.matmul(ps[:, YO + b // 2, (b % 2) * D:(b % 2 + 1) * D], btc[:, k, 1, b * P:(b + 1) * P],
                                           st[:, b, :], start=b % 2 == 0, stop=b % 2 == 1, skip_group_check=True)
                        mm.then_inc(s["yo_done"], 1)
                        pe.wait_ge(s["m_ready"], i + 1)
                        pe.wait_ge(s["xdt_ready"], i + 1)
                        pe.wait_ge(s["y_read"], i)
                        for b in range(BATCH):
                            for h in range(HEADS0):
                                lo = (b % 2) * D + h * P
                                mm = pe.matmul(ps[:, YD + b // 2, lo:lo + P], mt[:, b, h, :], xdt[:, b, h * P:(h + 1) * P],
                                               start=True, stop=True)
                        mm.then_inc(s["yd_done"], 1)
                        pe.wait_ge(s["xdd_ready"], i + 1)
                        pe.wait_ge(s["yo_read"], i + 1)
                        for b in range(BATCH):
                            mm = pe.matmul(ps[0:STATE0, ST + b // 2, (b % 2) * D:(b % 2 + 1) * D], bs[:, k, b, :],
                                           xdd[:, b, :], start=True, stop=True)
                        mm.then_inc(s["st_done"], 1)

            @block.scalar
            def _(act):
                with act.Fori(0, STEPS // 2) as j:
                    for k in range(2):
                        i = 2 * j + k
                        for half in range(2):
                            act.wait_ge(s["seg_done"], 2 * i + half + 1)
                            act.wait_ge(s["m_ready"], i)
                            act.activation(lm[:, half].rearrange("p b h l -> p (b h l)"), ps[:, SEG + half, :], ACT.Exp).then_inc(s["l_ready"], 1)
                        act.wait_ge(s["out_ready"], i + 1)
                        act.dma_start(x1[i], out[:, k]).then_inc(stored[k], 16)
                for k in range(2):
                    act.wait_ge(stored[k], 16 * (STEPS // 2))

            @block.vector
            def _(ve):
                NV = LN_LINKS + 1 + 3 + 8
                ch = Chain(ve, dve_own, NV)
                with ve.Fori(0, STEPS // 2) as j:
                    for k in range(2):
                        i = 2 * j + k
                        ch.turn(i)
                        ve.wait_ge(s["seg_done"], 2 * i)
                        for half in range(2):
                            for b in range(BATCH // 2):
                                for h in range(HEADS0):
                                    n = (half * BATCH // 2 + b) * HEADS0 + h
                                    last = ve.tensor_scalar(seg[:, half, b, h, :], tri[:], a[:, i, n:n + 1], None, ALU.mult)
                            last.then_inc(s["seg_ready"], 1)
                        ve.wait_ge(s["g_done"], i + 1)
                        ve.wait_ge(s["yd_done"], i)
                        ch.link(ve.tensor_tensor(gm[:], ps[:, G, :].rearrange("p (b l) -> p b l", b=BATCH),
                                                 tri[:].unsqueeze(1).to_broadcast([P, BATCH, P]), ALU.mult))
                        ve.wait_ge(s["l_ready"], 2 * i + 2)
                        for h in range(HEADS0):
                            for half in range(2):
                                bb = slice(half * 2, half * 2 + 2)
                                last = ve.tensor_tensor(mt[:, bb, h, :], gm[:, bb, :], lm[:, half, :, h, :], ALU.mult)
                                if (h, half) != (1, 1):
                                    ch.mark(last)
                        last.then_inc(s["m_ready"], 1)
                        ve.wait_ge(s["yo_done"], i + 1)
                        ve.wait_ge(s["t1_ready"], i + 1)
                        for b in range(BATCH):
                            for h in range(HEADS0):
                                n, cols = b * HEADS0 + h, slice(h * P, (h + 1) * P)
                                lo = (b % 2) * D + h * P
                                last = ve.scalar_tensor_tensor(z2[:, b, cols], ps[:, YO + b // 2, lo:lo + P], dec[:, 0, i, n:n + 1],
                                                               zz[:, k, b, cols], ALU.mult, ALU.add)
                                if n < 7:
                                    ch.mark(last)
                        last.then_inc(s["yo_read"], 1)
                        ve.wait_ge(s["yo_read"], i + 1)
                        ve.wait_ge(s["yd_done"], i + 1)
                        for half in range(2):
                            bb = slice(half * 2, half * 2 + 2)
                            last = ve.tensor_tensor(z2[:, bb], ps[:, YD + half, :].rearrange("p (b d) -> p b d", b=2), z2[:, bb], ALU.add)
                            if half == 0:
                                ch.mark(last)
                        last.then_inc(s["y_read"], 1)
                        ve.wait_ge(s["st_done"], i + 1)
                        for b in range(BATCH):
                            for h in range(HEADS0):
                                n, cols = b * HEADS0 + h, slice(h * P, (h + 1) * P)
                                lo = (b % 2) * D + h * P
                                last = ve.scalar_tensor_tensor(st[:, b, cols], st[:, b, cols], dec[0:STATE0, 2, i, n:n + 1],
                                                               ps[0:STATE0, ST + b // 2, lo:lo + P], ALU.mult, ALU.add)
                            last.then_inc(s["st_new"], 1)
                        ve.wait_ge(s["y_read"], i + 1)
                        ve.wait_ge(stored[k], 16 * j)
                        layernorm(ch, z2, out[:, k], stats, small, smalli, BATCH).then_inc(s["out_ready"], 1)
                        ch.end()


def phase_ffn(nc, x1, w1, b1, w2, b2, ident, x2, xg=None, zeros_done=None):
    HM = w1.shape[2] // P
    with ExitStack() as ctx:
        def sb(name, shape, dt=F32):
            return ctx.enter_context(nc.sbuf_tensor("b_" + name, shape, dt))

        def sem(name):
            return ctx.enter_context(nc.semaphore("b_" + name))

        w1s = sb("w1", [P, KD, HM * P])
        w2s = sb("w2", [P, HM, D])
        b1s = sb("b1", [P, HM])
        b2s = sb("b2", [P, D])
        ids = sb("ident", [P, P])
        xr = sb("xr", [P, 2, BATCH, D])
        xb = sb("xb", [P, 2, BATCH, D])
        xts = sb("xts", [P, 2, KD, TOK])
        ht = sb("ht", [P, 2, TOK])
        z = sb("z", [P, BATCH, D])
        out = sb("out", [P, 2, BATCH, D])
        stats = sb("stats", [P, BATCH, 6])
        small = sb("small", [P, 5, BATCH])
        smalli = sb("smalli", [P, BATCH], I32)
        ps = ctx.enter_context(nc.psum_tensor("b_ps", [P, 8, 512], F32))
        T, H, O = 0, 2, 4
        names = ("weights_in", "turned", "xt_ready", "h_done", "h_ready", "h_used", "o_done", "xb_ready", "z_ready", "out_ready", "dve_own")
        s = {n: sem(n) for n in names}
        x_in = [sem(f"x_in{k}") for k in range(2)]
        stored = [sem(f"stored{k}") for k in range(2)]
        zeros = sb("zeros", [P, ZERO_COLS])
        zeros_set = sem("zeros_set")
        block = ctx.enter_context(nc.Block())
        WEIGHTS = 16 * 5

        @block.sync
        def _(sp):
            sp.dma_start(ids[:], ident).then_inc(s["weights_in"], 16)
            for dst, src in ((w1s[:], w1), (b1s[:], b1), (w2s[:], w2), (b2s[:], b2.partition_broadcast(P))):
                sp.dma_start(dst, src).then_inc(s["weights_in"], 16)
            with sp.Fori(0, STEPS // 2) as j:
                for k in range(2):
                    sp.wait_ge(s["turned"], 2 * j)
                    sp.wait_ge(s["xb_ready"], 2 * j)
                    sp.dma_start(xr[:, k], x1[2 * j + k]).then_inc(x_in[k], 16)

        @block.gpsimd
        def _(gp):
            if xg is not None:
                gp.memset(zeros[:], 0.0).then_inc(zeros_set, 1)
                gp.wait_ge(zeros_set, 1)
                cleared = xg.rearrange("(n p m) d -> n p (m d)", p=P, n=ZERO_DMAS)
                for n in range(ZERO_DMAS):
                    gp.dma_start(cleared[n], zeros[:]).then_inc(zeros_done, 16)
            gp.wait_ge(s["weights_in"], WEIGHTS)
            with gp.Fori(0, STEPS // 2) as j:
                for k in range(2):
                    gp.wait_ge(x_in[k], 16 * (j + 1))
                    gp.wait_ge(s["z_ready"], 2 * j)
                    gp.tensor_tensor(xb[:, k], xr[:, k], b2s[:].unsqueeze(1).to_broadcast([P, BATCH, D]), ALU.add).then_inc(s["xb_ready"], 1)
                    gp.wait_ge(s["out_ready"], 2 * j + k + 1)
                    gp.dma_start(x2[2 * j + k], out[:, k]).then_inc(stored[k], 16)
            for k in range(2):
                gp.wait_ge(stored[k], 16 * (STEPS // 2))

        @block.tensor
        def _(pe):
            pe.wait_ge(s["weights_in"], WEIGHTS)
            with pe.Fori(0, STEPS // 2) as j:
                for k in range(2):
                    i = 2 * j + k
                    pe.wait_ge(x_in[k], 16 * (j + 1))
                    pe.wait_ge(s["xt_ready"], i)
                    for kd in range(KD):
                        for b in range(BATCH):
                            mm = pe.transpose(ps[:, T + kd, b * P:(b + 1) * P], xr[:, k, b, kd * P:(kd + 1) * P], ids[:])
                    mm.then_inc(s["turned"], 1)

                    def down(m):
                        pe.wait_ge(s["h_ready"], HM * i + m + 1)
                        for b in range(BATCH):
                            lo = (b % 2) * D
                            mm = pe.matmul(ps[:, O + 2 * k + b // 2, lo:lo + D], ht[:, m % 2, b * P:(b + 1) * P], w2s[:, m, :],
                                           start=m == 0 and b % 2 == 0, stop=m == HM - 1, skip_group_check=True)
                        mm.then_inc(s["h_used"], 1)
                        return mm

                    pe.wait_ge(s["xt_ready"], i + 1)
                    pe.wait_ge(s["z_ready"], 2 * j)
                    for m in range(HM):
                        pe.wait_ge(s["h_ready"], HM * i + max(m - 1, 0))
                        for kd in range(KD):
                            mm = pe.matmul(ps[:, H + m % 2, :], w1s[:, kd, m * P:(m + 1) * P], xts[:, k, kd, :],
                                           start=kd == 0, stop=kd == KD - 1)
                        mm.then_inc(s["h_done"], 1)
                        if m:
                            down(m - 1)
                    down(HM - 1)

        @block.scalar
        def _(act):
            act.wait_ge(s["weights_in"], WEIGHTS)
            with act.Fori(0, STEPS // 2) as j:
                for k in range(2):
                    i = 2 * j + k
                    act.wait_ge(s["turned"], i + 1)
                    act.activation(xts[:, k].rearrange("p k n -> p (k n)"), ps[:, T:T + KD, :].rearrange("p k n -> p (k n)"), ACT.Copy).then_inc(s["xt_ready"], 1)
                    for m in range(HM):
                        act.wait_ge(s["h_done"], HM * i + m + 1)
                        act.wait_ge(s["h_used"], HM * i + max(m - 1, 0))
                        act.activation(ht[:, m % 2, :], ps[:, H + m % 2, :], ACT.Gelu, bias=b1s[:, m:m + 1]).then_inc(s["h_ready"], 1)

        @block.vector
        def _(ve):
            ch = Chain(ve, s["dve_own"], LN_LINKS + 1)
            with ve.Fori(0, STEPS // 2) as j:
                for k in range(2):
                    i = 2 * j + k
                    ch.turn(i)
                    ve.wait_ge(s["xb_ready"], i + 1)
                    ve.wait_ge(s["h_used"], HM * (i + 1))
                    for half in range(2):
                        bb = slice(2 * half, 2 * half + 2)
                        last = ve.tensor_tensor(z[:, bb], ps[:, O + 2 * k + half, :].rearrange("p (b d) -> p b d", b=2), xb[:, k, bb], ALU.add)
                        if half == 0:
                            ch.mark(last)
                    last.then_inc(s["z_ready"], 1)
                    ve.wait_ge(s["z_ready"], i + 1)
                    ve.wait_ge(stored[k], 16 * j)
                    layernorm(ch, z, out[:, k], stats, small, smalli, BATCH).then_inc(s["out_ready"], 1)
                    ch.end()


def phase_attention(nc, x2, wqkv, bqkv, wout, bout, omega, nodes, weights, masks, ident, x3):
    with ExitStack() as ctx:
        def sb(name, shape, dt=F32):
            return ctx.enter_context(nc.sbuf_tensor("c_" + name, shape, dt))

        def sem(name):
            return ctx.enter_context(nc.semaphore("c_" + name))

        raw = sb("raw", [P, KD * 3 * D])
        wq = sb("wqkv", [P, 2, KD, 3 * D], F32R)
        wo = sb("wout", [P, 2, KD, D], F32R)
        om = sb("omega", [P, 2, PAIRS, P], F32R)
        bq = sb("bqkv", [P, 3 * D])
        bo = sb("bout", [P, D])
        ids = sb("ident", [P, P])
        tri = sb("tri", [P, P])
        nw = sb("nw", [P, 2])
        fc = sb("fc", [P, 4])
        ns = sb("ns", [P, 4, P])
        nsi = sb("nsi", [P, P], I32)
        xr = sb("xr", [P, BATCH, D])
        xb = sb("xb", [P, BATCH, D])
        xts = sb("xts", [P, 2, KD, TOK], F32R)
        qk = sb("qk", [P, BATCH, 2 * D])
        sq = sb("sq", [P, BATCH, 2 * D])
        va = sb("va", [P, BATCH, HEADS1, VP])
        nrm = sb("nrm", [P, 3, BATCH * 2 * HEADS1])
        nrmi = sb("nrmi", [P, BATCH * 2 * HEADS1], I32)
        qkt = sb("qkt", [P, 2, 2 * KD, TOK], F32R)
        cf = sb("cf", [P, 2, 2, TOK])
        ef = sb("ef", [P, TOK])
        qf = sb("qf", [P, 3, TOK])
        kf = sb("kf", [P, 3, TOK])
        kr = sb("kr", [P, 2, BATCH, P])
        sm = sb("sm", [P, 2, 2, BATCH, P])
        state = sb("state", [P, PAIRS, BATCH, 2, VP])
        ot = sb("ot", [P, PAIRS // 2, TOK])
        den = sb("den", [P, 2, BATCH, 4])
        cr = sb("cr", [P, BATCH, HEADS1, HD])
        ctxt = sb("ctxt", [P, 2, KD, TOK], F32R)
        z = sb("z", [P, BATCH, D])
        out = sb("out", [P, BATCH, D])
        stats = sb("stats", [P, BATCH, 6])
        small = sb("small", [P, 5, BATCH])
        smalli = sb("smalli", [P, BATCH], I32)
        ps = ctx.enter_context(nc.psum_tensor("c_ps", [P, 8, 512], F32))
        names = ("weights_in", "raw_hi", "raw_lo", "scaled", "fc_ready", "x_in", "res_in", "x_done", "x_hi", "x_free", "sq_ready",
                 "rnorm_ready", "qn_ready", "feat_done", "clip_done", "exp_done", "qf_ready", "score_done", "mask_done",
                 "kt_done", "kr_ready", "pair_done", "state_new", "ot_ready", "xb_ready", "z_ready", "out_ready", "stored",
                 "own", "act_own", "raw_in")
        s = {n: sem(n) for n in names}
        block = ctx.enter_context(nc.Block())
        HIGH, LOW, BIAS, AMP = (slice(n, n + 1) for n in range(4))
        FB, SC, KT, OB, SU, X = 0, 2, 4, 5, 6, 7
        LAST = STEPS - 1
        FRONT = {2: (("FT", 0), ("FT", 1)), 3: (("FQ", 0), ("FQ", 1)), 4: (("FQ", 2), ("FQ", 3)), 7: (("FN", 0), ("FN", 2)),
                 8: (("FN", 1), ("FN", 3)), 9: (("FV", 0), ("FV", 1))}
        BACK = {0: (("BO", 0), ("BO", 1)), 1: (("BO", 2), ("BO", 3)), 5: (("BC", 0), ("BC", 1)), 6: (("BW", 0), ("BW", 1))}
        NF, NB_ = 12, 8
        HI = ("FT", "FN", "BC")
        HF, HB = 6, 2

        def steps(i, front, back):
            if i is None:
                n, h = 0, 0
            elif isinstance(i, int) and i == 0:
                n, h = NF, HF
            else:
                n, h = (NF + NB_) * i + NF - NB_, (HF + HB) * i + HF - HB
            if isinstance(i, int) and i == LAST + 1:
                n, h = (NF + NB_) * LAST + NF - NB_ + NB_, (HF + HB) * LAST + HF - HB + HB
            found = []
            for t in range(PAIRS + 2):
                for name, a in (FRONT.get(t, ()) if front else ()) + (BACK.get(t, ()) if back else ()):
                    found.append((t, name, a, n, h))
                    n = n + 1
                    h = h + (name in HI)
            return found

        def everything(eng, body):
            body(None, True, False)
            body(0, True, False)
            with eng.Fori(1, LAST) as i:
                body(i, True, True)
            body(LAST, False, True)
            body(LAST + 1, False, True)

        def wait(eng, name, value):
            if not isinstance(value, int) or value > 0:
                eng.wait_ge(s[name], value)

        def turned_before(i, name, a):
            return next(n + 1 for _, m, b, n, _ in steps(i, True, not (i is None or (isinstance(i, int) and i == 0))) if (m, b) == (name, a))

        @block.sync
        def _(sp):
            sp.dma_start(raw[:], wqkv.rearrange("p k n -> p (k n)")).then_inc(s["raw_in"], 16)
            for dst, src in ((bq[:], bqkv.partition_broadcast(P)), (bo[:], bout.partition_broadcast(P)),
                             (ids[:], ident), (tri[:], masks[0]), (nw[:, 0:1], nodes), (nw[:, 1:2], weights),
                             (ns[:, 0], nodes.rearrange("p o -> (p o)").partition_broadcast(P))):
                sp.dma_start(dst, src).then_inc(s["weights_in"], 16)
            sp.dma_start(xr[:], x2[0]).then_inc(s["x_in"], 16)
            sp.wait_ge(s["raw_lo"], 1)
            sp.dma_start(raw[:, 0:KD * D], wout.rearrange("p k n -> p (k n)")).then_inc(s["raw_in"], 16)
            sp.wait_ge(s["raw_lo"], 2)
            sp.dma_start(raw[:, 0:PAIRS * P], omega.rearrange("p k n -> p (k n)")).then_inc(s["raw_in"], 16)
            sp.dma_start(xb[:], x2[0]).then_inc(s["res_in"], 16)

            def next_x(i, n):
                sp.wait_ge(s["x_done"], turned_before(i, "FT", 1))
                sp.dma_start(xr[:], x2[n]).then_inc(s["x_in"], 16)

            def next_residual(i):
                sp.wait_ge(s["z_ready"], i)
                sp.dma_start(xb[:], x2[i]).then_inc(s["res_in"], 16)

            next_x(None, 1)
            next_x(0, 2)
            with sp.Fori(1, LAST - 1) as i:
                next_x(i, i + 2)
                next_residual(i)
            next_residual(LAST - 1)
            next_residual(LAST)

        @block.gpsimd
        def _(gp):
            def body(i, front, back):
                if front:
                    f = 0 if i is None else i + 1
                    gp.wait_ge(s["x_free"], turned_before(i, "FQ", 3))
                    gp.tensor_tensor(sq[:], qk[:], qk[:], ALU.mult).then_inc(s["sq_ready"], 1)
                    gp.wait_ge(s["rnorm_ready"], f + 1)
                    gp.tensor_tensor(sq[:].rearrange("p b (n d) -> p (b n) d", d=HD), qk[:].rearrange("p b (n d) -> p (b n) d", d=HD),
                                     nrm[:, 1, :].unsqueeze(2).to_broadcast([P, BATCH * 2 * HEADS1, HD]), ALU.mult).then_inc(s["qn_ready"], 1)
                if back:
                    gp.wait_ge(s["out_ready"], i)
                    gp.dma_start(x3[i - 1], out[:]).then_inc(s["stored"], 16)
                if i is not None and not (isinstance(i, int) and i > LAST):
                    gp.wait_ge(s["res_in"], 16 * (i + 1))
                    gp.tensor_tensor(xb[:], xb[:], bo[:].unsqueeze(1).to_broadcast([P, BATCH, D]), ALU.add).then_inc(s["xb_ready"], 1)

            gp.wait_ge(s["weights_in"], 16 * 7)
            everything(gp, body)
            gp.wait_ge(s["stored"], 16 * STEPS)

        @block.tensor
        def _(pe):
            def split3(out_ap, lhs, rhs, kds, first=True, last=True):
                for kd in range(kds):
                    for q, (lp, rp) in enumerate(PARTS):
                        mm = pe.matmul(out_ap, lhs(lp, kd), rhs(rp, kd), start=kd == 0 and q == 0, stop=kd == kds - 1 and q == 2)
                return mm

            def x_step(i, name, a, n):
                wait(pe, "x_free", n)
                front_of = 0 if i is None else i + 1
                if name == "FT":
                    if a == 0:
                        pe.wait_ge(s["x_in"], 16 * (front_of + 1))
                    for b in range(BATCH):
                        mm = pe.transpose(ps[:, X, b * P:(b + 1) * P], xr[:, b, a * P:(a + 1) * P], ids[:])
                elif name == "FQ":
                    mm = split3(ps[:, X, :], lambda p, kd: xts[:, p, kd, a * P:(a + 1) * P], lambda p, kd: wq[:, p, kd, 0:2 * D], KD)
                elif name == "FV":
                    for h in range(2):
                        b = 2 * a + h
                        mm = split3(ps[:, X, h * D:(h + 1) * D], lambda p, kd: xts[:, p, kd, b * P:(b + 1) * P],
                                    lambda p, kd: wq[:, p, kd, 2 * D:3 * D], KD)
                elif name == "FN":
                    pe.wait_ge(s["qn_ready"], front_of + 1)
                    for b in range(BATCH):
                        mm = pe.transpose(ps[:, X, b * P:(b + 1) * P], sq[:, b, a * P:(a + 1) * P], ids[:])
                elif name == "BO":
                    pe.wait_ge(s["ot_ready"], 4 * (i - 1) + a + 1)
                    for b in range(BATCH):
                        mm = pe.transpose(ps[:, X, b * P:(b + 1) * P], ot[:, a, b * P:(b + 1) * P], ids[:])
                elif name == "BC":
                    for b in range(BATCH):
                        mm = pe.transpose(ps[:, X, b * P:(b + 1) * P], cr[:, b, 8 * a:8 * (a + 1), :], ids[:])
                else:
                    for h in range(2):
                        b = 2 * a + h
                        mm = split3(ps[:, X, h * D:(h + 1) * D], lambda p, kd: ctxt[:, p, kd, b * P:(b + 1) * P],
                                    lambda p, kd: wo[:, p, kd, :], KD)
                mm.then_inc(s["x_done"], 1)

            def body(i, front, back):
                pairs = i is not None and not (isinstance(i, int) and i > LAST)
                for t in range(PAIRS + 2):
                    xs = [x for x in steps(i, front, back) if x[0] == t]
                    if pairs and t < PAIRS:
                        for q in range(2):
                            n = 2 * t + q
                            wait(pe, "clip_done", 2 * PAIRS * i + n - 1 if n >= 2 else 2 * PAIRS * i)
                            mm = split3(ps[:, FB + q, :], lambda p, kd: om[:, p, t, :], lambda p, kd: qkt[:, p, KD * q + t // 4, :], 1)
                            mm.then_inc(s["feat_done"], 1)
                    for _, name, a, n, _ in xs[0:1]:
                        x_step(i, name, a, n)
                    if pairs and 1 <= t <= PAIRS:
                        u = t - 1
                        pe.wait_ge(s["exp_done"], 2 * (PAIRS * i + u + 1))
                        pe.wait_ge(s["qf_ready"], PAIRS * i + u + 1)
                        wait(pe, "mask_done", PAIRS * i + u)
                        for b in range(BATCH):
                            for h in range(2):
                                cols, f = slice(b * P, (b + 1) * P), slice(FD * h, FD * (h + 1))
                                mm = pe.matmul(ps[:, SC + h, cols], kf[f, u % 3, cols], qf[f, u % 3, cols], start=True, stop=True)
                        mm.then_inc(s["score_done"], 1)
                        wait(pe, "kr_ready", PAIRS * i + u)
                        for b in range(BATCH):
                            mm = pe.transpose(ps[:, KT, b * P:(b + 1) * P], kf[:, u % 3, b * P:(b + 1) * P], ids[:])
                        mm.then_inc(s["kt_done"], 1)
                    for _, name, a, n, _ in xs[1:2]:
                        if name != "FV":
                            x_step(i, name, a, n)
                    if pairs and t >= 2:
                        u = t - 2
                        pe.wait_ge(s["mask_done"], PAIRS * i + u + 1)
                        pe.wait_ge(s["kr_ready"], PAIRS * i + u + 1)
                        if u % 2 == 0:
                            wait(pe, "ot_ready", PAIRS // 2 * i + u // 2)
                        wait(pe, "state_new", PAIRS * i + u)
                        at = 2 * FD // 2 * (u % 2)
                        for b in range(BATCH):
                            pe.matmul(ps[at:at + 2 * VP, OB, b * P:(b + 1) * P], state[:, u, b].rearrange("p h w -> p (h w)"),
                                      qf[:, u % 3, b * P:(b + 1) * P], start=b == 0, stop=False, skip_group_check=True)
                        for b in range(BATCH):
                            for h in range(2):
                                pe.matmul(ps[at + h * VP:at + (h + 1) * VP, OB, b * P:(b + 1) * P], va[:, b, 2 * u + h, :],
                                          sm[:, u % 2, h, b, :], start=False, stop=True, skip_group_check=True)
                        for b in range(BATCH):
                            mm = pe.matmul(ps[:, SU, b * 2 * VP:(b + 1) * 2 * VP], kr[:, u % 2, b, :],
                                           va[:, b, 2 * u:2 * u + 2, :].rearrange("p h w -> p (h w)"), start=True, stop=True)
                        mm.then_inc(s["pair_done"], 1)
                    for _, name, a, n, _ in xs[1:2]:
                        if name == "FV":
                            x_step(i, name, a, n)

            pe.wait_ge(s["weights_in"], 16 * 7)
            pe.wait_ge(s["raw_lo"], 3)
            pe.wait_ge(s["fc_ready"], 1)
            everything(pe, body)

        @block.scalar
        def _(act):
            def high(dst, n):
                act.activation(dst, raw[:, 0:n], ACT.Copy).then_inc(s["raw_hi"], 1)

            act.wait_ge(s["raw_in"], 16)
            high(wq[:, 0].rearrange("p k n -> p (k n)"), KD * 3 * D)
            act.wait_ge(s["raw_in"], 32)
            high(wo[:, 0].rearrange("p k n -> p (k n)"), KD * D)
            act.wait_ge(s["scaled"], 1)
            high(om[:, 0].rearrange("p k n -> p (k n)"), PAIRS * P)
            act.wait_ge(s["fc_ready"], 1)

            def x_high(i, name, a, n):
                act.wait_ge(s["x_done"], n + 1)
                dst = {"FT": xts, "FN": qkt, "BC": ctxt}[name][:, 0, a, :]
                act.activation(dst, ps[:, X, :], ACT.Copy).then_inc(s["x_hi"], 1)

            def body(i, front, back):
                pairs = i is not None and not (isinstance(i, int) and i > LAST)
                for t in range(PAIRS + 2):
                    xs = [x for x in steps(i, front, back) if x[0] == t and x[1] in HI]
                    if pairs and t < PAIRS:
                        act.wait_ge(s["clip_done"], 2 * PAIRS * i + 2 * t + 1)
                        wait(act, "qf_ready", PAIRS * i + t)
                        act.activation(ef[:], cf[:, t % 2, 0], ACT.Exp, bias=fc[:, BIAS]).then_inc(s["exp_done"], 1)
                        wait(act, "pair_done", PAIRS * i + (t - 2 if t > 2 else 0))
                        act.wait_ge(s["clip_done"], 2 * PAIRS * i + 2 * t + 2)
                        act.activation(kf[:, t % 3, :], cf[:, t % 2, 1], ACT.Exp, bias=fc[:, BIAS]).then_inc(s["exp_done"], 1)
                        act.wait_ge(s["exp_done"], 2 * PAIRS * i + 2 * t + 1)
                        act.activation(qf[:, t % 3, :], ef[:], ACT.Copy, scale=fc[:, AMP]).then_inc(s["qf_ready"], 1)
                    for _, name, a, n, _ in xs[0:1]:
                        x_high(i, name, a, n)
                    if pairs and 1 <= t <= PAIRS:
                        u = t - 1
                        act.wait_ge(s["kt_done"], PAIRS * i + u + 1)
                        wait(act, "pair_done", PAIRS * i + (u - 1 if u > 1 else 0))
                        act.activation(kr[:, u % 2].rearrange("p b f -> p (b f)"), ps[:, KT, :], ACT.Copy).then_inc(s["kr_ready"], 1)
                    for _, name, a, n, _ in xs[1:2]:
                        x_high(i, name, a, n)
                    if pairs and t >= 3 and t % 2 == 1:
                        g = (t - 3) // 2
                        act.wait_ge(s["pair_done"], PAIRS * i + 2 * g + 2)
                        act.activation(ot[:, g], ps[:, OB, :], ACT.Copy).then_inc(s["ot_ready"], 1)

            everything(act, body)

        @block.vector
        def _(ve):
            pre = Chain(ve, s["own"], 0)
            pre.mark(ve.memset(state[:], 0.0))
            pre.link(ve.memset(va[:], 0.0))
            pre.mark(ve.memset(va[:, :, :, HD:HD + 1], 1.0))
            ve.wait_ge(s["weights_in"], 16 * 7)
            pre.link(ve.tensor_scalar(ns[:, 1], ns[:, 0], 0.0, 2.0, ALU.max, ALU.mult))
            rsqrt(pre, ns[:, 1], ns[:, 2], ns[:, 3], nsi[:])
            pre.link(ve.tensor_tensor(ns[:, 1], ns[:, 1], ns[:, 2], ALU.mult))
            pre.mark(ve.tensor_scalar(fc[:, HIGH], nw[:, 0:1], 20.0, None, ALU.add))
            pre.mark(ve.tensor_scalar(fc[:, LOW], nw[:, 0:1], -20.0, None, ALU.add))
            pre.link(ve.tensor_scalar(fc[:, BIAS], nw[:, 0:1], -1.0, None, ALU.mult))
            ve.tensor_scalar(fc[:, AMP], nw[:, 1:2], 0.0, 1.0 / MF, ALU.max, ALU.mult).then_inc(s["fc_ready"], 1)

            def low(dst, hi, n):
                ve.tensor_tensor(dst, raw[:, 0:n], hi.bitcast(F32), ALU.subtract).then_inc(s["raw_lo"], 1)

            ve.wait_ge(s["raw_hi"], 1)
            low(wq[:, 1].rearrange("p k n -> p (k n)"), wq[:, 0].rearrange("p k n -> p (k n)"), KD * 3 * D)
            ve.wait_ge(s["raw_hi"], 2)
            low(wo[:, 1].rearrange("p k n -> p (k n)"), wo[:, 0].rearrange("p k n -> p (k n)"), KD * D)
            ve.wait_ge(s["raw_in"], 48)
            scaled = raw[:, 0:PAIRS * P].rearrange("p (k n) -> p k n", k=PAIRS)
            ve.tensor_tensor(scaled, scaled, ns[:, 1].unsqueeze(1).to_broadcast([P, PAIRS, P]), ALU.mult).then_inc(s["scaled"], 1)
            ve.wait_ge(s["raw_hi"], 3)
            low(om[:, 1].rearrange("p k n -> p (k n)"), om[:, 0].rearrange("p k n -> p (k n)"), PAIRS * P)

            FRONT_OWN = 2 + RSQRT_LINKS - 1
            PAIR_OWN = 2 * PAIRS
            BACK_OWN = 2 * 4 + LN_LINKS

            def x_evac(i, ch, name, a, n, h):
                if name in HI:
                    dst = {"FT": xts, "FN": qkt, "BC": ctxt}[name]
                    ve.wait_ge(s["x_hi"], h + 1)
                    ins = ve.tensor_tensor(dst[:, 1, a, :], ps[:, X, :], dst[:, 0, a, :].bitcast(F32), ALU.subtract)
                else:
                    ve.wait_ge(s["x_done"], n + 1)
                    if name == "FQ":
                        if a == 0 and i is not None:
                            ve.wait_ge(s["qn_ready"], i + 1)
                        ins = ve.tensor_tensor(qk[:, a, :], ps[:, X, :], bq[:, 0:2 * D], ALU.add)
                    elif name == "FV":
                        if i is not None:
                            ve.wait_ge(s["pair_done"], PAIRS * (i + 1))
                        v_bias = bq[:, 2 * D:].rearrange("p (h d) -> p h d", h=HEADS1).unsqueeze(1).to_broadcast([P, 2, HEADS1, HD])
                        ins = ve.tensor_tensor(va[:, 2 * a:2 * a + 2, :, 0:HD], ps[:, X, :].rearrange("p (b h d) -> p b h d", b=2, h=HEADS1),
                                               v_bias, ALU.add)
                    elif name == "BO":
                        got = ps[:, X, :].rearrange("p (b j w) -> p b j w", b=BATCH, j=4)
                        ch.link(ve.tensor_scalar(den[:, 0], got[:, :, :, HD], 1e-6, None, ALU.max))
                        ch.link(ve.reciprocal(den[:, 1], den[:, 0]))
                        ins = ve.tensor_tensor(cr[:, :, 4 * a:4 * a + 4, :], got[:, :, :, 0:HD],
                                               den[:, 1].unsqueeze(3).to_broadcast([P, BATCH, 4, HD]), ALU.mult)
                    else:
                        if a == 0:
                            ve.wait_ge(s["xb_ready"], i)
                            wait(ve, "out_ready", i - 1)
                        ins = ve.tensor_tensor(z[:, 2 * a:2 * a + 2].rearrange("p b d -> p (b d)"), ps[:, X, :],
                                               xb[:, 2 * a:2 * a + 2].rearrange("p b d -> p (b d)"), ALU.add)
                ins.then_inc(s["x_free"], 1)
                if (name, a) == ("BW", 1):
                    ve.wait_ge(s["x_free"], n + 1)
                    ve.nop().then_inc(s["z_ready"], 1)

            def body(i, front, back):
                ch = Chain(ve, s["own"], 0)
                if i is None:
                    ch.n = pre.n
                elif isinstance(i, int) and i == 0:
                    ch.n = pre.n + FRONT_OWN
                else:
                    whole = FRONT_OWN + PAIR_OWN + BACK_OWN
                    ch.base = (i * whole + (pre.n + FRONT_OWN - BACK_OWN)) if not (isinstance(i, int) and i == LAST + 1) else (
                        LAST * whole + pre.n + FRONT_OWN - BACK_OWN + PAIR_OWN + BACK_OWN)
                n0 = ch.n
                pairs = i is not None and not (isinstance(i, int) and i > LAST)
                for t in range(PAIRS + 2):
                    xs = [x for x in steps(i, front, back) if x[0] == t]
                    if pairs and t < PAIRS:
                        for q in range(2):
                            n = 2 * t + q
                            ve.wait_ge(s["feat_done"], 2 * PAIRS * i + n + 1)
                            wait(ve, "exp_done", 2 * PAIRS * i + (n - 3 if n > 3 else 0))
                            ve.tensor_scalar(cf[:, t % 2, q], ps[:, FB + q, :], fc[:, HIGH], fc[:, LOW], ALU.min, ALU.max).then_inc(s["clip_done"], 1)
                    for _, name, a, n, h in xs[0:1]:
                        x_evac(i, ch, name, a, n, h)
                    if pairs and 1 <= t <= PAIRS:
                        u = t - 1
                        ve.wait_ge(s["score_done"], PAIRS * i + u + 1)
                        wait(ve, "pair_done", PAIRS * i + (u - 1 if u > 1 else 0))
                        for h in range(2):
                            ins = ve.tensor_tensor(sm[:, u % 2, h], ps[:, SC + h, :].rearrange("p (b t) -> p b t", t=P),
                                                   tri[:].unsqueeze(1).to_broadcast([P, BATCH, P]), ALU.mult)
                            if h == 0:
                                ch.mark(ins)
                        ins.then_inc(s["mask_done"], 1)
                    for _, name, a, n, h in xs[1:2]:
                        if name != "FV":
                            x_evac(i, ch, name, a, n, h)
                    if pairs and t >= 2:
                        u = t - 2
                        ve.wait_ge(s["pair_done"], PAIRS * i + u + 1)
                        su = ps[:, SU, 0:BATCH * 2 * VP].rearrange("p (b h w) -> p b h w", b=BATCH, h=2)
                        for h in range(2):
                            f = slice(FD * h, FD * (h + 1))
                            ins = ve.tensor_tensor(state[f, u, :, h, :], su[f, :, h, :], state[f, u, :, h, :], ALU.add)
                            if h == 0:
                                ch.mark(ins)
                        ins.then_inc(s["state_new"], 1)
                    for _, name, a, n, h in xs[1:2]:
                        if name == "FV":
                            x_evac(i, ch, name, a, n, h)
                    if front and t == 5:
                        nv, nr, nt = nrm[:, 0, :], nrm[:, 1, :], nrm[:, 2, :]
                        ve.wait_ge(s["sq_ready"], (0 if i is None else i + 1) + 1)
                        ch.link(ve.tensor_reduce(nv, sq[:].rearrange("p b (n d) -> p (b n) d", d=HD), AX.X, ALU.add))
                        ch.link(ve.tensor_scalar(nv, nv, 1e-24, None, ALU.max))
                        rsqrt(ch, nv, nr, nt, nrmi[:], s["rnorm_ready"])
                    if back and t == 7:
                        wait(ve, "stored", 16 * (i - 1))
                        layernorm(ch, z, out, stats, small, smalli, BATCH).then_inc(s["out_ready"], 1)
                assert ch.n - n0 == front * FRONT_OWN + pairs * PAIR_OWN + back * BACK_OWN, (ch.n - n0, front, pairs, back)

            everything(ve, body)


def phase_shared(nc, x3, sw, rw, rb, ident, xs, routed_w, wall, logits, wall_in):
    with ExitStack() as ctx:
        def sb(name, shape, dt=F32):
            return ctx.enter_context(nc.sbuf_tensor("d_" + name, shape, dt))

        def sem(name):
            return ctx.enter_context(nc.semaphore("d_" + name))

        raw = sb("raw", [P, 2, 1024])
        whl = sb("whl", [P, 2, SHARED, WCOLS], F32R)
        rws = sb("rw", [P, KD, EXPERTS])
        rbs = sb("rb", [P, EXPERTS])
        ids = sb("ident", [P, P])
        xr = sb("xr", [P, 2, BATCH, D])
        xtf = sb("xtf", [P, KD, TOK])
        xhl = sb("xhl", [P, 2, KD, TOK], F32R)
        act_h = sb("act_h", [P, 2, TOK])
        g = sb("g", [P, 2, TOK])
        ghl = sb("ghl", [P, 2, 2, TOK], F32R)
        z = sb("z", [P, 2, BATCH, D])
        ps = ctx.enter_context(nc.psum_tensor("d_ps", [P, 8, 512], F32))
        names = ("consts_in", "raw_hi", "raw_lo", "turned", "xtf_ready", "xhi_ready", "xlo_ready", "h_done", "silu_done",
                 "g_ready", "ghi_ready", "glo_ready", "g_used", "logits_done", "logits_read", "z_ready", "own")
        raw_in = [sem(f"raw_in{k}") for k in range(2)]
        s = {n: sem(n) for n in names}
        x_in = [sem(f"x_in{k}") for k in range(2)]
        stored = [sem(f"stored{k}") for k in range(2)]
        block = ctx.enter_context(nc.Block())
        NCH = SHARED * WCOLS // 1024
        NM = SHARED * HM
        T, H, O = 0, 2, 6
        swf = sw.rearrange("p e n -> p (e n)")
        whlf = whl[:].rearrange("p t e n -> p t (e n)")

        @block.sync
        def _(sp):
            for dst, src in ((rws[:], rw), (ids[:], ident), (rbs[:], rb.partition_broadcast(P))):
                sp.dma_start(dst, src).then_inc(s["consts_in"], 16)
            for n in range(NCH):
                if n >= 2:
                    sp.wait_ge(s["raw_lo"], n - 1)
                sp.dma_start(raw[:, n % 2], swf[:, n * 1024:(n + 1) * 1024]).then_inc(raw_in[n % 2], 16)
                if n < 2:
                    sp.dma_start(xr[:, n], x3[n]).then_inc(x_in[n], 16)
            for e in range(EXPERTS):
                sp.dma_start(wall[:, e], routed_w[:, e]).then_inc(wall_in, 16)
            with sp.Fori(1, STEPS // 2) as j:
                for k in range(2):
                    sp.wait_ge(s["turned"], 2 * j - 1 + k)
                    sp.wait_ge(s["z_ready"], 2 * j - 1 + k)
                    sp.dma_start(xr[:, k], x3[2 * j + k]).then_inc(x_in[k], 16)

        @block.gpsimd
        def _(gp):
            for n in range(NCH):
                gp.wait_ge(s["raw_hi"], n + 1)
                cols = slice(n * 1024, (n + 1) * 1024)
                gp.tensor_tensor(whlf[:, 1, cols], raw[:, n % 2], whlf[:, 0, cols].bitcast(F32), ALU.subtract).then_inc(s["raw_lo"], 1)
            with gp.Fori(0, STEPS // 2) as j:
                for k in range(2):
                    gp.wait_ge(s["z_ready"], 2 * j + k + 1)
                    gp.dma_start(xs[2 * j + k], z[:, k]).then_inc(stored[k], 16)
            for k in range(2):
                gp.wait_ge(stored[k], 16 * (STEPS // 2))

        @block.tensor
        def _(pe):
            pe.wait_ge(s["consts_in"], 48)
            pe.wait_ge(s["raw_lo"], NCH)
            with pe.Fori(0, STEPS // 2) as j:
                for k in range(2):
                    i = 2 * j + k
                    pe.wait_ge(x_in[k], 16 * (j + 1))
                    pe.wait_ge(s["xtf_ready"], i)
                    pe.wait_ge(s["logits_read"], i)
                    for kd in range(KD):
                        for b in range(BATCH):
                            mm = pe.transpose(ps[:, T + kd, b * P:(b + 1) * P], xr[:, k, b, kd * P:(kd + 1) * P], ids[:])
                    mm.then_inc(s["turned"], 1)

                    def down(n):
                        pe.wait_ge(s["ghi_ready"], NM * i + n + 1)
                        pe.wait_ge(s["glo_ready"], NM * i + n + 1)
                        for b in range(BATCH):
                            for q, (gp_, wp_) in enumerate(PARTS):
                                lo = W2AT + (n % HM) * D
                                mm = pe.matmul(ps[:, O + b // 2, (b % 2) * D:(b % 2 + 1) * D], ghl[:, n % 2, gp_, b * P:(b + 1) * P],
                                               whl[:, wp_, n // HM, lo:lo + D],
                                               start=n == 0 and q == 0 and b % 2 == 0, stop=n == NM - 1 and q == 2, skip_group_check=True)
                        mm.then_inc(s["g_used"], 1)

                    pe.wait_ge(s["xhi_ready"], i + 1)
                    pe.wait_ge(s["xlo_ready"], i + 1)
                    for n in range(NM):
                        e, m = n // HM, n % HM
                        pe.wait_ge(s["g_ready"], NM * i + max(n - 1, 0))
                        for w, at in enumerate((W1AT, W3AT)):
                            for q in range(3 * KD):
                                kd, (xp, wp) = q // 3, PARTS[q % 3]
                                lo = at + kd * HID + m * P
                                mm = pe.matmul(ps[:, H + 2 * (n % 2) + w, :], whl[:, wp, e, lo:lo + P], xhl[:, xp, kd, :],
                                               start=q == 0, stop=q == 3 * KD - 1)
                            mm.then_inc(s["h_done"], 1)
                        if n == 0:
                            pe.wait_ge(s["z_ready"], i)
                            pe.wait_ge(s["xtf_ready"], i + 1)
                            for b in range(BATCH):
                                for kd in range(KD):
                                    mm = pe.matmul(ps[:, T, b * EXPERTS:(b + 1) * EXPERTS], xtf[:, kd, b * P:(b + 1) * P], rws[:, kd, :],
                                                   start=kd == 0, stop=kd == KD - 1)
                            mm.then_inc(s["logits_done"], 1)
                        if n:
                            down(n - 1)
                    down(NM - 1)

        @block.scalar
        def _(act):
            for n in range(NCH):
                act.wait_ge(raw_in[n % 2], 16 * (n // 2 + 1))
                act.activation(whlf[:, 0, n * 1024:(n + 1) * 1024], raw[:, n % 2], ACT.Copy).then_inc(s["raw_hi"], 1)
            with act.Fori(0, STEPS // 2) as j:
                for k in range(2):
                    i = 2 * j + k
                    act.wait_ge(s["xtf_ready"], i + 1)
                    act.wait_ge(s["g_used"], NM * i)
                    act.activation(xhl[:, 0].rearrange("p k n -> p (k n)"), xtf[:].rearrange("p k n -> p (k n)"), ACT.Copy).then_inc(s["xhi_ready"], 1)
                    for n in range(NM):
                        act.wait_ge(s["h_done"], 2 * (NM * i + n) + 1)
                        act.wait_ge(s["g_ready"], NM * i + max(n - 1, 0))
                        act.activation(act_h[:, n % 2], ps[:, H + 2 * (n % 2), :], ACT.Silu).then_inc(s["silu_done"], 1)
                        act.wait_ge(s["g_ready"], NM * i + n + 1)
                        act.wait_ge(s["g_used"], NM * i + max(n - 1, 0))
                        act.activation(ghl[:, n % 2, 0], g[:, n % 2], ACT.Copy).then_inc(s["ghi_ready"], 1)

        @block.vector
        def _(ve):
            ch = Chain(ve, s["own"], 1)
            ve.wait_ge(s["consts_in"], 48)
            with ve.Fori(0, STEPS // 2) as j:
                for k in range(2):
                    i = 2 * j + k
                    ch.turn(i)
                    ve.wait_ge(s["turned"], i + 1)
                    ve.wait_ge(s["xhi_ready"], i)
                    ve.wait_ge(s["logits_done"], i)
                    ve.tensor_copy(xtf[:], ps[:, T:T + KD, :]).then_inc(s["xtf_ready"], 1)
                    ve.wait_ge(s["xhi_ready"], i + 1)
                    ve.wait_ge(s["xtf_ready"], i + 1)
                    ve.tensor_tensor(xhl[:, 1], xtf[:], xhl[:, 0].bitcast(F32), ALU.subtract).then_inc(s["xlo_ready"], 1)
                    for n in range(NM):
                        ve.wait_ge(s["silu_done"], NM * i + n + 1)
                        ve.wait_ge(s["h_done"], 2 * (NM * i + n) + 2)
                        ve.wait_ge(s["ghi_ready"], NM * i + max(n - 1, 0))
                        ve.tensor_tensor(g[:, n % 2], ps[:, H + 2 * (n % 2) + 1, :], act_h[:, n % 2], ALU.mult).then_inc(s["g_ready"], 1)
                        ve.wait_ge(s["ghi_ready"], NM * i + n + 1)
                        ve.tensor_tensor(ghl[:, n % 2, 1], g[:, n % 2], ghl[:, n % 2, 0].bitcast(F32), ALU.subtract).then_inc(s["glo_ready"], 1)
                        if n == 0:
                            ve.wait_ge(s["logits_done"], i + 1)
                            ve.tensor_tensor(logits[:, i], ps[:, T, 0:BATCH * EXPERTS].rearrange("p (b e) -> p b e", b=BATCH),
                                             rbs[:].unsqueeze(1).to_broadcast([P, BATCH, EXPERTS]), ALU.add).then_inc(s["logits_read"], 1)
                    ve.wait_ge(s["g_used"], NM * (i + 1))
                    ve.wait_ge(stored[k], 16 * j)
                    for half in range(2):
                        bb = slice(2 * half, 2 * half + 2)
                        last = ve.tensor_tensor(z[:, k, bb], ps[:, O + half, :].rearrange("p (b d) -> p b d", b=2), xr[:, k, bb], ALU.add)
                        if half == 0:
                            ch.mark(last)
                    last.then_inc(s["z_ready"], 1)
                    ch.end()


def phase_route(nc, logits, masks, zeros_done, x3, xg, pos, prob, tile_expert):
    E = EXPERTS
    with ExitStack() as ctx:
        def sb(name, shape, dt=F32):
            return ctx.enter_context(nc.sbuf_tensor("r_" + name, shape, dt))

        def sem(name):
            return ctx.enter_context(nc.semaphore("r_" + name))

        rows = sb("rows", [P, STEPS, BATCH, D])
        tri = sb("tri", [P, P])
        ones = sb("ones", [P, P])
        iota = sb("iota", [P, E])
        ioti = sb("ioti", [P, E], I32)
        gidx = sb("gidx", [P, GROUPS + 1])
        gidxi = sb("gidxi", [P, GROUPS + 1], I32)
        w = {n: sb(n, [P, TILES, E]) for n in ("lg", "cand", "oh0", "oh1", "incl", "tmp")}
        m = sb("m", [P, 2, TILES])
        idx = sb("idx", [P, TILES])
        ex = sb("ex", [P, TILES])
        tot = sb("tot", [P, E, TILES])
        cum = sb("cum", [P, E, TILES])
        cnt = sb("cnt", [P, 6, E])
        cnti = sb("cnti", [P, E], I32)
        te = sb("te", [P, GROUPS + 1, E])
        tf = sb("tf", [P, GROUPS + 1])
        posf = sb("posf", [P, TOPK, TILES])
        ps = ctx.enter_context(nc.psum_tensor("r_ps", [P, 2, 512], F32))
        names = ("in", "iota", "ex_ready", "diff_ready", "sel_ready", "sums_done", "pos_ready", "scattered", "own", "rows_in")
        s = {n: sem(n) for n in names}
        block = ctx.enter_context(nc.Block())
        lgv = logits[:].rearrange("p i b e -> p (i b) e")
        BIG = 3.0e38

        @block.sync
        def _(sp):
            sp.dma_start(tri[:], masks[0]).then_inc(s["in"], 16)
            sp.dma_start(ones[:], masks[2]).then_inc(s["in"], 16)
            for i in range(STEPS):
                sp.dma_start(rows[:, i], x3[i]).then_inc(s["rows_in"], 16)

        @block.gpsimd
        def _(gp):
            gp.iota(ioti[:], [[1, E]], channel_multiplier=0).then_inc(s["iota"], 1)
            gp.iota(gidxi[:], [[SLOT, GROUPS + 1]], channel_multiplier=0).then_inc(s["iota"], 1)
            gp.wait_ge(s["rows_in"], 16 * STEPS)
            gp.wait_ge(s["pos_ready"], 1)
            gp.wait_ge(zeros_done, 16 * ZERO_DMAS)
            for t in range(TILES):
                for k in range(TOPK):
                    gp.indirect_dma_start(xg, bass.IndirectOffsetOnAxis(ap=pos[:, k, t:t + 1], axis=0),
                                          rows[:, t // BATCH, t % BATCH, :], None).then_inc(s["scattered"], 16)
            gp.wait_ge(s["scattered"], 16 * TILES * TOPK)

        @block.tensor
        def _(pe):
            pe.wait_ge(s["in"], 32)
            pe.wait_ge(s["sel_ready"], 1)
            sel = w["tmp"][:].rearrange("p t e -> p (t e)")
            pe.matmul(ps[:, 0, 0:TILES * E], tri[:], sel, start=True, stop=True)
            pe.matmul(ps[:, 1, 0:TILES * E], ones[:], sel, start=True, stop=True).then_inc(s["sums_done"], 1)

        @block.scalar
        def _(act):
            act.wait_ge(s["diff_ready"], 1)
            act.activation(ex[:], idx[:], ACT.Exp).then_inc(s["ex_ready"], 1)

        @block.vector
        def _(ve):
            ch = Chain(ve, s["own"], 0)
            V = ve
            by_e = lambda ap: ap.unsqueeze(1).to_broadcast([P, TILES, E])
            by_t = lambda ap: ap.unsqueeze(2).to_broadcast([P, TILES, E])
            lg, cand, incl, tmp = (w[n][:] for n in ("lg", "cand", "incl", "tmp"))
            ohs = (w["oh0"][:], w["oh1"][:])
            ve.wait_ge(s["iota"], 2)
            ch.mark(V.tensor_copy(iota[:], ioti[:]))
            ch.mark(V.tensor_copy(gidx[:], gidxi[:]))
            ch.link(V.tensor_copy(lg, lgv))
            for k in range(TOPK):
                ch.link(V.tensor_reduce(m[:, k], lg, AX.X, ALU.max))
                ch.link(V.tensor_tensor(cand, lg, by_t(m[:, k]), ALU.is_lt))
                ch.link(V.scalar_tensor_tensor(cand, cand, float(E), by_e(iota[:]), ALU.mult, ALU.add))
                ch.link(V.tensor_reduce(idx[:], cand, AX.X, ALU.min))
                ch.link(V.tensor_tensor(ohs[k], by_e(iota[:]), by_t(idx[:]), ALU.is_equal))
                if k == 0:
                    ch.link(V.scalar_tensor_tensor(lg, ohs[0], -BIG, lg, ALU.mult, ALU.add))
            V.tensor_tensor(tmp, ohs[0], ohs[1], ALU.add).then_inc(s["sel_ready"], 1)
            V.tensor_tensor(idx[:], m[:, 1], m[:, 0], ALU.subtract).then_inc(s["diff_ready"], 1)
            ve.wait_ge(s["ex_ready"], 1)
            ch.link(V.tensor_scalar(posf[:, 0], ex[:], 1.0, None, ALU.add))
            ch.link(V.reciprocal(prob[:, 0], posf[:, 0]))
            ch.mark(V.tensor_tensor(prob[:, 1], prob[:, 0], ex[:], ALU.mult))
            ve.wait_ge(s["sums_done"], 1)
            ch.mark(V.tensor_copy(incl, ps[:, 0, 0:TILES * E].rearrange("p (t e) -> p t e", e=E)))
            ch.link(V.tensor_copy(tot[:], ps[:, 1, 0:TILES * E].rearrange("p (t e) -> p e t", e=E)))
            totf, cumf = tot[:].rearrange("p e t -> p (e t)"), cum[:].rearrange("p e t -> p (e t)")
            ch.link(V.tensor_tensor_scan(cumf, totf, totf, 0.0, ALU.add, ALU.max))
            last = cum[:, :, TILES - 1]
            ch.mark(V.tensor_copy(cnt[:, 0, 0:1], last[:, 0:1]))
            ch.link(V.tensor_tensor(cnt[:, 0, 1:E], last[:, 1:E], last[:, 0:E - 1], ALU.subtract))
            ch.link(V.tensor_scalar(cnti[:], cnt[:, 0], float(SLOT - 1), None, ALU.add))
            ch.link(V.tensor_scalar(cnti[:], cnti[:], SLOT.bit_length() - 1, SLOT.bit_length() - 1, ALU.logical_shift_right, ALU.logical_shift_left))
            ch.link(V.tensor_copy(cnt[:, 1], cnti[:]))
            ch.link(V.tensor_tensor_scan(cnt[:, 2], cnt[:, 1], cnt[:, 1], 0.0, ALU.add, ALU.max))
            ch.link(V.tensor_tensor(cnt[:, 3], cnt[:, 2], cnt[:, 1], ALU.subtract))
            ch.mark(V.tensor_tensor(cnt[:, 4], last, cnt[:, 0], ALU.subtract))
            ch.link(V.tensor_tensor(te[:], gidx[:].unsqueeze(2).to_broadcast([P, GROUPS + 1, E]),
                                    cnt[:, 2].unsqueeze(1).to_broadcast([P, GROUPS + 1, E]), ALU.is_ge))
            ch.link(V.tensor_tensor(cnt[:, 4], cnt[:, 3], cnt[:, 4], ALU.subtract))
            ch.link(V.tensor_reduce(tf[:], te[:], AX.X, ALU.add))
            ch.mark(V.tensor_scalar(tile_expert[:], tf[:], float(E - 1), None, ALU.min))
            ch.link(V.tensor_tensor(cum[:], cum[:], tot[:], ALU.subtract))
            ch.link(V.tensor_tensor(incl, incl, cum[:].rearrange("p e t -> p t e"), ALU.add))
            ch.link(V.tensor_tensor(incl, incl, by_e(cnt[:, 4]), ALU.add))
            for k in range(TOPK):
                ch.link(V.tensor_tensor(cand, incl, ohs[k], ALU.mult))
                ch.link(V.tensor_reduce(posf[:, k], cand, AX.X, ALU.add))
            V.tensor_scalar(pos[:], posf[:], -1.0, None, ALU.add).then_inc(s["pos_ready"], 1)



def phase_experts(nc, wall, wall_in, tile_expert, ident, xg, yg):
    SB = SLOT // P
    with ExitStack() as ctx:
        def sb(name, shape, dt=F32):
            return ctx.enter_context(nc.sbuf_tensor("e_" + name, shape, dt))

        def sem(name):
            return ctx.enter_context(nc.semaphore("e_" + name))

        whl = sb("whl", [P, 2, 2, WCOLS], F32R)
        ids = sb("ident", [P, P])
        xr = sb("xr", [P, 2, SB, D])
        xhl = sb("xhl", [P, 2, 2, KD, SLOT], F32R)
        act_h = sb("act_h", [P, 2, SLOT])
        g = sb("g", [P, 2, SLOT])
        ghl = sb("ghl", [P, 2, 2, SLOT], F32R)
        y = sb("y", [P, 2, SB, D])
        ps = ctx.enter_context(nc.psum_tensor("e_ps", [P, 8, 512], F32))
        names = ("consts_in", "turned", "whi_ready", "wlo_ready", "xhi_ready", "xlo_ready", "h_done", "silu_done", "g_ready",
                 "ghi_ready", "glo_ready", "g_used", "y_ready")
        s = {n: sem(n) for n in names}
        x_in = [sem(f"x_in{k}") for k in range(2)]
        stored = [sem(f"stored{k}") for k in range(2)]
        block = ctx.enter_context(nc.Block())
        xgv = xg.rearrange("(n b p) d -> n p b d", p=P, b=SB)
        ygv = yg.rearrange("(n b p) d -> n p b d", p=P, b=SB)
        PAIR = GROUPS // 2
        NQ = 4
        QC = WCOLS // NQ
        T, H, O = 0, 2, 6

        @block.sync
        def _(sp):
            sp.dma_start(ids[:], ident).then_inc(s["consts_in"], 16)
            for k in range(2):
                sp.dma_start(xr[:, k], xgv[k]).then_inc(x_in[k], 16)
            with sp.Fori(0, PAIR - 1) as j:
                for k in range(2):
                    sp.wait_ge(s["y_ready"], 2 * j + k + 1)
                    sp.dma_start(ygv[2 * j + k], y[:, k]).then_inc(stored[k], 16)
                    sp.dma_start(xr[:, k], xgv[2 * j + k + 2]).then_inc(x_in[k], 16)
            for k in range(2):
                sp.wait_ge(s["y_ready"], GROUPS - 1 + k)
                sp.dma_start(ygv[GROUPS - 2 + k], y[:, k]).then_inc(stored[k], 16)
            for k in range(2):
                sp.wait_ge(stored[k], 16 * PAIR)

        @block.gpsimd
        def _(gp):
            gp.wait_ge(wall_in, 16 * EXPERTS)
            with gp.Fori(0, PAIR) as j:
                for k in range(2):
                    i = 2 * j + k
                    e = gp.value_load(tile_expert[0:1, bass.ds(i, 1)], min_val=0, max_val=EXPERTS - 1)
                    for q in range(NQ):
                        cols = slice(q * QC, (q + 1) * QC)
                        gp.wait_ge(s["whi_ready"], NQ * i + q + 1)
                        gp.tensor_tensor(whl[:, k, 1, cols], wall[:, e, cols], whl[:, k, 0, cols].bitcast(F32), ALU.subtract).then_inc(s["wlo_ready"], 1)

        @block.scalar
        def _(act):
            act.wait_ge(wall_in, 16 * EXPERTS)

            def expert_of(i):
                return act.value_load(tile_expert[0:1, bass.ds(i, 1)], min_val=0, max_val=EXPERTS - 1)

            def split_weights(e, k, q):
                cols = slice(q * QC, (q + 1) * QC)
                act.activation(whl[:, k, 0, cols], wall[:, e, cols], ACT.Copy).then_inc(s["whi_ready"], 1)

            first = expert_of(0)
            for q in range(NQ):
                split_weights(first, 0, q)
            with act.Fori(0, PAIR) as j:
                for k in range(2):
                    i = 2 * j + k
                    e_next = expert_of(i + 1)
                    act.wait_ge(s["turned"], i + 1)
                    act.activation(xhl[:, k, 0], ps[:, k, :].rearrange("p (k n) -> p k n", k=KD), ACT.Copy).then_inc(s["xhi_ready"], 1)
                    for m in range(HM):
                        n = HM * i + m
                        act.wait_ge(s["h_done"], n + 1)
                        act.wait_ge(s["g_ready"], HM * i + max(m - 1, 0))
                        act.activation(act_h[:, m % 2], ps[:, H + m % 2, 0:SLOT], ACT.Silu).then_inc(s["silu_done"], 1)
                        act.wait_ge(s["g_ready"], n + 1)
                        act.wait_ge(s["g_used"], HM * i + max(m - 1, 0))
                        act.activation(ghl[:, m % 2, 0], g[:, m % 2], ACT.Copy).then_inc(s["ghi_ready"], 1)
                        act.wait_ge(s["g_used"], HM * i)
                        split_weights(e_next, 1 - k, m)

        @block.tensor
        def _(pe):
            pe.wait_ge(s["consts_in"], 16)
            with pe.Fori(0, PAIR) as j:
                for k in range(2):
                    i = 2 * j + k
                    pe.wait_ge(x_in[k], 16 * (j + 1))
                    pe.wait_ge(s["xlo_ready"], i)
                    for kd in range(KD):
                        for b in range(SB):
                            mm = pe.transpose(ps[:, k, kd * SLOT + b * P:kd * SLOT + (b + 1) * P], xr[:, k, b, kd * P:(kd + 1) * P], ids[:])
                    mm.then_inc(s["turned"], 1)
                    pe.wait_ge(s["xhi_ready"], i + 1)
                    pe.wait_ge(s["xlo_ready"], i + 1)
                    pe.wait_ge(s["wlo_ready"], NQ * (i + 1))

                    def down(m):
                        pe.wait_ge(s["ghi_ready"], HM * i + m + 1)
                        pe.wait_ge(s["glo_ready"], HM * i + m + 1)
                        for b in range(SB):
                            for q, (gp_, wp_) in enumerate(PARTS):
                                lo = W2AT + m * D
                                mm = pe.matmul(ps[:, O + k, b * D:(b + 1) * D], ghl[:, m % 2, gp_, b * P:(b + 1) * P], whl[:, k, wp_, lo:lo + D],
                                               start=m == 0 and q == 0 and b == 0, stop=m == HM - 1 and q == 2, skip_group_check=True)
                        mm.then_inc(s["g_used"], 1)
                        return mm

                    for m in range(HM):
                        pe.wait_ge(s["g_ready"], HM * i + max(m - 1, 0))
                        for w, at in enumerate((W1AT, W3AT)):
                            for q in range(3 * KD):
                                kd, (xp, wp) = q // 3, PARTS[q % 3]
                                lo = at + kd * HID + m * P
                                mm = pe.matmul(ps[:, H + m % 2, w * SLOT:(w + 1) * SLOT], whl[:, k, wp, lo:lo + P], xhl[:, k, xp, kd, :],
                                               start=q == 0, stop=q == 3 * KD - 1)
                        mm.then_inc(s["h_done"], 1)
                        if m == 0:
                            pe.wait_ge(s["y_ready"], 2 * j)
                        if m:
                            down(m - 1)
                    down(HM - 1)

        @block.vector
        def _(ve):
            with ve.Fori(0, PAIR) as j:
                for k in range(2):
                    i = 2 * j + k
                    ve.wait_ge(s["xhi_ready"], i + 1)
                    ve.tensor_tensor(xhl[:, k, 1], ps[:, k, :].rearrange("p (k n) -> p k n", k=KD), xhl[:, k, 0].bitcast(F32), ALU.subtract).then_inc(s["xlo_ready"], 1)
                    for m in range(HM):
                        n = HM * i + m
                        ve.wait_ge(s["silu_done"], n + 1)
                        ve.wait_ge(s["ghi_ready"], HM * i + max(m - 1, 0))
                        ve.tensor_tensor(g[:, m % 2], ps[:, H + m % 2, SLOT:2 * SLOT], act_h[:, m % 2], ALU.mult).then_inc(s["g_ready"], 1)
                        ve.wait_ge(s["ghi_ready"], n + 1)
                        ve.tensor_tensor(ghl[:, m % 2, 1], g[:, m % 2], ghl[:, m % 2, 0].bitcast(F32), ALU.subtract).then_inc(s["glo_ready"], 1)
                    ve.wait_ge(s["g_used"], HM * (i + 1))
                    ve.wait_ge(stored[k], 16 * j)
                    ve.tensor_copy(y[:, k].rearrange("p b d -> p (b d)"), ps[:, O + k, :]).then_inc(s["y_ready"], 1)


def phase_combine(nc, xs, yg, pos, prob, out):
    with ExitStack() as ctx:
        def sb(name, shape, dt=F32):
            return ctx.enter_context(nc.sbuf_tensor("f_" + name, shape, dt))

        def sem(name):
            return ctx.enter_context(nc.semaphore("f_" + name))

        xr = sb("xr", [P, 2, BATCH, D])
        y = sb("y", [P, 2, TOPK, BATCH, D])
        z = sb("z", [P, BATCH, D])
        o = sb("o", [P, 2, BATCH, D])
        stats = sb("stats", [P, BATCH, 6])
        small = sb("small", [P, 5, BATCH])
        smalli = sb("smalli", [P, BATCH], I32)
        used = sem("used")
        own = sem("own")
        out_ready = sem("out_ready")
        x_in = [sem(f"x_in{k}") for k in range(2)]
        y_in = [sem(f"y_in{k}") for k in range(2)]
        stored = [sem(f"stored{k}") for k in range(2)]
        block = ctx.enter_context(nc.Block())

        @block.sync
        def _(sp):
            with sp.Fori(0, STEPS // 2) as j:
                for k in range(2):
                    sp.wait_ge(used, 2 * j)
                    sp.dma_start(xr[:, k], xs[2 * j + k]).then_inc(x_in[k], 16)

        @block.gpsimd
        def _(gp):
            for i in range(STEPS):
                if i >= 2:
                    gp.wait_ge(used, i - 1)
                for b in range(BATCH):
                    for k in range(TOPK):
                        t = i * BATCH + b
                        gp.indirect_dma_start(y[:, i % 2, k, b, :], None, yg,
                                              bass.IndirectOffsetOnAxis(ap=pos[:, k, t:t + 1], axis=0)).then_inc(y_in[i % 2], 16)

        @block.scalar
        def _(act):
            with act.Fori(0, STEPS // 2) as j:
                for k in range(2):
                    act.wait_ge(out_ready, 2 * j + k + 1)
                    act.dma_start(out[2 * j + k], o[:, k]).then_inc(stored[k], 16)
            for k in range(2):
                act.wait_ge(stored[k], 16 * (STEPS // 2))

        @block.vector
        def _(ve):
            ch = Chain(ve, own, 2 * BATCH - 1 + LN_LINKS)
            with ve.Fori(0, STEPS // 2) as j:
                for k in range(2):
                    i = 2 * j + k
                    ch.turn(i)
                    ve.wait_ge(x_in[k], 16 * (j + 1))
                    ve.wait_ge(y_in[k], 16 * BATCH * TOPK * (j + 1))
                    ve.wait_ge(out_ready, i)
                    for b in range(BATCH):
                        ch.mark(ve.scalar_tensor_tensor(z[:, b], y[:, k, 0, b], prob[:, 0, bass.ds(i * BATCH + b, 1)], xr[:, k, b], ALU.mult, ALU.add))
                    ch.wait()
                    for b in range(BATCH):
                        last = ve.scalar_tensor_tensor(z[:, b], y[:, k, 1, b], prob[:, 1, bass.ds(i * BATCH + b, 1)], z[:, b], ALU.mult, ALU.add)
                        if b < BATCH - 1:
                            ch.mark(last)
                    last.then_inc(used, 1)
                    ve.wait_ge(used, i + 1)
                    ve.wait_ge(stored[k], 16 * j)
                    layernorm(ch, z, o[:, k], stats, small, smalli, BATCH).then_inc(out_ready, 1)
                    ch.end()


def build_program(nc, A, out):
    def views(ap):
        return ap.rearrange("(b c p) d -> c p b d", b=BATCH, p=P)

    x1, x2, x3, xs = (nc.dram_tensor(n, [TILES * P, D], F32, kind="Internal").ap() for n in ("x1", "x2", "x3", "xs"))
    xg, yg = (nc.dram_tensor(n, [SLOTS, D], F32, kind="Internal").ap() for n in ("xg", "yg"))
    flat = lambda ap: ap.rearrange("b t d -> (b t) d")
    with ExitStack() as ctx:
        def sb(name, shape, dt=F32, ctx=ctx):
            return ctx.enter_context(nc.sbuf_tensor(name, shape, dt))

        wall_in = ctx.enter_context(nc.semaphore("wall_in"))
        zeros_done = ctx.enter_context(nc.semaphore("zeros_done"))
        pos = sb("pos", [P, TOPK, TILES], I32)
        prob = sb("prob", [P, TOPK, TILES])
        tile_expert = sb("tile_expert", [P, GROUPS + 1], I32)
        phase_ssd(nc, views(flat(A["x"])), A["x_t"], A["w_xproj"], A["dt_bias"], A["a_log"], A["d_skip"], A["masks"], views(x1))
        phase_ffn(nc, views(x1), A["w1"], A["b1"], A["w2"], A["b2"], A["ident"], views(x2), xg, zeros_done)
        phase_attention(nc, views(x2), A["wqkv"], A["bqkv"], A["wout"], A["bout"], A["omega"], A["nodes"], A["weights"],
                        A["masks"], A["ident"], views(x3))
        with ExitStack() as inner:
            wall = sb("wall", [P, EXPERTS, WCOLS], ctx=inner)
            logits = sb("logits", [P, STEPS, BATCH, EXPERTS], ctx=inner)
            phase_shared(nc, views(x3), A["shared_w"], A["router_w"], A["router_b"], A["ident"], views(xs), A["expert_w"], wall, logits, wall_in)
            phase_route(nc, logits, A["masks"], zeros_done, views(x3), xg, pos, prob, tile_expert)
            phase_experts(nc, wall, wall_in, tile_expert, A["ident"], xg, yg)
        phase_combine(nc, views(xs), yg, pos, prob, views(flat(out)))


def kernel(L0_attn_x, L0_attn_W_xproj, L0_attn_dt_bias, L0_attn_A_log, L0_attn_D, L0_ffn_w1, L0_ffn_b1, L0_ffn_w2, L0_ffn_b2,
           L1_attn_Wqkv, L1_attn_bqkv, L1_attn_Wout, L1_attn_bout, L1_attn_omega, L1_attn_quad_nodes, L1_attn_quad_weights,
           L1_ffn_router_w, L1_ffn_expert_bias, L1_ffn_w1, L1_ffn_w3, L1_ffn_w2, L1_ffn_sw1, L1_ffn_sw3, L1_ffn_sw2):
    import concourse.bacc as bacc
    from concourse.bass_utils import run_bass_kernel_spmd

    def rows_first(w):
        return w.reshape(-1, P, w.shape[-1]).transpose(1, 0, 2)

    def expert_weights(w1, w3, w2):
        def part(w):
            n = w.shape[0]
            return w.transpose(0, 2, 1).reshape(n, w.shape[2] // P, P, w.shape[1]).transpose(2, 0, 1, 3).reshape(P, n, -1)
        return np.concatenate([part(w1), part(w3), part(w2)], -1)

    x = np.asarray(L0_attn_x)
    k = np.arange(P)
    omega_in = np.asarray(L1_attn_omega)
    omega = np.zeros((P, PAIRS, P), omega_in.dtype)
    per = P // HD
    for h in range(HEADS1):
        r0, c0 = HD * (h % per), FD * (h % 2)
        omega[r0:r0 + HD, h // 2, c0:c0 + FD] = omega_in[:, h].transpose(1, 0, 2).reshape(HD, FD)

    def per_feature(v):
        return np.tile(np.repeat(np.asarray(v), MF), 2).reshape(P, 1)

    arrays = {
        "x": x,
        "x_t": x.reshape(BATCH, STEPS, P, KD, P).transpose(1, 4, 3, 0, 2).reshape(STEPS, P, KD, TOK),
        "w_xproj": rows_first(np.asarray(L0_attn_W_xproj).T),
        "dt_bias": L0_attn_dt_bias, "a_log": L0_attn_A_log, "d_skip": L0_attn_D,
        "masks": np.stack([k[:, None] <= k[None, :], k[:, None] > k[None, :], np.ones((P, P), bool)]).astype(np.float32),
        "ident": np.eye(P, dtype=np.float32),
        "w1": rows_first(np.asarray(L0_ffn_w1)), "b1": np.asarray(L0_ffn_b1).reshape(-1, P).T,
        "w2": rows_first(np.asarray(L0_ffn_w2)), "b2": L0_ffn_b2,
        "wqkv": rows_first(np.asarray(L1_attn_Wqkv)), "bqkv": L1_attn_bqkv,
        "wout": rows_first(np.asarray(L1_attn_Wout)), "bout": L1_attn_bout,
        "omega": omega, "nodes": per_feature(L1_attn_quad_nodes), "weights": per_feature(L1_attn_quad_weights),
        "router_w": rows_first(np.asarray(L1_ffn_router_w).T), "router_b": L1_ffn_expert_bias,
        "shared_w": expert_weights(*map(np.asarray, (L1_ffn_sw1, L1_ffn_sw3, L1_ffn_sw2))),
        "expert_w": expert_weights(*map(np.asarray, (L1_ffn_w1, L1_ffn_w3, L1_ffn_w2))),
    }
    arrays = {"in_" + n: np.ascontiguousarray(a) for n, a in arrays.items()}
    nc = bacc.Bacc("TRN2", target_bir_lowering=False, num_devices=1)
    aps = {n[3:]: nc.dram_tensor(n, a.shape, mybir.dt.from_np(a.dtype), kind="ExternalInput").ap() for n, a in arrays.items()}
    out = nc.dram_tensor("out", x.shape, F32, kind="ExternalOutput").ap()
    build_program(nc, aps, out)
    return run_bass_kernel_spmd(nc, [arrays], core_ids=[0]).results[0]["out"]
```

```python
from contextlib import ExitStack

import numpy as np
import concourse.bass as bass
from concourse import mybir

F32 = mybir.dt.float32
I32 = mybir.dt.int32
ALU = mybir.AluOpType
ACT = mybir.ActivationFunctionType
AX = mybir.AxisListType

P = 128
BATCH, SEQ, D = 4, 1024, 256
KD = D // P
CHUNK = 128
STEPS = SEQ // CHUNK
TOK = BATCH * CHUNK
HEADS0, HEADDIM0, STATE0 = 2, 128, 64
EPS = 1e-5
HEADS1, HD, MF, RF = 16, 16, 32, 2
FD = MF * RF
PAIRS = HEADS1 // 2
VP = 32
EXPERTS, SHARED, TOPK, HID = 8, 2, 2, 512
HM = HID // P
F32R = mybir.dt.float32r
WCOLS = 2 * KD * HID + HM * D
W1AT, W3AT, W2AT = 0, KD * HID, 2 * KD * HID
TILES = STEPS * BATCH
SLOT = 256
GROUPS = (TILES * P * TOPK - EXPERTS) // SLOT + EXPERTS
GROUPS += GROUPS % 2
SLOTS = GROUPS * SLOT
PARTS = ((0, 0), (0, 1), (1, 0))
ZERO_DMAS = 5
ZERO_COLS = SLOTS * D // (ZERO_DMAS * P)


PRIMED = 1


def prime(eng, sems):
    for sem in sems:
        eng.sem_inc(sem, PRIMED)


class Chain:

    def __init__(self, eng, sem, per_turn):
        self.eng, self.sem, self.per_turn, self.base, self.n = eng, sem, per_turn, 0, 0

    def turn(self, i):
        self.base, self.n = i * self.per_turn, 0

    def end(self):
        assert self.n == self.per_turn, (self.n, self.per_turn)

    def mark(self, ins):
        ins.then_inc(self.sem, 1)
        self.n += 1

    def wait(self):
        self.eng.wait_ge(self.sem, self.base + self.n)

    def link(self, ins):
        self.mark(ins)
        self.wait()


def rsqrt(chain, v, r, t, ti, ready=None):
    ve = chain.eng
    chain.link(ve.tensor_scalar(ti, v.bitcast(I32), 1, None, ALU.logical_shift_right))
    chain.link(ve.tensor_scalar(r.bitcast(I32), ti, -1.0, float(0x5F3759DF), ALU.mult, ALU.add))
    for n in range(3):
        chain.link(ve.tensor_tensor(t, r, r, ALU.mult))
        chain.link(ve.tensor_tensor(t, t, v, ALU.mult))
        chain.link(ve.tensor_scalar(t, t, -0.5, 1.5, ALU.mult, ALU.add))
        ins = ve.tensor_tensor(r, r, t, ALU.mult)
        if n == 2 and ready is not None:
            ins.then_inc(ready, 1)
        else:
            chain.link(ins)


RSQRT_LINKS = 14


def layernorm(chain, z, out, stats, small, smalli, n):
    ve = chain.eng
    for b in range(n):
        chain.mark(ve.bn_stats(stats[:, b, :], z[:, b, :]))
    chain.wait()
    mean, half, v, r, t = (small[:, k, 0:n] for k in range(5))
    chain.mark(ve.tensor_tensor(mean, stats[:, 0:n, 1], stats[:, 0:n, 4], ALU.add))
    chain.mark(ve.tensor_tensor(half, stats[:, 0:n, 1], stats[:, 0:n, 4], ALU.subtract))
    chain.link(ve.tensor_tensor(v, stats[:, 0:n, 2], stats[:, 0:n, 5], ALU.add))
    chain.mark(ve.tensor_scalar(mean, mean, 0.5, None, ALU.mult))
    chain.mark(ve.tensor_tensor(half, half, half, ALU.mult))
    chain.link(ve.tensor_scalar(v, v, 1.0 / D, EPS, ALU.mult, ALU.add))
    chain.link(ve.scalar_tensor_tensor(v, half, 0.25, v, ALU.mult, ALU.add))
    rsqrt(chain, v, r, t, smalli[:, 0:n])
    last = None
    for b in range(n):
        last = ve.tensor_scalar(out[:, b, :], z[:, b, :], mean[:, b:b + 1], r[:, b:b + 1], ALU.subtract, ALU.mult)
    return last


LN_LINKS = 4 + 3 + 3 + 1 + RSQRT_LINKS


def phase_ssd(nc, x, xt, w, dtb, alog, dskip, masks, x1):
    NB = BATCH * HEADS0
    RW = HEADS0 + STATE0
    with ExitStack() as outer:
        def sb(name, shape, dt=F32, ctx=outer):
            return ctx.enter_context(nc.sbuf_tensor("a_" + name, shape, dt))

        def sem(name, ctx=outer):
            return ctx.enter_context(nc.semaphore("a_" + name))

        bt_all = sb("bt_all", [STATE0, STEPS, TOK])
        ct_all = sb("ct_all", [STATE0, STEPS, TOK])
        rows = sb("rows", [P, STEPS, BATCH, RW])
        tri = sb("tri", [P, P])
        strict = sb("strict", [P, P])
        ones = sb("ones", [P, P])
        dt = sb("dt", [P, STEPS, NB])
        a = sb("a", [P, STEPS, NB])
        dec = sb("dec", [P, 3, STEPS, NB])
        dx = sb("dx", [P, STEPS, NB])
        dcoef = sb("dcoef", [P, D])

        with ExitStack() as ctx:
            wsb = sb("w", [P, KD, 2 * STATE0 + HEADS0], ctx=ctx)
            xts = sb("xts", [P, 2, KD, TOK], ctx=ctx)
            dtb_sb = sb("dtb", [P, NB], ctx=ctx)
            nega = sb("nega", [P, NB], ctx=ctx)
            neg = sb("neg", [P, NB], ctx=ctx)
            dsk = sb("dsk", [P, HEADS0], ctx=ctx)
            z = sb("z", [P, STEPS, NB], ctx=ctx)
            e = sb("e", [P, STEPS, NB], ctx=ctx)
            l1 = sb("l1", [P, STEPS, NB], ctx=ctx)
            q = sb("q", [P, STEPS, NB], ctx=ctx)
            ps = ctx.enter_context(nc.psum_tensor("a_ps", [P, 8, 512], F32))
            consts_in = sem("consts_in", ctx)
            xt_in = [sem(f"xt_in{k}", ctx) for k in range(2)]
            proj = sem("proj", ctx)
            bc_out = sem("bc_out", ctx)
            rows_out = sem("rows_out", ctx)
            dve_own = sem("dve_own0", ctx)
            nega_done = sem("nega_done", ctx)
            na_ready = sem("na_ready", ctx)
            act_own = sem("act_own0", ctx)
            log_ready = sem("log_ready", ctx)
            a_ready = sem("a_ready", ctx)
            cum_ready = sem("cum_ready", ctx)
            dec_ready = sem("dec_ready", ctx)
            block = ctx.enter_context(nc.Block())
            W2 = HEADS0

            @block.sync
            def _(sp):
                prime(sp, [proj, bc_out, rows_out])
                sp.dma_start(wsb[:], w).then_inc(consts_in, 16)
                sp.dma_start(tri[:], masks[0]).then_inc(consts_in, 16)
                sp.dma_start(strict[:], masks[1]).then_inc(consts_in, 16)
                sp.dma_start(ones[:], masks[2]).then_inc(consts_in, 16)
                for b in range(BATCH):
                    sp.dma_start(dtb_sb[:, b * HEADS0:(b + 1) * HEADS0], dtb.partition_broadcast(P)).then_inc(consts_in, 16)
                    sp.dma_start(nega[:, b * HEADS0:(b + 1) * HEADS0], alog.partition_broadcast(P)).then_inc(consts_in, 16)
                sp.dma_start(dsk[:], dskip.partition_broadcast(P)).then_inc(consts_in, 16)
                with sp.Fori(0, STEPS // 2) as j:
                    for k in range(2):
                        sp.wait_ge(proj, PRIMED + 2 * j)
                        sp.dma_start(xts[:, k], xt[2 * j + k]).then_inc(xt_in[k], 16)

            CONSTS = 16 * (5 + 2 * BATCH)

            @block.tensor
            def _(pe):
                pe.wait_ge(consts_in, CONSTS)
                with pe.Fori(0, STEPS // 2) as j:
                    for k in range(2):
                        pe.wait_ge(xt_in[k], 16 * (j + 1))
                        pe.wait_ge(bc_out, PRIMED + 2 * (2 * j))
                        pe.wait_ge(rows_out, PRIMED + 2 * j)
                        for part in range(2):
                            lo = W2 + part * STATE0
                            for kd in range(KD):
                                pe.matmul(ps[0:STATE0, 4 * k + part, :], wsb[:, kd, lo:lo + STATE0], xts[:, k, kd, :],
                                          start=kd == 0, stop=kd == KD - 1)
                        for b in range(BATCH):
                            for kd in range(KD):
                                mm = pe.matmul(ps[:, 4 * k + 2, b * RW:(b + 1) * RW], xts[:, k, kd, b * P:(b + 1) * P],
                                               wsb[:, kd, 0:RW], start=kd == 0, stop=kd == KD - 1)
                        mm.then_inc(proj, 1)
                pe.wait_ge(a_ready, 1)
                af = a[:].rearrange("p c n -> p (c n)")
                for n, mask in enumerate((tri, strict, ones)):
                    mm = pe.matmul(ps[:, n, 0:STEPS * NB], mask[:], af, start=True, stop=True)
                mm.then_inc(cum_ready, 1)

            @block.scalar
            def _(act):
                act.wait_ge(consts_in, CONSTS)
                nc.scalar.activation(neg[:], nega[:], ACT.Exp).then_inc(nega_done, 1)
                with act.Fori(0, STEPS // 2) as j:
                    for k in range(2):
                        act.wait_ge(proj, PRIMED + 2 * j + k + 1)
                        act.activation(bt_all[:, 2 * j + k, :], ps[0:STATE0, 4 * k, :], ACT.Copy).then_inc(bc_out, 1)
                        act.activation(ct_all[:, 2 * j + k, :], ps[0:STATE0, 4 * k + 1, :], ACT.Copy).then_inc(bc_out, 1)
                act.wait_ge(na_ready, 1)
                act.activation(e[:], l1[:], ACT.Exp).then_inc(act_own, 1)
                act.wait_ge(act_own, 1)
                act.activation(q[:], e[:], ACT.Ln, bias=1.0).then_inc(log_ready, 1)
                act.wait_ge(cum_ready, 1)
                for n in range(3):
                    act.activation(dec[:, n].rearrange("p c n -> p (c n)"), ps[:, n, 0:STEPS * NB], ACT.Exp).then_inc(dec_ready, 1)

            @block.vector
            def _(ve):
                ch = Chain(ve, dve_own, 100)
                ve.wait_ge(consts_in, CONSTS)
                for h in range(HEADS0):
                    ch.mark(ve.tensor_scalar(dcoef[:, h * P:(h + 1) * P], ones[:], dsk[:, h:h + 1], None, ALU.add))
                with ve.Fori(0, STEPS // 2) as j:
                    for k in range(2):
                        ve.wait_ge(proj, PRIMED + 2 * j + k + 1)
                        ve.tensor_copy(rows[:, 2 * j + k].rearrange("p b w -> p (b w)"), ps[:, 4 * k + 2, 0:BATCH * RW]).then_inc(rows_out, 1)
                ve.wait_ge(rows_out, PRIMED + STEPS)
                bias = dtb_sb[:].rearrange("p (b h) -> p b h", b=BATCH)
                for c in range(STEPS):
                    ch.mark(ve.tensor_tensor(z[:, c].rearrange("p (b h) -> p b h", b=BATCH), rows[:, c, :, 0:HEADS0], bias, ALU.add))
                ch.wait()
                ve.scalar_tensor_tensor(l1[:], z[:], -1.0, z[:], ALU.mult, ALU.min).then_inc(na_ready, 1)
                ve.wait_ge(log_ready, 1)
                ch.link(ve.tensor_scalar(l1[:], e[:], 0.2, -0.25, ALU.mult, ALU.add))
                for cst in (1.0 / 3.0, -0.5, 1.0):
                    ch.link(ve.tensor_tensor(l1[:], l1[:], e[:], ALU.mult))
                    ch.link(ve.tensor_scalar(l1[:], l1[:], cst, None, ALU.add))
                ch.link(ve.tensor_tensor(l1[:], l1[:], e[:], ALU.mult))
                ch.link(ve.tensor_tensor(l1[:], l1[:], q[:], ALU.subtract))
                ch.link(ve.tensor_scalar(e[:], e[:], 1.0 / 32.0, None, ALU.is_lt))
                ch.link(ve.tensor_tensor(l1[:], l1[:], e[:], ALU.mult))
                ch.link(ve.tensor_tensor(q[:], q[:], l1[:], ALU.add))
                ch.link(ve.scalar_tensor_tensor(dt[:], z[:], 0.0, q[:], ALU.max, ALU.add))
                ve.wait_ge(nega_done, 1)
                ch.link(ve.tensor_scalar(neg[:], neg[:], -1.0, None, ALU.mult))
                for c in range(STEPS):
                    ins = ve.tensor_tensor(a[:, c], dt[:, c], neg[:], ALU.mult)
                    if c < STEPS - 1:
                        ch.mark(ins)
                ins.then_inc(a_ready, 1)
                ve.wait_ge(dec_ready, 3)
                ch.link(ve.tensor_tensor(dx[:], dt[:], dec[:, 1], ALU.mult))

        with ExitStack() as ctx:
            xr = sb("xr", [P, 2, BATCH, D], ctx=ctx)
            bs = sb("bs", [P, 2, BATCH, STATE0], ctx=ctx)
            btc = sb("btc", [STATE0, 2, 2, TOK], ctx=ctx)
            seg = sb("seg", [P, 2, BATCH // 2, HEADS0, P], ctx=ctx)
            lm = sb("lm", [P, 2, BATCH // 2, HEADS0, P], ctx=ctx)
            gm = sb("gm", [P, BATCH, P], ctx=ctx)
            mt = sb("mt", [P, BATCH, HEADS0, P], ctx=ctx)
            xdt = sb("xdt", [P, BATCH, D], ctx=ctx)
            xdd = sb("xdd", [P, BATCH, D], ctx=ctx)
            zz = sb("zz", [P, 2, BATCH, D], ctx=ctx)
            z2 = sb("z2", [P, BATCH, D], ctx=ctx)
            st = sb("st", [STATE0, BATCH, D], ctx=ctx)
            out = sb("out", [P, 2, BATCH, D], ctx=ctx)
            stats = sb("stats", [P, BATCH, 6], ctx=ctx)
            small = sb("small", [P, 5, BATCH], ctx=ctx)
            smalli = sb("smalli", [P, BATCH], I32, ctx=ctx)
            ps = ctx.enter_context(nc.psum_tensor("a_ps2", [P, 8, 512], F32))
            G, SEG, YD, YO, ST = 0, 1, 3, 5, 5
            names = ("seg_ready", "seg_done", "l_ready", "g_done", "m_ready", "yd_done", "yo_done",
                     "yo_read", "st_done", "st_new", "xdt_ready", "xdd_ready", "t1_ready", "y_read", "out_ready", "z_ready")
            s = {n: sem(n, ctx) for n in names}
            x_in = [sem(f"x_in{k}", ctx) for k in range(2)]
            stored = [sem(f"stored{k}", ctx) for k in range(2)]
            dve_own = sem("dve_own", ctx)
            pool_own = sem("pool_own", ctx)
            block = ctx.enter_context(nc.Block())
            LOADS = 16 * 4

            @block.sync
            def _(sp):
                prime(sp, [s[n] for n in ("m_ready", "seg_done", "st_done", "t1_ready", "xdd_ready", "y_read", "yd_done", "yo_done")] + stored)
                with sp.Fori(0, STEPS // 2) as j:
                    for k in range(2):
                        i = 2 * j + k
                        sp.wait_ge(s["st_done"], PRIMED + 2 * j)
                        sp.wait_ge(s["xdd_ready"], PRIMED + 2 * j)
                        sp.wait_ge(s["t1_ready"], PRIMED + 2 * j)
                        sp.wait_ge(s["yo_done"], PRIMED + 2 * j)
                        sp.dma_start(xr[:, k], x[i]).then_inc(x_in[k], 16)
                        sp.dma_start(bs[:, k], rows[:, i, :, HEADS0:RW]).then_inc(x_in[k], 16)
                        sp.dma_start(btc[:, k, 0], bt_all[:, i, :]).then_inc(x_in[k], 16)
                        sp.dma_start(btc[:, k, 1], ct_all[:, i, :]).then_inc(x_in[k], 16)

            @block.gpsimd
            def _(gp):
                gp.memset(st[:], 0.0).then_inc(s["st_new"], 1)
                with gp.Fori(0, STEPS // 2) as j:
                    for k in range(2):
                        i = 2 * j + k
                        gp.wait_ge(x_in[k], LOADS * (j + 1))
                        gp.wait_ge(s["yd_done"], PRIMED + i)
                        gp.wait_ge(s["st_done"], PRIMED + i)
                        for dst, weight, ready in ((xdt, dt, "xdt_ready"), (xdd, dx, "xdd_ready")):
                            by_head = weight[:, i, :].rearrange("p (n o) -> p n o", o=1).to_broadcast([P, NB, P])
                            gp.tensor_tensor(dst[:].rearrange("p b (h d) -> p (b h) d", h=HEADS0),
                                             xr[:, k].rearrange("p b (h d) -> p (b h) d", h=HEADS0), by_head, ALU.mult).then_inc(s[ready], 1)
                        gp.wait_ge(s["y_read"], PRIMED + 2 * j)
                        for b in range(BATCH):
                            last = gp.tensor_tensor(zz[:, k, b], xr[:, k, b], dcoef[:], ALU.mult)
                        last.then_inc(s["t1_ready"], 1)

            @block.tensor
            def _(pe):
                pe.wait_ge(s["st_new"], 1)
                with pe.Fori(0, STEPS // 2) as j:
                    for k in range(2):
                        i = 2 * j + k
                        pe.wait_ge(x_in[k], LOADS * (j + 1))
                        pe.wait_ge(s["m_ready"], PRIMED + i)
                        for b in range(BATCH):
                            mm = pe.matmul(ps[:, G, b * P:(b + 1) * P], btc[:, k, 0, b * P:(b + 1) * P],
                                           btc[:, k, 1, b * P:(b + 1) * P], start=True, stop=True)
                        mm.then_inc(s["g_done"], 1)
                        for half in range(2):
                            pe.wait_ge(s["seg_ready"], 2 * i + half + 1)
                            pe.matmul(ps[:, SEG + half, :], strict[:], seg[:, half].rearrange("p b h l -> p (b h l)"),
                                      start=True, stop=True).then_inc(s["seg_done"], 1)
                        pe.wait_ge(s["st_new"], BATCH * i + 1)
                        for b in range(BATCH):
                            mm = pe.matmul(ps[:, YO + b // 2, (b % 2) * D:(b % 2 + 1) * D], btc[:, k, 1, b * P:(b + 1) * P],
                                           st[:, b, :], start=b % 2 == 0, stop=b % 2 == 1, skip_group_check=True)
                        mm.then_inc(s["yo_done"], 1)
                        pe.wait_ge(s["m_ready"], PRIMED + i + 1)
                        pe.wait_ge(s["xdt_ready"], i + 1)
                        pe.wait_ge(s["y_read"], PRIMED + i)
                        for b in range(BATCH):
                            for h in range(HEADS0):
                                lo = (b % 2) * D + h * P
                                mm = pe.matmul(ps[:, YD + b // 2, lo:lo + P], mt[:, b, h, :], xdt[:, b, h * P:(h + 1) * P],
                                               start=True, stop=True)
                        mm.then_inc(s["yd_done"], 1)
                        pe.wait_ge(s["xdd_ready"], PRIMED + i + 1)
                        pe.wait_ge(s["yo_read"], i + 1)
                        for b in range(BATCH):
                            mm = pe.matmul(ps[0:STATE0, ST + b // 2, (b % 2) * D:(b % 2 + 1) * D], bs[:, k, b, :],
                                           xdd[:, b, :], start=True, stop=True)
                        mm.then_inc(s["st_done"], 1)

            @block.scalar
            def _(act):
                with act.Fori(0, STEPS // 2) as j:
                    for k in range(2):
                        i = 2 * j + k
                        for half in range(2):
                            act.wait_ge(s["seg_done"], PRIMED + 2 * i + half + 1)
                            act.wait_ge(s["m_ready"], PRIMED + i)
                            act.activation(lm[:, half].rearrange("p b h l -> p (b h l)"), ps[:, SEG + half, :], ACT.Exp).then_inc(s["l_ready"], 1)
                        act.wait_ge(s["out_ready"], i + 1)
                        act.dma_start(x1[i], out[:, k]).then_inc(stored[k], 16)
                for k in range(2):
                    act.wait_ge(stored[k], PRIMED + 16 * (STEPS // 2))

            @block.vector
            def _(ve):
                NV = LN_LINKS + 1 + 3 + 8
                ch = Chain(ve, dve_own, NV)
                with ve.Fori(0, STEPS // 2) as j:
                    for k in range(2):
                        i = 2 * j + k
                        ch.turn(i)
                        ve.wait_ge(s["seg_done"], PRIMED + 2 * i)
                        for half in range(2):
                            for b in range(BATCH // 2):
                                for h in range(HEADS0):
                                    n = (half * BATCH // 2 + b) * HEADS0 + h
                                    last = ve.tensor_scalar(seg[:, half, b, h, :], tri[:], a[:, i, n:n + 1], None, ALU.mult)
                            last.then_inc(s["seg_ready"], 1)
                        ve.wait_ge(s["g_done"], i + 1)
                        ve.wait_ge(s["yd_done"], PRIMED + i)
                        ch.link(ve.tensor_tensor(gm[:], ps[:, G, :].rearrange("p (b l) -> p b l", b=BATCH),
                                                 tri[:].unsqueeze(1).to_broadcast([P, BATCH, P]), ALU.mult))
                        ve.wait_ge(s["l_ready"], 2 * i + 2)
                        for h in range(HEADS0):
                            for half in range(2):
                                bb = slice(half * 2, half * 2 + 2)
                                last = ve.tensor_tensor(mt[:, bb, h, :], gm[:, bb, :], lm[:, half, :, h, :], ALU.mult)
                                if (h, half) != (1, 1):
                                    ch.mark(last)
                        last.then_inc(s["m_ready"], 1)
                        ve.wait_ge(s["yo_done"], PRIMED + i + 1)
                        ve.wait_ge(s["t1_ready"], PRIMED + i + 1)
                        for b in range(BATCH):
                            for h in range(HEADS0):
                                n, cols = b * HEADS0 + h, slice(h * P, (h + 1) * P)
                                lo = (b % 2) * D + h * P
                                last = ve.scalar_tensor_tensor(z2[:, b, cols], ps[:, YO + b // 2, lo:lo + P], dec[:, 0, i, n:n + 1],
                                                               zz[:, k, b, cols], ALU.mult, ALU.add)
                                if n < 7:
                                    ch.mark(last)
                        last.then_inc(s["yo_read"], 1)
                        ve.wait_ge(s["yo_read"], i + 1)
                        ve.wait_ge(s["yd_done"], PRIMED + i + 1)
                        for half in range(2):
                            bb = slice(half * 2, half * 2 + 2)
                            last = ve.tensor_tensor(z2[:, bb], ps[:, YD + half, :].rearrange("p (b d) -> p b d", b=2), z2[:, bb], ALU.add)
                            if half == 0:
                                ch.mark(last)
                        last.then_inc(s["y_read"], 1)
                        ve.wait_ge(s["st_done"], PRIMED + i + 1)
                        for b in range(BATCH):
                            for h in range(HEADS0):
                                n, cols = b * HEADS0 + h, slice(h * P, (h + 1) * P)
                                lo = (b % 2) * D + h * P
                                last = ve.scalar_tensor_tensor(st[:, b, cols], st[:, b, cols], dec[0:STATE0, 2, i, n:n + 1],
                                                               ps[0:STATE0, ST + b // 2, lo:lo + P], ALU.mult, ALU.add)
                            last.then_inc(s["st_new"], 1)
                        ve.wait_ge(s["y_read"], PRIMED + i + 1)
                        ve.wait_ge(stored[k], PRIMED + 16 * j)
                        layernorm(ch, z2, out[:, k], stats, small, smalli, BATCH).then_inc(s["out_ready"], 1)
                        ch.end()


def wait(eng, sem, value):
    if not isinstance(value, int) or value > 0:
        eng.wait_ge(sem, value)


def in_pairs(eng, pairs, body):
    def pair(j):
        for k in range(2):
            body(j, k)

    pair(0)
    with eng.Fori(1, pairs - 1) as j:
        pair(j)
    pair(pairs - 1)


def is_turn(j, k, n):
    return isinstance(j, int) and 2 * j + k == n


def phase_ffn(nc, x1, w1, b1, w2, b2, ident, x2, xg=None, zeros_done=None):
    MT = w1.shape[2] // P
    with ExitStack() as ctx:
        def sb(name, shape, dt=F32):
            return ctx.enter_context(nc.sbuf_tensor("b_" + name, shape, dt))

        def sem(name):
            return ctx.enter_context(nc.semaphore("b_" + name))

        w1r = sb("w1r", [P, KD, MT * P])
        w2r = sb("w2r", [P, MT, D])
        w1s = sb("w1", [P, 2, KD, MT * P], F32R)
        w2s = sb("w2", [P, 2, MT, D], F32R)
        b1s = sb("b1", [P, MT])
        b2s = sb("b2", [P, D])
        ids = sb("ident", [P, P])
        xr = sb("xr", [P, 2, BATCH, D])
        xb = sb("xb", [P, 2, BATCH, D])
        xhl = sb("xhl", [P, 2, 2, KD, TOK], F32R)
        h = sb("h", [P, 4, TOK])
        hhl = sb("hhl", [P, 4, 2, TOK], F32R)
        z = sb("z", [P, BATCH, D])
        out = sb("out", [P, 2, BATCH, D])
        stats = sb("stats", [P, BATCH, 6])
        small = sb("small", [P, 5, BATCH])
        smalli = sb("smalli", [P, BATCH], I32)
        zeros = sb("zeros", [P, ZERO_COLS])
        ps = ctx.enter_context(nc.psum_tensor("b_ps", [P, 8, 512], F32))
        T, H, O = 0, 2, 4
        names = ("weights_in", "w1_hi", "w2_hi", "w1_lo", "w2_lo", "turned", "xhi_ready", "xlo_ready", "h_done", "h_ready", "hhi_ready",
                 "hlo_ready", "h_used", "xb_ready", "z_ready", "out_ready", "zeros_set", "dve_own")
        s = {n: sem(n) for n in names}
        x_in = [sem(f"x_in{k}") for k in range(2)]
        stored = [sem(f"stored{k}") for k in range(2)]
        block = ctx.enter_context(nc.Block())
        WEIGHTS = 16 * 5
        PAIR = STEPS // 2

        def flat(ap):
            return ap.rearrange("p k n -> p (k n)")

        @block.sync
        def _(sp):
            sp.dma_start(ids[:], ident).then_inc(s["weights_in"], 16)
            for k in range(2):
                sp.dma_start(xr[:, k], x1[k]).then_inc(x_in[k], 16)
            for dst, src in ((w1r[:], w1), (w2r[:], w2), (b1s[:], b1), (b2s[:], b2.partition_broadcast(P))):
                sp.dma_start(dst, src).then_inc(s["weights_in"], 16)

            def store(i, k):
                sp.wait_ge(s["out_ready"], i + 1)
                sp.dma_start(x2[i], out[:, k]).then_inc(stored[k], 16)

            def body(j, k):
                i = 2 * j + k
                if not is_turn(j, k, 0):
                    store(i - 1, 1 - k)
                if not (isinstance(j, int) and j == PAIR - 1):
                    sp.wait_ge(s["xb_ready"], i + 1)
                    sp.dma_start(xr[:, k], x1[i + 2]).then_inc(x_in[k], 16)

            in_pairs(sp, PAIR, body)
            store(STEPS - 1, 1)
            for k in range(2):
                sp.wait_ge(stored[k], 16 * PAIR)

        @block.gpsimd
        def _(gp):
            if xg is not None:
                gp.memset(zeros[:], 0.0).then_inc(s["zeros_set"], 1)
                gp.wait_ge(s["zeros_set"], 1)
                cleared = xg.rearrange("(n p m) d -> n p (m d)", p=P, n=ZERO_DMAS)
                for n in range(ZERO_DMAS):
                    gp.dma_start(cleared[n], zeros[:]).then_inc(zeros_done, 16)
            gp.wait_ge(s["weights_in"], WEIGHTS)
            gp.wait_ge(s["w2_hi"], 1)
            gp.tensor_tensor(flat(w2s[:, 1]), flat(w2r[:]), flat(w2s[:, 0]).bitcast(F32), ALU.subtract).then_inc(s["w2_lo"], 1)

            def body(j, k):
                i = 2 * j + k
                for m in range(MT):
                    n = MT * i + m
                    gp.wait_ge(s["hhi_ready"], n + 1)
                    wait(gp, s["h_used"], n - 3)
                    gp.tensor_tensor(hhl[:, m % 4, 1], h[:, m % 4], hhl[:, m % 4, 0].bitcast(F32), ALU.subtract).then_inc(s["hlo_ready"], 1)
                    if m == 3:
                        gp.wait_ge(s["turned"], i + 1)
                        wait(gp, s["z_ready"], i - 1)
                        gp.tensor_tensor(xb[:, k], xr[:, k], b2s[:].unsqueeze(1).to_broadcast([P, BATCH, D]), ALU.add).then_inc(s["xb_ready"], 1)

            in_pairs(gp, PAIR, body)

        @block.tensor
        def _(pe):
            def turn(i, k, rows_in):
                pe.wait_ge(x_in[k], 16 * rows_in)
                wait(pe, s["xlo_ready"], i)
                for kd in range(KD):
                    for b in range(BATCH):
                        mm = pe.transpose(ps[:, T + kd, b * P:(b + 1) * P], xr[:, k, b, kd * P:(kd + 1) * P], ids[:])
                mm.then_inc(s["turned"], 1)

            def down(i, k, m):
                n = MT * i + m
                pe.wait_ge(s["hlo_ready"], n + 1)
                pe.wait_ge(s["hhi_ready"], n + 1)
                if m == 0:
                    wait(pe, s["z_ready"], i - 1)
                for b in range(BATCH):
                    lo = (b % 2) * D
                    for q, (hp, wp) in enumerate(PARTS):
                        mm = pe.matmul(ps[:, O + 2 * k + b // 2, lo:lo + D], hhl[:, m % 4, hp, b * P:(b + 1) * P], w2s[:, wp, m, :],
                                       start=m == 0 and q == 0 and b % 2 == 0, stop=m == MT - 1 and q == 2, skip_group_check=True)
                mm.then_inc(s["h_used"], 1)

            def body(j, k):
                i = 2 * j + k
                pe.wait_ge(s["xhi_ready"], i + 1)
                pe.wait_ge(s["xlo_ready"], i + 1)
                for m in range(MT):
                    n = MT * i + m
                    wait(pe, s["h_ready"], n - 1)
                    for q in range(3 * KD):
                        kd, (wp, xp) = q // 3, PARTS[q % 3]
                        mm = pe.matmul(ps[:, H + m % 2, :], w1s[:, wp, kd, m * P:(m + 1) * P], xhl[:, k, xp, kd, :],
                                       start=q == 0, stop=q == 3 * KD - 1)
                    mm.then_inc(s["h_done"], 1)
                    if m == 4 and not is_turn(j, k, STEPS - 1):
                        turn(i + 1, 1 - k, j + k + 1)
                    if m >= 2:
                        down(i, k, m - 2)
                    elif not is_turn(j, k, 0):
                        down(i - 1, 1 - k, MT + m - 2)

            pe.wait_ge(s["weights_in"], WEIGHTS)
            turn(0, 0, 1)
            pe.wait_ge(s["w1_lo"], 1)
            pe.wait_ge(s["w2_lo"], 1)
            in_pairs(pe, PAIR, body)
            for m in range(MT - 2, MT):
                down(STEPS - 1, 1, m)

        @block.scalar
        def _(act):
            act.wait_ge(s["weights_in"], WEIGHTS)
            act.activation(flat(w2s[:, 0]), flat(w2r[:]), ACT.Copy).then_inc(s["w2_hi"], 1)

            def body(j, k):
                i = 2 * j + k
                for m in range(MT):
                    n = MT * i + m
                    act.wait_ge(s["h_done"], n + 1)
                    wait(act, s["hlo_ready"], n - 3)
                    wait(act, s["hhi_ready"], n - 3)
                    act.activation(h[:, m % 4], ps[:, H + m % 2, :], ACT.Gelu, bias=b1s[:, m:m + 1]).then_inc(s["h_ready"], 1)
                    act.wait_ge(s["h_ready"], n + 1)
                    wait(act, s["h_used"], n - 3)
                    act.activation(hhl[:, m % 4, 0], h[:, m % 4], ACT.Copy).then_inc(s["hhi_ready"], 1)

            in_pairs(act, PAIR, body)

        @block.vector
        def _(ve):
            ch = Chain(ve, s["dve_own"], LN_LINKS + 1)

            def split_x(i, k):
                ve.wait_ge(s["turned"], i + 1)
                wait(ve, s["h_done"], MT * (i - 1))
                ve.tensor_copy(xhl[:, k, 0], ps[:, T:T + KD, :]).then_inc(s["xhi_ready"], 1)
                ve.wait_ge(s["xhi_ready"], i + 1)
                ve.tensor_tensor(xhl[:, k, 1], ps[:, T:T + KD, :], xhl[:, k, 0].bitcast(F32), ALU.subtract).then_inc(s["xlo_ready"], 1)

            def normalise(i, k, before):
                ch.turn(i)
                ve.wait_ge(s["xb_ready"], i + 1)
                wait(ve, s["out_ready"], i)
                ve.wait_ge(s["h_used"], MT * (i + 1))
                for half in range(2):
                    bb = slice(2 * half, 2 * half + 2)
                    last = ve.tensor_tensor(z[:, bb], ps[:, O + 2 * k + half, :].rearrange("p (b d) -> p b d", b=2), xb[:, k, bb], ALU.add)
                    if half == 0:
                        ch.mark(last)
                last.then_inc(s["z_ready"], 1)
                ve.wait_ge(s["z_ready"], i + 1)
                wait(ve, stored[k], 16 * before)
                layernorm(ch, z, out[:, k], stats, small, smalli, BATCH).then_inc(s["out_ready"], 1)
                ch.end()

            def body(j, k):
                i = 2 * j + k
                if not is_turn(j, k, 0):
                    normalise(i - 1, 1 - k, j + k - 1)
                if not is_turn(j, k, STEPS - 1):
                    split_x(i + 1, 1 - k)

            ve.wait_ge(s["weights_in"], WEIGHTS)
            ve.tensor_copy(flat(w1s[:, 0]), flat(w1r[:])).then_inc(s["w1_hi"], 1)
            split_x(0, 0)
            ve.wait_ge(s["w1_hi"], 1)
            ve.tensor_tensor(flat(w1s[:, 1]), flat(w1r[:]), flat(w1s[:, 0]).bitcast(F32), ALU.subtract).then_inc(s["w1_lo"], 1)
            in_pairs(ve, PAIR, body)
            normalise(STEPS - 1, 1, PAIR - 1)


def phase_attention(nc, x2, wqkv, bqkv, wout, bout, omega, nodes, weights, masks, ident, x3):
    with ExitStack() as ctx:
        def sb(name, shape, dt=F32):
            return ctx.enter_context(nc.sbuf_tensor("c_" + name, shape, dt))

        def sem(name):
            return ctx.enter_context(nc.semaphore("c_" + name))

        raw = sb("raw", [P, KD * 3 * D])
        wq = sb("wqkv", [P, 2, KD, 3 * D], F32R)
        wo = sb("wout", [P, 2, KD, D], F32R)
        om = sb("omega", [P, 2, PAIRS, P], F32R)
        bq = sb("bqkv", [P, 3 * D])
        bo = sb("bout", [P, D])
        ids = sb("ident", [P, P])
        tri = sb("tri", [P, P])
        nw = sb("nw", [P, 2])
        fc = sb("fc", [P, 4])
        ns = sb("ns", [P, 4, P])
        nsi = sb("nsi", [P, P], I32)
        xr = sb("xr", [P, BATCH, D])
        xb = sb("xb", [P, BATCH, D])
        xts = sb("xts", [P, 2, KD, TOK], F32R)
        qk = sb("qk", [P, BATCH, 2 * D])
        sq = sb("sq", [P, BATCH, 2 * D])
        va = sb("va", [P, BATCH, HEADS1, VP])
        nrm = sb("nrm", [P, 3, BATCH * 2 * HEADS1])
        nrmi = sb("nrmi", [P, BATCH * 2 * HEADS1], I32)
        qkt = sb("qkt", [P, 2, 2 * KD, TOK], F32R)
        cf = sb("cf", [P, 2, 2, TOK])
        ef = sb("ef", [P, TOK])
        qf = sb("qf", [P, 3, TOK])
        kf = sb("kf", [P, 3, TOK])
        kr = sb("kr", [P, 2, BATCH, P])
        sm = sb("sm", [P, 2, 2, BATCH, P])
        state = sb("state", [P, PAIRS, BATCH, 2, VP])
        ot = sb("ot", [P, PAIRS // 2, TOK])
        den = sb("den", [P, 2, BATCH, 4])
        cr = sb("cr", [P, BATCH, HEADS1, HD])
        ctxt = sb("ctxt", [P, 2, KD, TOK], F32R)
        z = sb("z", [P, BATCH, D])
        out = sb("out", [P, BATCH, D])
        stats = sb("stats", [P, BATCH, 6])
        small = sb("small", [P, 5, BATCH])
        smalli = sb("smalli", [P, BATCH], I32)
        ps = ctx.enter_context(nc.psum_tensor("c_ps", [P, 8, 512], F32))
        names = ("weights_in", "raw_hi", "raw_lo", "scaled", "fc_ready", "x_in", "res_in", "x_done", "x_hi", "x_free", "sq_ready",
                 "rnorm_ready", "qn_ready", "feat_done", "clip_done", "exp_done", "qf_ready", "score_done", "mask_done",
                 "kt_done", "kr_ready", "pair_done", "state_new", "ot_ready", "xb_ready", "z_ready", "out_ready", "stored",
                 "own", "act_own", "raw_in")
        s = {n: sem(n) for n in names}
        block = ctx.enter_context(nc.Block())
        HIGH, LOW, BIAS, AMP = (slice(n, n + 1) for n in range(4))
        FB, SC, KT, OB, SU, X = 0, 2, 4, 5, 6, 7
        LAST = STEPS - 1
        FRONT = {2: (("FT", 0), ("FT", 1)), 3: (("FQ", 0), ("FQ", 1)), 4: (("FQ", 2), ("FQ", 3)), 7: (("FN", 0), ("FN", 2)),
                 8: (("FN", 1), ("FN", 3)), 9: (("FV", 0), ("FV", 1))}
        BACK = {0: (("BO", 0), ("BO", 1)), 1: (("BO", 2), ("BO", 3)), 5: (("BC", 0), ("BC", 1)), 6: (("BW", 0), ("BW", 1))}
        NF, NB_ = 12, 8
        HI = ("FT", "FN", "BC")
        HF, HB = 6, 2

        def steps(i, front, back):
            if i is None:
                n, h = 0, 0
            elif isinstance(i, int) and i == 0:
                n, h = NF, HF
            else:
                n, h = (NF + NB_) * i + NF - NB_, (HF + HB) * i + HF - HB
            if isinstance(i, int) and i == LAST + 1:
                n, h = (NF + NB_) * LAST + NF - NB_ + NB_, (HF + HB) * LAST + HF - HB + HB
            found = []
            for t in range(PAIRS + 2):
                for name, a in (FRONT.get(t, ()) if front else ()) + (BACK.get(t, ()) if back else ()):
                    found.append((t, name, a, n, h))
                    n = n + 1
                    h = h + (name in HI)
            return found

        def everything(eng, body):
            body(None, True, False)
            body(0, True, False)
            with eng.Fori(1, LAST) as i:
                body(i, True, True)
            body(LAST, False, True)
            body(LAST + 1, False, True)

        def wait(eng, name, value):
            if not isinstance(value, int) or value > 0:
                eng.wait_ge(s[name], value)

        def turned_before(i, name, a):
            return next(n + 1 for _, m, b, n, _ in steps(i, True, not (i is None or (isinstance(i, int) and i == 0))) if (m, b) == (name, a))

        @block.sync
        def _(sp):
            prime(sp, [s[n] for n in ("out_ready", "stored")])
            sp.dma_start(raw[:], wqkv.rearrange("p k n -> p (k n)")).then_inc(s["raw_in"], 16)
            for dst, src in ((bq[:], bqkv.partition_broadcast(P)), (bo[:], bout.partition_broadcast(P)),
                             (ids[:], ident), (tri[:], masks[0]), (nw[:, 0:1], nodes), (nw[:, 1:2], weights),
                             (ns[:, 0], nodes.rearrange("p o -> (p o)").partition_broadcast(P))):
                sp.dma_start(dst, src).then_inc(s["weights_in"], 16)
            sp.dma_start(xr[:], x2[0]).then_inc(s["x_in"], 16)
            sp.wait_ge(s["raw_lo"], 1)
            sp.dma_start(raw[:, 0:KD * D], wout.rearrange("p k n -> p (k n)")).then_inc(s["raw_in"], 16)
            sp.wait_ge(s["raw_lo"], 2)
            sp.dma_start(raw[:, 0:PAIRS * P], omega.rearrange("p k n -> p (k n)")).then_inc(s["raw_in"], 16)
            sp.dma_start(xb[:], x2[0]).then_inc(s["res_in"], 16)

            def next_x(i, n):
                sp.wait_ge(s["x_done"], turned_before(i, "FT", 1))
                sp.dma_start(xr[:], x2[n]).then_inc(s["x_in"], 16)

            def next_residual(i):
                sp.wait_ge(s["z_ready"], i)
                sp.dma_start(xb[:], x2[i]).then_inc(s["res_in"], 16)

            def store(i):
                sp.wait_ge(s["out_ready"], PRIMED + i)
                sp.dma_start(x3[i - 1], out[:]).then_inc(s["stored"], 16)

            next_x(None, 1)
            next_x(0, 2)
            with sp.Fori(1, LAST - 1) as i:
                next_x(i, i + 2)
                next_residual(i)
                store(i)
            next_residual(LAST - 1)
            store(LAST - 1)
            next_residual(LAST)
            store(LAST)
            store(LAST + 1)
            sp.wait_ge(s["stored"], PRIMED + 16 * STEPS)

        @block.gpsimd
        def _(gp):
            def body(i, front, back):
                if front:
                    f = 0 if i is None else i + 1
                    gp.wait_ge(s["x_free"], turned_before(i, "FQ", 3))
                    gp.tensor_tensor(sq[:], qk[:], qk[:], ALU.mult).then_inc(s["sq_ready"], 1)
                    gp.wait_ge(s["rnorm_ready"], f + 1)
                    gp.tensor_tensor(sq[:].rearrange("p b (n d) -> p (b n) d", d=HD), qk[:].rearrange("p b (n d) -> p (b n) d", d=HD),
                                     nrm[:, 1, :].unsqueeze(2).to_broadcast([P, BATCH * 2 * HEADS1, HD]), ALU.mult).then_inc(s["qn_ready"], 1)
                if i is not None and not (isinstance(i, int) and i > LAST):
                    gp.wait_ge(s["res_in"], 16 * (i + 1))
                    gp.tensor_tensor(xb[:], xb[:], bo[:].unsqueeze(1).to_broadcast([P, BATCH, D]), ALU.add).then_inc(s["xb_ready"], 1)

            gp.wait_ge(s["weights_in"], 16 * 7)
            everything(gp, body)

        @block.tensor
        def _(pe):
            def split3(out_ap, lhs, rhs, kds, first=True, last=True):
                for kd in range(kds):
                    for q, (lp, rp) in enumerate(PARTS):
                        mm = pe.matmul(out_ap, lhs(lp, kd), rhs(rp, kd), start=kd == 0 and q == 0, stop=kd == kds - 1 and q == 2)
                return mm

            def x_step(i, name, a, n):
                wait(pe, "x_free", n)
                front_of = 0 if i is None else i + 1
                if name == "FT":
                    if a == 0:
                        pe.wait_ge(s["x_in"], 16 * (front_of + 1))
                    for b in range(BATCH):
                        mm = pe.transpose(ps[:, X, b * P:(b + 1) * P], xr[:, b, a * P:(a + 1) * P], ids[:])
                elif name == "FQ":
                    mm = split3(ps[:, X, :], lambda p, kd: xts[:, p, kd, a * P:(a + 1) * P], lambda p, kd: wq[:, p, kd, 0:2 * D], KD)
                elif name == "FV":
                    for h in range(2):
                        b = 2 * a + h
                        mm = split3(ps[:, X, h * D:(h + 1) * D], lambda p, kd: xts[:, p, kd, b * P:(b + 1) * P],
                                    lambda p, kd: wq[:, p, kd, 2 * D:3 * D], KD)
                elif name == "FN":
                    pe.wait_ge(s["qn_ready"], front_of + 1)
                    for b in range(BATCH):
                        mm = pe.transpose(ps[:, X, b * P:(b + 1) * P], sq[:, b, a * P:(a + 1) * P], ids[:])
                elif name == "BO":
                    pe.wait_ge(s["ot_ready"], 4 * (i - 1) + a + 1)
                    for b in range(BATCH):
                        mm = pe.transpose(ps[:, X, b * P:(b + 1) * P], ot[:, a, b * P:(b + 1) * P], ids[:])
                elif name == "BC":
                    for b in range(BATCH):
                        mm = pe.transpose(ps[:, X, b * P:(b + 1) * P], cr[:, b, 8 * a:8 * (a + 1), :], ids[:])
                else:
                    for h in range(2):
                        b = 2 * a + h
                        mm = split3(ps[:, X, h * D:(h + 1) * D], lambda p, kd: ctxt[:, p, kd, b * P:(b + 1) * P],
                                    lambda p, kd: wo[:, p, kd, :], KD)
                mm.then_inc(s["x_done"], 1)

            def body(i, front, back):
                pairs = i is not None and not (isinstance(i, int) and i > LAST)
                for t in range(PAIRS + 2):
                    xs = [x for x in steps(i, front, back) if x[0] == t]
                    if pairs and t < PAIRS:
                        for q in range(2):
                            n = 2 * t + q
                            wait(pe, "clip_done", 2 * PAIRS * i + n - 1 if n >= 2 else 2 * PAIRS * i)
                            mm = split3(ps[:, FB + q, :], lambda p, kd: om[:, p, t, :], lambda p, kd: qkt[:, p, KD * q + t // 4, :], 1)
                            mm.then_inc(s["feat_done"], 1)
                    for _, name, a, n, _ in xs[0:1]:
                        x_step(i, name, a, n)
                    if pairs and 1 <= t <= PAIRS:
                        u = t - 1
                        pe.wait_ge(s["exp_done"], 2 * (PAIRS * i + u + 1))
                        pe.wait_ge(s["qf_ready"], PAIRS * i + u + 1)
                        wait(pe, "mask_done", PAIRS * i + u)
                        for b in range(BATCH):
                            for h in range(2):
                                cols, f = slice(b * P, (b + 1) * P), slice(FD * h, FD * (h + 1))
                                mm = pe.matmul(ps[:, SC + h, cols], kf[f, u % 3, cols], qf[f, u % 3, cols], start=True, stop=True)
                        mm.then_inc(s["score_done"], 1)
                        wait(pe, "kr_ready", PAIRS * i + u)
                        for b in range(BATCH):
                            mm = pe.transpose(ps[:, KT, b * P:(b + 1) * P], kf[:, u % 3, b * P:(b + 1) * P], ids[:])
                        mm.then_inc(s["kt_done"], 1)
                    for _, name, a, n, _ in xs[1:2]:
                        if name != "FV":
                            x_step(i, name, a, n)
                    if pairs and t >= 2:
                        u = t - 2
                        pe.wait_ge(s["mask_done"], PAIRS * i + u + 1)
                        pe.wait_ge(s["kr_ready"], PAIRS * i + u + 1)
                        if u % 2 == 0:
                            wait(pe, "ot_ready", PAIRS // 2 * i + u // 2)
                        wait(pe, "state_new", PAIRS * i + u)
                        at = 2 * FD // 2 * (u % 2)
                        for b in range(BATCH):
                            pe.matmul(ps[at:at + 2 * VP, OB, b * P:(b + 1) * P], state[:, u, b].rearrange("p h w -> p (h w)"),
                                      qf[:, u % 3, b * P:(b + 1) * P], start=b == 0, stop=False, skip_group_check=True)
                        for b in range(BATCH):
                            for h in range(2):
                                pe.matmul(ps[at + h * VP:at + (h + 1) * VP, OB, b * P:(b + 1) * P], va[:, b, 2 * u + h, :],
                                          sm[:, u % 2, h, b, :], start=False, stop=True, skip_group_check=True)
                        for b in range(BATCH):
                            mm = pe.matmul(ps[:, SU, b * 2 * VP:(b + 1) * 2 * VP], kr[:, u % 2, b, :],
                                           va[:, b, 2 * u:2 * u + 2, :].rearrange("p h w -> p (h w)"), start=True, stop=True)
                        mm.then_inc(s["pair_done"], 1)
                    for _, name, a, n, _ in xs[1:2]:
                        if name == "FV":
                            x_step(i, name, a, n)

            pe.wait_ge(s["weights_in"], 16 * 7)
            pe.wait_ge(s["raw_lo"], 3)
            pe.wait_ge(s["fc_ready"], 1)
            everything(pe, body)

        @block.scalar
        def _(act):
            def high(dst, n):
                act.activation(dst, raw[:, 0:n], ACT.Copy).then_inc(s["raw_hi"], 1)

            act.wait_ge(s["raw_in"], 16)
            high(wq[:, 0].rearrange("p k n -> p (k n)"), KD * 3 * D)
            act.wait_ge(s["raw_in"], 32)
            high(wo[:, 0].rearrange("p k n -> p (k n)"), KD * D)
            act.wait_ge(s["scaled"], 1)
            high(om[:, 0].rearrange("p k n -> p (k n)"), PAIRS * P)
            act.wait_ge(s["fc_ready"], 1)

            def x_high(i, name, a, n):
                act.wait_ge(s["x_done"], n + 1)
                dst = {"FT": xts, "FN": qkt, "BC": ctxt}[name][:, 0, a, :]
                act.activation(dst, ps[:, X, :], ACT.Copy).then_inc(s["x_hi"], 1)

            def body(i, front, back):
                pairs = i is not None and not (isinstance(i, int) and i > LAST)
                for t in range(PAIRS + 2):
                    xs = [x for x in steps(i, front, back) if x[0] == t and x[1] in HI]
                    if pairs and t < PAIRS:
                        act.wait_ge(s["clip_done"], 2 * PAIRS * i + 2 * t + 1)
                        wait(act, "qf_ready", PAIRS * i + t)
                        act.activation(ef[:], cf[:, t % 2, 0], ACT.Exp, bias=fc[:, BIAS]).then_inc(s["exp_done"], 1)
                        wait(act, "pair_done", PAIRS * i + (t - 2 if t > 2 else 0))
                        act.wait_ge(s["clip_done"], 2 * PAIRS * i + 2 * t + 2)
                        act.activation(kf[:, t % 3, :], cf[:, t % 2, 1], ACT.Exp, bias=fc[:, BIAS]).then_inc(s["exp_done"], 1)
                        act.wait_ge(s["exp_done"], 2 * PAIRS * i + 2 * t + 1)
                        act.activation(qf[:, t % 3, :], ef[:], ACT.Copy, scale=fc[:, AMP]).then_inc(s["qf_ready"], 1)
                    for _, name, a, n, _ in xs[0:1]:
                        x_high(i, name, a, n)
                    if pairs and 1 <= t <= PAIRS:
                        u = t - 1
                        act.wait_ge(s["kt_done"], PAIRS * i + u + 1)
                        wait(act, "pair_done", PAIRS * i + (u - 1 if u > 1 else 0))
                        act.activation(kr[:, u % 2].rearrange("p b f -> p (b f)"), ps[:, KT, :], ACT.Copy).then_inc(s["kr_ready"], 1)
                    for _, name, a, n, _ in xs[1:2]:
                        x_high(i, name, a, n)
                    if pairs and t >= 3 and t % 2 == 1:
                        g = (t - 3) // 2
                        act.wait_ge(s["pair_done"], PAIRS * i + 2 * g + 2)
                        act.activation(ot[:, g], ps[:, OB, :], ACT.Copy).then_inc(s["ot_ready"], 1)

            everything(act, body)

        @block.vector
        def _(ve):
            pre = Chain(ve, s["own"], 0)
            pre.mark(ve.memset(state[:], 0.0))
            pre.link(ve.memset(va[:], 0.0))
            pre.mark(ve.memset(va[:, :, :, HD:HD + 1], 1.0))
            ve.wait_ge(s["weights_in"], 16 * 7)
            pre.link(ve.tensor_scalar(ns[:, 1], ns[:, 0], 0.0, 2.0, ALU.max, ALU.mult))
            rsqrt(pre, ns[:, 1], ns[:, 2], ns[:, 3], nsi[:])
            pre.link(ve.tensor_tensor(ns[:, 1], ns[:, 1], ns[:, 2], ALU.mult))
            pre.mark(ve.tensor_scalar(fc[:, HIGH], nw[:, 0:1], 20.0, None, ALU.add))
            pre.mark(ve.tensor_scalar(fc[:, LOW], nw[:, 0:1], -20.0, None, ALU.add))
            pre.link(ve.tensor_scalar(fc[:, BIAS], nw[:, 0:1], -1.0, None, ALU.mult))
            ve.tensor_scalar(fc[:, AMP], nw[:, 1:2], 0.0, 1.0 / MF, ALU.max, ALU.mult).then_inc(s["fc_ready"], 1)

            def low(dst, hi, n):
                ve.tensor_tensor(dst, raw[:, 0:n], hi.bitcast(F32), ALU.subtract).then_inc(s["raw_lo"], 1)

            ve.wait_ge(s["raw_hi"], 1)
            low(wq[:, 1].rearrange("p k n -> p (k n)"), wq[:, 0].rearrange("p k n -> p (k n)"), KD * 3 * D)
            ve.wait_ge(s["raw_hi"], 2)
            low(wo[:, 1].rearrange("p k n -> p (k n)"), wo[:, 0].rearrange("p k n -> p (k n)"), KD * D)
            ve.wait_ge(s["raw_in"], 48)
            scaled = raw[:, 0:PAIRS * P].rearrange("p (k n) -> p k n", k=PAIRS)
            ve.tensor_tensor(scaled, scaled, ns[:, 1].unsqueeze(1).to_broadcast([P, PAIRS, P]), ALU.mult).then_inc(s["scaled"], 1)
            ve.wait_ge(s["raw_hi"], 3)
            low(om[:, 1].rearrange("p k n -> p (k n)"), om[:, 0].rearrange("p k n -> p (k n)"), PAIRS * P)

            FRONT_OWN = 2 + RSQRT_LINKS - 1
            PAIR_OWN = 2 * PAIRS
            BACK_OWN = 2 * 4 + LN_LINKS

            def x_evac(i, ch, name, a, n, h):
                if name in HI:
                    dst = {"FT": xts, "FN": qkt, "BC": ctxt}[name]
                    ve.wait_ge(s["x_hi"], h + 1)
                    ins = ve.tensor_tensor(dst[:, 1, a, :], ps[:, X, :], dst[:, 0, a, :].bitcast(F32), ALU.subtract)
                else:
                    ve.wait_ge(s["x_done"], n + 1)
                    if name == "FQ":
                        if a == 0 and i is not None:
                            ve.wait_ge(s["qn_ready"], i + 1)
                        ins = ve.tensor_tensor(qk[:, a, :], ps[:, X, :], bq[:, 0:2 * D], ALU.add)
                    elif name == "FV":
                        if i is not None:
                            ve.wait_ge(s["pair_done"], PAIRS * (i + 1))
                        v_bias = bq[:, 2 * D:].rearrange("p (h d) -> p h d", h=HEADS1).unsqueeze(1).to_broadcast([P, 2, HEADS1, HD])
                        ins = ve.tensor_tensor(va[:, 2 * a:2 * a + 2, :, 0:HD], ps[:, X, :].rearrange("p (b h d) -> p b h d", b=2, h=HEADS1),
                                               v_bias, ALU.add)
                    elif name == "BO":
                        got = ps[:, X, :].rearrange("p (b j w) -> p b j w", b=BATCH, j=4)
                        ch.link(ve.tensor_scalar(den[:, 0], got[:, :, :, HD], 1e-6, None, ALU.max))
                        ch.link(ve.reciprocal(den[:, 1], den[:, 0]))
                        ins = ve.tensor_tensor(cr[:, :, 4 * a:4 * a + 4, :], got[:, :, :, 0:HD],
                                               den[:, 1].unsqueeze(3).to_broadcast([P, BATCH, 4, HD]), ALU.mult)
                    else:
                        if a == 0:
                            ve.wait_ge(s["xb_ready"], i)
                            wait(ve, "out_ready", PRIMED + i - 1)
                        ins = ve.tensor_tensor(z[:, 2 * a:2 * a + 2].rearrange("p b d -> p (b d)"), ps[:, X, :],
                                               xb[:, 2 * a:2 * a + 2].rearrange("p b d -> p (b d)"), ALU.add)
                ins.then_inc(s["x_free"], 1)
                if (name, a) == ("BW", 1):
                    ve.wait_ge(s["x_free"], n + 1)
                    ve.nop().then_inc(s["z_ready"], 1)

            def body(i, front, back):
                ch = Chain(ve, s["own"], 0)
                if i is None:
                    ch.n = pre.n
                elif isinstance(i, int) and i == 0:
                    ch.n = pre.n + FRONT_OWN
                else:
                    whole = FRONT_OWN + PAIR_OWN + BACK_OWN
                    ch.base = (i * whole + (pre.n + FRONT_OWN - BACK_OWN)) if not (isinstance(i, int) and i == LAST + 1) else (
                        LAST * whole + pre.n + FRONT_OWN - BACK_OWN + PAIR_OWN + BACK_OWN)
                n0 = ch.n
                pairs = i is not None and not (isinstance(i, int) and i > LAST)
                for t in range(PAIRS + 2):
                    xs = [x for x in steps(i, front, back) if x[0] == t]
                    if pairs and t < PAIRS:
                        for q in range(2):
                            n = 2 * t + q
                            ve.wait_ge(s["feat_done"], 2 * PAIRS * i + n + 1)
                            wait(ve, "exp_done", 2 * PAIRS * i + (n - 3 if n > 3 else 0))
                            ve.tensor_scalar(cf[:, t % 2, q], ps[:, FB + q, :], fc[:, HIGH], fc[:, LOW], ALU.min, ALU.max).then_inc(s["clip_done"], 1)
                    for _, name, a, n, h in xs[0:1]:
                        x_evac(i, ch, name, a, n, h)
                    if pairs and 1 <= t <= PAIRS:
                        u = t - 1
                        ve.wait_ge(s["score_done"], PAIRS * i + u + 1)
                        wait(ve, "pair_done", PAIRS * i + (u - 1 if u > 1 else 0))
                        for h in range(2):
                            ins = ve.tensor_tensor(sm[:, u % 2, h], ps[:, SC + h, :].rearrange("p (b t) -> p b t", t=P),
                                                   tri[:].unsqueeze(1).to_broadcast([P, BATCH, P]), ALU.mult)
                            if h == 0:
                                ch.mark(ins)
                        ins.then_inc(s["mask_done"], 1)
                    for _, name, a, n, h in xs[1:2]:
                        if name != "FV":
                            x_evac(i, ch, name, a, n, h)
                    if pairs and t >= 2:
                        u = t - 2
                        ve.wait_ge(s["pair_done"], PAIRS * i + u + 1)
                        su = ps[:, SU, 0:BATCH * 2 * VP].rearrange("p (b h w) -> p b h w", b=BATCH, h=2)
                        for h in range(2):
                            f = slice(FD * h, FD * (h + 1))
                            ins = ve.tensor_tensor(state[f, u, :, h, :], su[f, :, h, :], state[f, u, :, h, :], ALU.add)
                            if h == 0:
                                ch.mark(ins)
                        ins.then_inc(s["state_new"], 1)
                    for _, name, a, n, h in xs[1:2]:
                        if name == "FV":
                            x_evac(i, ch, name, a, n, h)
                    if front and t == 5:
                        nv, nr, nt = nrm[:, 0, :], nrm[:, 1, :], nrm[:, 2, :]
                        ve.wait_ge(s["sq_ready"], (0 if i is None else i + 1) + 1)
                        ch.link(ve.tensor_reduce(nv, sq[:].rearrange("p b (n d) -> p (b n) d", d=HD), AX.X, ALU.add))
                        ch.link(ve.tensor_scalar(nv, nv, 1e-24, None, ALU.max))
                        rsqrt(ch, nv, nr, nt, nrmi[:], s["rnorm_ready"])
                    if back and t == 7:
                        wait(ve, "stored", PRIMED + 16 * (i - 1))
                        layernorm(ch, z, out, stats, small, smalli, BATCH).then_inc(s["out_ready"], 1)
                assert ch.n - n0 == front * FRONT_OWN + pairs * PAIR_OWN + back * BACK_OWN, (ch.n - n0, front, pairs, back)

            everything(ve, body)


def phase_shared(nc, x3, sw, rw, rb, ident, xs, routed_w, wall, logits, wall_in):
    with ExitStack() as ctx:
        def sb(name, shape, dt=F32):
            return ctx.enter_context(nc.sbuf_tensor("d_" + name, shape, dt))

        def sem(name):
            return ctx.enter_context(nc.semaphore("d_" + name))

        raw = sb("raw", [P, 2, 1024])
        whl = sb("whl", [P, 2, SHARED, WCOLS], F32R)
        rws = sb("rw", [P, KD, EXPERTS])
        rbs = sb("rb", [P, EXPERTS])
        ids = sb("ident", [P, P])
        xr = sb("xr", [P, 2, BATCH, D])
        xtf = sb("xtf", [P, KD, TOK])
        xhl = sb("xhl", [P, 2, KD, TOK], F32R)
        act_h = sb("act_h", [P, 2, TOK])
        g = sb("g", [P, 2, TOK])
        ghl = sb("ghl", [P, 2, 2, TOK], F32R)
        z = sb("z", [P, 2, BATCH, D])
        ps = ctx.enter_context(nc.psum_tensor("d_ps", [P, 8, 512], F32))
        names = ("consts_in", "raw_hi", "raw_lo", "turned", "xtf_ready", "xhi_ready", "xlo_ready", "h_done", "silu_done",
                 "g_ready", "ghi_ready", "glo_ready", "g_used", "logits_done", "logits_read", "z_ready", "own")
        raw_in = [sem(f"raw_in{k}") for k in range(2)]
        s = {n: sem(n) for n in names}
        x_in = [sem(f"x_in{k}") for k in range(2)]
        stored = [sem(f"stored{k}") for k in range(2)]
        block = ctx.enter_context(nc.Block())
        NCH = SHARED * WCOLS // 1024
        NM = SHARED * HM
        T, H, O = 0, 2, 6
        swf = sw.rearrange("p e n -> p (e n)")
        whlf = whl[:].rearrange("p t e n -> p t (e n)")

        @block.sync
        def _(sp):
            prime(sp, [s[n] for n in ("g_ready", "g_used", "ghi_ready", "logits_done", "logits_read", "xhi_ready", "xtf_ready", "z_ready")] + stored)
            for dst, src in ((rws[:], rw), (ids[:], ident), (rbs[:], rb.partition_broadcast(P))):
                sp.dma_start(dst, src).then_inc(s["consts_in"], 16)
            for n in range(NCH):
                if n >= 2:
                    sp.wait_ge(s["raw_lo"], n - 1)
                sp.dma_start(raw[:, n % 2], swf[:, n * 1024:(n + 1) * 1024]).then_inc(raw_in[n % 2], 16)
                if n < 2:
                    sp.dma_start(xr[:, n], x3[n]).then_inc(x_in[n], 16)
            for e in range(EXPERTS):
                sp.dma_start(wall[:, e], routed_w[:, e]).then_inc(wall_in, 16)
            with sp.Fori(0, STEPS // 2 - 1) as j:
                for k in range(2):
                    sp.wait_ge(s["z_ready"], PRIMED + 2 * j + k + 1)
                    sp.dma_start(xs[2 * j + k], z[:, k]).then_inc(stored[k], 16)
                    sp.dma_start(xr[:, k], x3[2 * j + k + 2]).then_inc(x_in[k], 16)
            for k in range(2):
                sp.wait_ge(s["z_ready"], PRIMED + STEPS - 1 + k)
                sp.dma_start(xs[STEPS - 2 + k], z[:, k]).then_inc(stored[k], 16)
            for k in range(2):
                sp.wait_ge(stored[k], PRIMED + 16 * (STEPS // 2))

        @block.gpsimd
        def _(gp):
            for n in range(NCH):
                gp.wait_ge(s["raw_hi"], n + 1)
                cols = slice(n * 1024, (n + 1) * 1024)
                gp.tensor_tensor(whlf[:, 1, cols], raw[:, n % 2], whlf[:, 0, cols].bitcast(F32), ALU.subtract).then_inc(s["raw_lo"], 1)

        @block.tensor
        def _(pe):
            pe.wait_ge(s["consts_in"], 48)
            pe.wait_ge(s["raw_lo"], NCH)
            with pe.Fori(0, STEPS // 2) as j:
                for k in range(2):
                    i = 2 * j + k
                    pe.wait_ge(x_in[k], 16 * (j + 1))
                    pe.wait_ge(s["xtf_ready"], PRIMED + i)
                    pe.wait_ge(s["logits_read"], PRIMED + i)
                    for kd in range(KD):
                        for b in range(BATCH):
                            mm = pe.transpose(ps[:, T + kd, b * P:(b + 1) * P], xr[:, k, b, kd * P:(kd + 1) * P], ids[:])
                    mm.then_inc(s["turned"], 1)

                    def down(n):
                        pe.wait_ge(s["ghi_ready"], PRIMED + NM * i + n + 1)
                        pe.wait_ge(s["glo_ready"], NM * i + n + 1)
                        for b in range(BATCH):
                            for q, (gp_, wp_) in enumerate(PARTS):
                                lo = W2AT + (n % HM) * D
                                mm = pe.matmul(ps[:, O + b // 2, (b % 2) * D:(b % 2 + 1) * D], ghl[:, n % 2, gp_, b * P:(b + 1) * P],
                                               whl[:, wp_, n // HM, lo:lo + D],
                                               start=n == 0 and q == 0 and b % 2 == 0, stop=n == NM - 1 and q == 2, skip_group_check=True)
                        mm.then_inc(s["g_used"], 1)

                    pe.wait_ge(s["xhi_ready"], PRIMED + i + 1)
                    pe.wait_ge(s["xlo_ready"], i + 1)
                    for n in range(NM):
                        e, m = n // HM, n % HM
                        pe.wait_ge(s["g_ready"], PRIMED + NM * i + max(n - 1, 0))
                        for w, at in enumerate((W1AT, W3AT)):
                            for q in range(3 * KD):
                                kd, (xp, wp) = q // 3, PARTS[q % 3]
                                lo = at + kd * HID + m * P
                                mm = pe.matmul(ps[:, H + 2 * (n % 2) + w, :], whl[:, wp, e, lo:lo + P], xhl[:, xp, kd, :],
                                               start=q == 0, stop=q == 3 * KD - 1)
                            mm.then_inc(s["h_done"], 1)
                        if n == 0:
                            pe.wait_ge(s["z_ready"], PRIMED + i)
                            pe.wait_ge(s["xtf_ready"], PRIMED + i + 1)
                            for b in range(BATCH):
                                for kd in range(KD):
                                    mm = pe.matmul(ps[:, T, b * EXPERTS:(b + 1) * EXPERTS], xtf[:, kd, b * P:(b + 1) * P], rws[:, kd, :],
                                                   start=kd == 0, stop=kd == KD - 1)
                            mm.then_inc(s["logits_done"], 1)
                        if n:
                            down(n - 1)
                    down(NM - 1)

        @block.scalar
        def _(act):
            for n in range(NCH):
                act.wait_ge(raw_in[n % 2], 16 * (n // 2 + 1))
                act.activation(whlf[:, 0, n * 1024:(n + 1) * 1024], raw[:, n % 2], ACT.Copy).then_inc(s["raw_hi"], 1)
            with act.Fori(0, STEPS // 2) as j:
                for k in range(2):
                    i = 2 * j + k
                    act.wait_ge(s["xtf_ready"], PRIMED + i + 1)
                    act.wait_ge(s["g_used"], PRIMED + NM * i)
                    act.activation(xhl[:, 0].rearrange("p k n -> p (k n)"), xtf[:].rearrange("p k n -> p (k n)"), ACT.Copy).then_inc(s["xhi_ready"], 1)
                    for n in range(NM):
                        act.wait_ge(s["h_done"], 2 * (NM * i + n) + 1)
                        act.wait_ge(s["g_ready"], PRIMED + NM * i + max(n - 1, 0))
                        act.activation(act_h[:, n % 2], ps[:, H + 2 * (n % 2), :], ACT.Silu).then_inc(s["silu_done"], 1)
                        act.wait_ge(s["g_ready"], PRIMED + NM * i + n + 1)
                        act.wait_ge(s["g_used"], PRIMED + NM * i + max(n - 1, 0))
                        act.activation(ghl[:, n % 2, 0], g[:, n % 2], ACT.Copy).then_inc(s["ghi_ready"], 1)

        @block.vector
        def _(ve):
            ch = Chain(ve, s["own"], 1)
            ve.wait_ge(s["consts_in"], 48)
            with ve.Fori(0, STEPS // 2) as j:
                for k in range(2):
                    i = 2 * j + k
                    ch.turn(i)
                    ve.wait_ge(s["turned"], i + 1)
                    ve.wait_ge(s["xhi_ready"], PRIMED + i)
                    ve.wait_ge(s["logits_done"], PRIMED + i)
                    ve.tensor_copy(xtf[:], ps[:, T:T + KD, :]).then_inc(s["xtf_ready"], 1)
                    ve.wait_ge(s["xhi_ready"], PRIMED + i + 1)
                    ve.wait_ge(s["xtf_ready"], PRIMED + i + 1)
                    ve.tensor_tensor(xhl[:, 1], xtf[:], xhl[:, 0].bitcast(F32), ALU.subtract).then_inc(s["xlo_ready"], 1)
                    for n in range(NM):
                        ve.wait_ge(s["silu_done"], NM * i + n + 1)
                        ve.wait_ge(s["h_done"], 2 * (NM * i + n) + 2)
                        ve.wait_ge(s["ghi_ready"], PRIMED + NM * i + max(n - 1, 0))
                        ve.tensor_tensor(g[:, n % 2], ps[:, H + 2 * (n % 2) + 1, :], act_h[:, n % 2], ALU.mult).then_inc(s["g_ready"], 1)
                        ve.wait_ge(s["ghi_ready"], PRIMED + NM * i + n + 1)
                        ve.tensor_tensor(ghl[:, n % 2, 1], g[:, n % 2], ghl[:, n % 2, 0].bitcast(F32), ALU.subtract).then_inc(s["glo_ready"], 1)
                        if n == 0:
                            ve.wait_ge(s["logits_done"], PRIMED + i + 1)
                            ve.tensor_tensor(logits[:, i], ps[:, T, 0:BATCH * EXPERTS].rearrange("p (b e) -> p b e", b=BATCH),
                                             rbs[:].unsqueeze(1).to_broadcast([P, BATCH, EXPERTS]), ALU.add).then_inc(s["logits_read"], 1)
                    ve.wait_ge(s["g_used"], PRIMED + NM * (i + 1))
                    ve.wait_ge(stored[k], PRIMED + 16 * j)
                    for half in range(2):
                        bb = slice(2 * half, 2 * half + 2)
                        last = ve.tensor_tensor(z[:, k, bb], ps[:, O + half, :].rearrange("p (b d) -> p b d", b=2), xr[:, k, bb], ALU.add)
                        if half == 0:
                            ch.mark(last)
                    last.then_inc(s["z_ready"], 1)
                    ch.end()


def phase_route(nc, logits, masks, zeros_done, x3, xg, pos, prob, tile_expert):
    E = EXPERTS
    with ExitStack() as ctx:
        def sb(name, shape, dt=F32):
            return ctx.enter_context(nc.sbuf_tensor("r_" + name, shape, dt))

        def sem(name):
            return ctx.enter_context(nc.semaphore("r_" + name))

        rows = sb("rows", [P, STEPS, BATCH, D])
        tri = sb("tri", [P, P])
        ones = sb("ones", [P, P])
        iota = sb("iota", [P, E])
        ioti = sb("ioti", [P, E], I32)
        gidx = sb("gidx", [P, GROUPS + 1])
        gidxi = sb("gidxi", [P, GROUPS + 1], I32)
        w = {n: sb(n, [P, TILES, E]) for n in ("lg", "cand", "oh0", "oh1", "incl", "tmp")}
        m = sb("m", [P, 2, TILES])
        idx = sb("idx", [P, TILES])
        ex = sb("ex", [P, TILES])
        tot = sb("tot", [P, E, TILES])
        cum = sb("cum", [P, E, TILES])
        cnt = sb("cnt", [P, 6, E])
        cnti = sb("cnti", [P, E], I32)
        te = sb("te", [P, GROUPS + 1, E])
        tf = sb("tf", [P, GROUPS + 1])
        posf = sb("posf", [P, TOPK, TILES])
        ps = ctx.enter_context(nc.psum_tensor("r_ps", [P, 2, 512], F32))
        names = ("in", "iota", "ex_ready", "diff_ready", "sel_ready", "sums_done", "pos_ready", "scattered", "own", "rows_in")
        s = {n: sem(n) for n in names}
        block = ctx.enter_context(nc.Block())
        lgv = logits[:].rearrange("p i b e -> p (i b) e")
        BIG = 3.0e38

        @block.sync
        def _(sp):
            sp.dma_start(tri[:], masks[0]).then_inc(s["in"], 16)
            sp.dma_start(ones[:], masks[2]).then_inc(s["in"], 16)
            for i in range(STEPS):
                sp.dma_start(rows[:, i], x3[i]).then_inc(s["rows_in"], 16)

        @block.gpsimd
        def _(gp):
            gp.iota(ioti[:], [[1, E]], channel_multiplier=0).then_inc(s["iota"], 1)
            gp.iota(gidxi[:], [[SLOT, GROUPS + 1]], channel_multiplier=0).then_inc(s["iota"], 1)
            gp.wait_ge(s["rows_in"], 16 * STEPS)
            gp.wait_ge(s["pos_ready"], 1)
            gp.wait_ge(zeros_done, 16 * ZERO_DMAS)
            for t in range(TILES):
                for k in range(TOPK):
                    gp.indirect_dma_start(xg, bass.IndirectOffsetOnAxis(ap=pos[:, k, t:t + 1], axis=0),
                                          rows[:, t // BATCH, t % BATCH, :], None).then_inc(s["scattered"], 16)
            gp.wait_ge(s["scattered"], 16 * TILES * TOPK)

        @block.tensor
        def _(pe):
            pe.wait_ge(s["in"], 32)
            pe.wait_ge(s["sel_ready"], 1)
            sel = w["tmp"][:].rearrange("p t e -> p (t e)")
            pe.matmul(ps[:, 0, 0:TILES * E], tri[:], sel, start=True, stop=True)
            pe.matmul(ps[:, 1, 0:TILES * E], ones[:], sel, start=True, stop=True).then_inc(s["sums_done"], 1)

        @block.scalar
        def _(act):
            act.wait_ge(s["diff_ready"], 1)
            act.activation(ex[:], idx[:], ACT.Exp).then_inc(s["ex_ready"], 1)

        @block.vector
        def _(ve):
            ch = Chain(ve, s["own"], 0)
            V = ve
            by_e = lambda ap: ap.unsqueeze(1).to_broadcast([P, TILES, E])
            by_t = lambda ap: ap.unsqueeze(2).to_broadcast([P, TILES, E])
            lg, cand, incl, tmp = (w[n][:] for n in ("lg", "cand", "incl", "tmp"))
            ohs = (w["oh0"][:], w["oh1"][:])
            ve.wait_ge(s["iota"], 2)
            ch.mark(V.tensor_copy(iota[:], ioti[:]))
            ch.mark(V.tensor_copy(gidx[:], gidxi[:]))
            ch.link(V.tensor_copy(lg, lgv))
            for k in range(TOPK):
                ch.link(V.tensor_reduce(m[:, k], lg, AX.X, ALU.max))
                ch.link(V.tensor_tensor(cand, lg, by_t(m[:, k]), ALU.is_lt))
                ch.link(V.scalar_tensor_tensor(cand, cand, float(E), by_e(iota[:]), ALU.mult, ALU.add))
                ch.link(V.tensor_reduce(idx[:], cand, AX.X, ALU.min))
                ch.link(V.tensor_tensor(ohs[k], by_e(iota[:]), by_t(idx[:]), ALU.is_equal))
                if k == 0:
                    ch.link(V.scalar_tensor_tensor(lg, ohs[0], -BIG, lg, ALU.mult, ALU.add))
            V.tensor_tensor(tmp, ohs[0], ohs[1], ALU.add).then_inc(s["sel_ready"], 1)
            V.tensor_tensor(idx[:], m[:, 1], m[:, 0], ALU.subtract).then_inc(s["diff_ready"], 1)
            ve.wait_ge(s["ex_ready"], 1)
            ch.link(V.tensor_scalar(posf[:, 0], ex[:], 1.0, None, ALU.add))
            ch.link(V.reciprocal(prob[:, 0], posf[:, 0]))
            ch.mark(V.tensor_tensor(prob[:, 1], prob[:, 0], ex[:], ALU.mult))
            ve.wait_ge(s["sums_done"], 1)
            ch.mark(V.tensor_copy(incl, ps[:, 0, 0:TILES * E].rearrange("p (t e) -> p t e", e=E)))
            ch.link(V.tensor_copy(tot[:], ps[:, 1, 0:TILES * E].rearrange("p (t e) -> p e t", e=E)))
            totf, cumf = tot[:].rearrange("p e t -> p (e t)"), cum[:].rearrange("p e t -> p (e t)")
            ch.link(V.tensor_tensor_scan(cumf, totf, totf, 0.0, ALU.add, ALU.max))
            last = cum[:, :, TILES - 1]
            ch.mark(V.tensor_copy(cnt[:, 0, 0:1], last[:, 0:1]))
            ch.link(V.tensor_tensor(cnt[:, 0, 1:E], last[:, 1:E], last[:, 0:E - 1], ALU.subtract))
            ch.link(V.tensor_scalar(cnti[:], cnt[:, 0], float(SLOT - 1), None, ALU.add))
            ch.link(V.tensor_scalar(cnti[:], cnti[:], SLOT.bit_length() - 1, SLOT.bit_length() - 1, ALU.logical_shift_right, ALU.logical_shift_left))
            ch.link(V.tensor_copy(cnt[:, 1], cnti[:]))
            ch.link(V.tensor_tensor_scan(cnt[:, 2], cnt[:, 1], cnt[:, 1], 0.0, ALU.add, ALU.max))
            ch.link(V.tensor_tensor(cnt[:, 3], cnt[:, 2], cnt[:, 1], ALU.subtract))
            ch.mark(V.tensor_tensor(cnt[:, 4], last, cnt[:, 0], ALU.subtract))
            ch.link(V.tensor_tensor(te[:], gidx[:].unsqueeze(2).to_broadcast([P, GROUPS + 1, E]),
                                    cnt[:, 2].unsqueeze(1).to_broadcast([P, GROUPS + 1, E]), ALU.is_ge))
            ch.link(V.tensor_tensor(cnt[:, 4], cnt[:, 3], cnt[:, 4], ALU.subtract))
            ch.link(V.tensor_reduce(tf[:], te[:], AX.X, ALU.add))
            ch.mark(V.tensor_scalar(tile_expert[:], tf[:], float(E - 1), None, ALU.min))
            ch.link(V.tensor_tensor(cum[:], cum[:], tot[:], ALU.subtract))
            ch.link(V.tensor_tensor(incl, incl, cum[:].rearrange("p e t -> p t e"), ALU.add))
            ch.link(V.tensor_tensor(incl, incl, by_e(cnt[:, 4]), ALU.add))
            for k in range(TOPK):
                ch.link(V.tensor_tensor(cand, incl, ohs[k], ALU.mult))
                ch.link(V.tensor_reduce(posf[:, k], cand, AX.X, ALU.add))
            V.tensor_scalar(pos[:], posf[:], -1.0, None, ALU.add).then_inc(s["pos_ready"], 1)



def phase_experts(nc, wall, wall_in, tile_expert, ident, xg, yg):
    SB = SLOT // P
    with ExitStack() as ctx:
        def sb(name, shape, dt=F32):
            return ctx.enter_context(nc.sbuf_tensor("e_" + name, shape, dt))

        def sem(name):
            return ctx.enter_context(nc.semaphore("e_" + name))

        whl = sb("whl", [P, 2, 2, WCOLS], F32R)
        ids = sb("ident", [P, P])
        xr = sb("xr", [P, 2, SB, D])
        xhl = sb("xhl", [P, 2, 2, KD, SLOT], F32R)
        act_h = sb("act_h", [P, HM, SLOT])
        g = sb("g", [P, HM, SLOT])
        ghl = sb("ghl", [P, HM, 2, SLOT], F32R)
        y = sb("y", [P, 2, SB, D])
        ps = ctx.enter_context(nc.psum_tensor("e_ps", [P, 8, 512], F32))
        names = ("consts_in", "turned", "whi_dve", "whi_act", "wlo_ready", "xhi_ready", "xlo_ready", "h_done", "silu_done", "g_ready",
                 "ghi_ready", "glo_ready", "g_used", "y_ready")
        s = {n: sem(n) for n in names}
        x_in = [sem(f"x_in{k}") for k in range(2)]
        stored = [sem(f"stored{k}") for k in range(2)]
        block = ctx.enter_context(nc.Block())
        xgv = xg.rearrange("(n b p) d -> n p b d", p=P, b=SB)
        ygv = yg.rearrange("(n b p) d -> n p b d", p=P, b=SB)
        PAIR = GROUPS // 2
        NQ = 3
        QC = WCOLS // NQ
        assert W2AT == 2 * QC
        T, H, O = 0, 2, 6
        part = [slice(q * QC, (q + 1) * QC) for q in range(NQ)]

        def expert_of(eng, i):
            return eng.value_load(tile_expert[0:1, bass.ds(i, 1)], min_val=0, max_val=EXPERTS - 1)

        @block.sync
        def _(sp):
            sp.dma_start(ids[:], ident).then_inc(s["consts_in"], 16)
            for k in range(2):
                sp.dma_start(xr[:, k], xgv[k]).then_inc(x_in[k], 16)
            def body(j, k):
                i = 2 * j + k
                if not (isinstance(j, int) and j == PAIR - 1):
                    sp.wait_ge(s["turned"], i + 1)
                    sp.dma_start(xr[:, k], xgv[i + 2]).then_inc(x_in[k], 16)
                if not is_turn(j, k, 0):
                    sp.wait_ge(s["y_ready"], i)
                    sp.dma_start(ygv[i - 1], y[:, 1 - k]).then_inc(stored[1 - k], 16)

            in_pairs(sp, PAIR, body)
            sp.wait_ge(s["y_ready"], GROUPS)
            sp.dma_start(ygv[GROUPS - 1], y[:, 1]).then_inc(stored[1], 16)
            for k in range(2):
                sp.wait_ge(stored[k], 16 * PAIR)

        @block.gpsimd
        def _(gp):
            gp.wait_ge(wall_in, 16 * EXPERTS)

            def low(e, i, k, q):
                if q < 2:
                    gp.wait_ge(s["whi_dve"], 2 * i + q + 1)
                else:
                    gp.wait_ge(s["whi_act"], i + 1)
                gp.tensor_tensor(whl[:, k, 1, part[q]], wall[:, e, part[q]], whl[:, k, 0, part[q]].bitcast(F32), ALU.subtract).then_inc(s["wlo_ready"], 1)

            def body(j, k):
                i = 2 * j + k
                if not is_turn(j, k, GROUPS - 1):
                    e = expert_of(gp, i + 1)
                    for q in range(NQ):
                        low(e, i + 1, 1 - k, q)

            first = expert_of(gp, 0)
            for q in range(NQ):
                low(first, 0, 0, q)
            in_pairs(gp, PAIR, body)

        @block.scalar
        def _(act):
            act.wait_ge(wall_in, 16 * EXPERTS)

            def high(e, k):
                act.activation(whl[:, k, 0, part[2]], wall[:, e, part[2]], ACT.Copy).then_inc(s["whi_act"], 1)

            def output(i, k):
                act.wait_ge(s["g_used"], HM * (i + 1))
                return act.activation(y[:, k].rearrange("p b d -> p (b d)"), ps[:, O + k, :], ACT.Copy)

            high(expert_of(act, 0), 0)

            def body(j, k):
                i = 2 * j + k
                last = is_turn(j, k, GROUPS - 1)
                for m in range(HM):
                    n = HM * i + m
                    act.wait_ge(s["h_done"], n + 1)
                    wait(act, s["g_ready"], n - 3)
                    act.activation(act_h[:, m], ps[:, H + m, 0:SLOT], ACT.Silu).then_inc(s["silu_done"], 1)
                    if m == 2 and not is_turn(j, k, 0):
                        wait(act, stored[1 - k], 16 * (j - 1 + k))
                        output(i - 1, 1 - k).then_inc(s["y_ready"], 1)
                    if m == 3 and not last:
                        wait(act, s["g_used"], HM * i)
                        high(expert_of(act, i + 1), 1 - k)
                    act.wait_ge(s["g_ready"], n + 1)
                    wait(act, s["g_used"], n - 3)
                    act.activation(ghl[:, m, 0], g[:, m], ACT.Copy).then_inc(s["ghi_ready"], 1)

            in_pairs(act, PAIR, body)
            act.wait_ge(stored[1], 16 * (PAIR - 1))
            output(GROUPS - 1, 1).then_inc(s["y_ready"], 1)

        @block.tensor
        def _(pe):
            def turn(k, i, rows_in):
                pe.wait_ge(x_in[k], 16 * rows_in)
                wait(pe, s["xlo_ready"], i - 1)
                for kd in range(KD):
                    for b in range(SB):
                        mm = pe.transpose(ps[:, T + k, kd * SLOT + b * P:kd * SLOT + (b + 1) * P], xr[:, k, b, kd * P:(kd + 1) * P], ids[:])
                mm.then_inc(s["turned"], 1)

            def down(i, k, m):
                n = HM * i + m
                pe.wait_ge(s["ghi_ready"], n + 1)
                pe.wait_ge(s["glo_ready"], n + 1)
                if m == 0:
                    pe.wait_ge(s["wlo_ready"], NQ * (i + 1))
                    wait(pe, s["y_ready"], i - 1)
                for b in range(SB):
                    for q, (gp_, wp_) in enumerate(PARTS):
                        lo = W2AT + m * D
                        mm = pe.matmul(ps[:, O + k, b * D:(b + 1) * D], ghl[:, m, gp_, b * P:(b + 1) * P], whl[:, k, wp_, lo:lo + D],
                                       start=m == 0 and q == 0 and b == 0, stop=m == HM - 1 and q == 2, skip_group_check=True)
                mm.then_inc(s["g_used"], 1)

            def body(j, k):
                i = 2 * j + k
                for m in range(HM):
                    n = HM * i + m
                    if m == 0:
                        pe.wait_ge(s["xhi_ready"], i + 1)
                        pe.wait_ge(s["xlo_ready"], i + 1)
                        pe.wait_ge(s["wlo_ready"], NQ * i + 2)
                    wait(pe, s["g_ready"], n - 3)
                    for w, at in enumerate((W1AT, W3AT)):
                        for q in range(3 * KD):
                            kd, (xp, wp) = q // 3, PARTS[q % 3]
                            lo = at + kd * HID + m * P
                            mm = pe.matmul(ps[:, H + m, w * SLOT:(w + 1) * SLOT], whl[:, k, wp, lo:lo + P], xhl[:, k, xp, kd, :],
                                           start=q == 0, stop=q == 3 * KD - 1)
                    mm.then_inc(s["h_done"], 1)
                    if m == 1 and not is_turn(j, k, GROUPS - 1):
                        turn(1 - k, i + 1, j + k + 1)
                    if m >= 2:
                        down(i, k, m - 2)
                    elif not is_turn(j, k, 0):
                        down(i - 1, 1 - k, m + 2)

            pe.wait_ge(s["consts_in"], 16)
            turn(0, 0, 1)
            in_pairs(pe, PAIR, body)
            for m in (2, 3):
                down(GROUPS - 1, 1, m)

        @block.vector
        def _(ve):
            def high(e, k, q):
                ve.tensor_copy(whl[:, k, 0, part[q]], wall[:, e, part[q]]).then_inc(s["whi_dve"], 1)

            def turned_rows(i, k):
                return ps[:, T + k, :].rearrange("p (k n) -> p k n", k=KD)

            def x_high(i, k):
                ve.wait_ge(s["turned"], i + 1)
                wait(ve, s["h_done"], HM * (i - 1))
                ve.tensor_copy(xhl[:, k, 0], turned_rows(i, k)).then_inc(s["xhi_ready"], 1)

            def x_low(i, k):
                ve.wait_ge(s["xhi_ready"], i + 1)
                ve.tensor_tensor(xhl[:, k, 1], turned_rows(i, k), xhl[:, k, 0].bitcast(F32), ALU.subtract).then_inc(s["xlo_ready"], 1)

            ve.wait_ge(wall_in, 16 * EXPERTS)
            first = expert_of(ve, 0)
            for q in range(2):
                high(first, 0, q)
            x_high(0, 0)
            x_low(0, 0)

            def body(j, k):
                i = 2 * j + k
                last = is_turn(j, k, GROUPS - 1)
                if not last:
                    e = expert_of(ve, i + 1)
                for m in range(HM):
                    n = HM * i + m
                    ve.wait_ge(s["silu_done"], n + 1)
                    wait(ve, s["ghi_ready"], n - 3)
                    wait(ve, s["glo_ready"], n - 3)
                    ve.tensor_tensor(g[:, m], ps[:, H + m, SLOT:2 * SLOT], act_h[:, m], ALU.mult).then_inc(s["g_ready"], 1)
                    if m < 2 and not last:
                        wait(ve, s["h_done"], HM * i)
                        high(e, 1 - k, m)
                    if m == 2 and not last:
                        x_high(i + 1, 1 - k)
                    if m == 3 and not last:
                        x_low(i + 1, 1 - k)
                    ve.wait_ge(s["ghi_ready"], n + 1)
                    ve.tensor_tensor(ghl[:, m, 1], g[:, m], ghl[:, m, 0].bitcast(F32), ALU.subtract).then_inc(s["glo_ready"], 1)

            in_pairs(ve, PAIR, body)


def phase_combine(nc, xs, yg, pos, prob, out):
    with ExitStack() as ctx:
        def sb(name, shape, dt=F32):
            return ctx.enter_context(nc.sbuf_tensor("f_" + name, shape, dt))

        def sem(name):
            return ctx.enter_context(nc.semaphore("f_" + name))

        xr = sb("xr", [P, 2, BATCH, D])
        y = sb("y", [P, 2, TOPK, BATCH, D])
        z = sb("z", [P, BATCH, D])
        o = sb("o", [P, 2, BATCH, D])
        stats = sb("stats", [P, BATCH, 6])
        small = sb("small", [P, 5, BATCH])
        smalli = sb("smalli", [P, BATCH], I32)
        used = sem("used")
        own = sem("own")
        out_ready = sem("out_ready")
        x_in = [sem(f"x_in{k}") for k in range(2)]
        y_in = [sem(f"y_in{k}") for k in range(2)]
        stored = [sem(f"stored{k}") for k in range(2)]
        block = ctx.enter_context(nc.Block())

        @block.sync
        def _(sp):
            prime(sp, [out_ready, used] + stored)
            with sp.Fori(0, STEPS // 2) as j:
                for k in range(2):
                    sp.wait_ge(used, PRIMED + 2 * j)
                    sp.dma_start(xr[:, k], xs[2 * j + k]).then_inc(x_in[k], 16)

        @block.gpsimd
        def _(gp):
            for i in range(STEPS):
                if i >= 2:
                    gp.wait_ge(used, PRIMED + i - 1)
                for b in range(BATCH):
                    for k in range(TOPK):
                        t = i * BATCH + b
                        gp.indirect_dma_start(y[:, i % 2, k, b, :], None, yg,
                                              bass.IndirectOffsetOnAxis(ap=pos[:, k, t:t + 1], axis=0)).then_inc(y_in[i % 2], 16)

        @block.scalar
        def _(act):
            with act.Fori(0, STEPS // 2) as j:
                for k in range(2):
                    act.wait_ge(out_ready, PRIMED + 2 * j + k + 1)
                    act.dma_start(out[2 * j + k], o[:, k]).then_inc(stored[k], 16)
            for k in range(2):
                act.wait_ge(stored[k], PRIMED + 16 * (STEPS // 2))

        @block.vector
        def _(ve):
            ch = Chain(ve, own, 2 * BATCH - 1 + LN_LINKS)
            with ve.Fori(0, STEPS // 2) as j:
                for k in range(2):
                    i = 2 * j + k
                    ch.turn(i)
                    ve.wait_ge(x_in[k], 16 * (j + 1))
                    ve.wait_ge(y_in[k], 16 * BATCH * TOPK * (j + 1))
                    ve.wait_ge(out_ready, PRIMED + i)
                    for b in range(BATCH):
                        ch.mark(ve.scalar_tensor_tensor(z[:, b], y[:, k, 0, b], prob[:, 0, bass.ds(i * BATCH + b, 1)], xr[:, k, b], ALU.mult, ALU.add))
                    ch.wait()
                    for b in range(BATCH):
                        last = ve.scalar_tensor_tensor(z[:, b], y[:, k, 1, b], prob[:, 1, bass.ds(i * BATCH + b, 1)], z[:, b], ALU.mult, ALU.add)
                        if b < BATCH - 1:
                            ch.mark(last)
                    last.then_inc(used, 1)
                    ve.wait_ge(used, PRIMED + i + 1)
                    ve.wait_ge(stored[k], PRIMED + 16 * j)
                    layernorm(ch, z, o[:, k], stats, small, smalli, BATCH).then_inc(out_ready, 1)
                    ch.end()


def build_program(nc, A, out):
    def views(ap):
        return ap.rearrange("(b c p) d -> c p b d", b=BATCH, p=P)

    x1, x2, x3, xs = (nc.dram_tensor(n, [TILES * P, D], F32, kind="Internal").ap() for n in ("x1", "x2", "x3", "xs"))
    xg, yg = (nc.dram_tensor(n, [SLOTS, D], F32, kind="Internal").ap() for n in ("xg", "yg"))
    flat = lambda ap: ap.rearrange("b t d -> (b t) d")
    with ExitStack() as ctx:
        def sb(name, shape, dt=F32, ctx=ctx):
            return ctx.enter_context(nc.sbuf_tensor(name, shape, dt))

        wall_in = ctx.enter_context(nc.semaphore("wall_in"))
        zeros_done = ctx.enter_context(nc.semaphore("zeros_done"))
        pos = sb("pos", [P, TOPK, TILES], I32)
        prob = sb("prob", [P, TOPK, TILES])
        tile_expert = sb("tile_expert", [P, GROUPS + 1], I32)
        phase_ssd(nc, views(flat(A["x"])), A["x_t"], A["w_xproj"], A["dt_bias"], A["a_log"], A["d_skip"], A["masks"], views(x1))
        phase_ffn(nc, views(x1), A["w1"], A["b1"], A["w2"], A["b2"], A["ident"], views(x2), xg, zeros_done)
        phase_attention(nc, views(x2), A["wqkv"], A["bqkv"], A["wout"], A["bout"], A["omega"], A["nodes"], A["weights"],
                        A["masks"], A["ident"], views(x3))
        with ExitStack() as inner:
            wall = sb("wall", [P, EXPERTS, WCOLS], ctx=inner)
            logits = sb("logits", [P, STEPS, BATCH, EXPERTS], ctx=inner)
            phase_shared(nc, views(x3), A["shared_w"], A["router_w"], A["router_b"], A["ident"], views(xs), A["expert_w"], wall, logits, wall_in)
            phase_route(nc, logits, A["masks"], zeros_done, views(x3), xg, pos, prob, tile_expert)
            phase_experts(nc, wall, wall_in, tile_expert, A["ident"], xg, yg)
        phase_combine(nc, views(xs), yg, pos, prob, views(flat(out)))


def kernel(L0_attn_x, L0_attn_W_xproj, L0_attn_dt_bias, L0_attn_A_log, L0_attn_D, L0_ffn_w1, L0_ffn_b1, L0_ffn_w2, L0_ffn_b2,
           L1_attn_Wqkv, L1_attn_bqkv, L1_attn_Wout, L1_attn_bout, L1_attn_omega, L1_attn_quad_nodes, L1_attn_quad_weights,
           L1_ffn_router_w, L1_ffn_expert_bias, L1_ffn_w1, L1_ffn_w3, L1_ffn_w2, L1_ffn_sw1, L1_ffn_sw3, L1_ffn_sw2):
    import concourse.bacc as bacc
    from concourse.bass_utils import run_bass_kernel_spmd

    def rows_first(w):
        return w.reshape(-1, P, w.shape[-1]).transpose(1, 0, 2)

    def expert_weights(w1, w3, w2):
        def part(w):
            n = w.shape[0]
            return w.transpose(0, 2, 1).reshape(n, w.shape[2] // P, P, w.shape[1]).transpose(2, 0, 1, 3).reshape(P, n, -1)
        return np.concatenate([part(w1), part(w3), part(w2)], -1)

    x = np.asarray(L0_attn_x)
    k = np.arange(P)
    omega_in = np.asarray(L1_attn_omega)
    omega = np.zeros((P, PAIRS, P), omega_in.dtype)
    per = P // HD
    for h in range(HEADS1):
        r0, c0 = HD * (h % per), FD * (h % 2)
        omega[r0:r0 + HD, h // 2, c0:c0 + FD] = omega_in[:, h].transpose(1, 0, 2).reshape(HD, FD)

    def per_feature(v):
        return np.tile(np.repeat(np.asarray(v), MF), 2).reshape(P, 1)

    arrays = {
        "x": x,
        "x_t": x.reshape(BATCH, STEPS, P, KD, P).transpose(1, 4, 3, 0, 2).reshape(STEPS, P, KD, TOK),
        "w_xproj": rows_first(np.asarray(L0_attn_W_xproj).T),
        "dt_bias": L0_attn_dt_bias, "a_log": L0_attn_A_log, "d_skip": L0_attn_D,
        "masks": np.stack([k[:, None] <= k[None, :], k[:, None] > k[None, :], np.ones((P, P), bool)]).astype(np.float32),
        "ident": np.eye(P, dtype=np.float32),
        "w1": rows_first(np.asarray(L0_ffn_w1)), "b1": np.asarray(L0_ffn_b1).reshape(-1, P).T,
        "w2": rows_first(np.asarray(L0_ffn_w2)), "b2": L0_ffn_b2,
        "wqkv": rows_first(np.asarray(L1_attn_Wqkv)), "bqkv": L1_attn_bqkv,
        "wout": rows_first(np.asarray(L1_attn_Wout)), "bout": L1_attn_bout,
        "omega": omega, "nodes": per_feature(L1_attn_quad_nodes), "weights": per_feature(L1_attn_quad_weights),
        "router_w": rows_first(np.asarray(L1_ffn_router_w).T), "router_b": L1_ffn_expert_bias,
        "shared_w": expert_weights(*map(np.asarray, (L1_ffn_sw1, L1_ffn_sw3, L1_ffn_sw2))),
        "expert_w": expert_weights(*map(np.asarray, (L1_ffn_w1, L1_ffn_w3, L1_ffn_w2))),
    }
    arrays = {"in_" + n: np.ascontiguousarray(a) for n, a in arrays.items()}
    nc = bacc.Bacc("TRN2", target_bir_lowering=False, num_devices=1)
    aps = {n[3:]: nc.dram_tensor(n, a.shape, mybir.dt.from_np(a.dtype), kind="ExternalInput").ap() for n, a in arrays.items()}
    out = nc.dram_tensor("out", x.shape, F32, kind="ExternalOutput").ap()
    build_program(nc, aps, out)
    return run_bass_kernel_spmd(nc, [arrays], core_ids=[0]).results[0]["out"]
```
